# Optimizing a Trainium2 kernel written in Bass

```python
import numpy as np
import jax
import jax.numpy as jnp

def _softmax(x, axis=-1):
    return jax.nn.softmax(x, axis=axis)

def _gelu(x):
    return jax.nn.gelu(x, approximate=True)

def _silu(x):
    return jax.nn.silu(x)

def _sigmoid(x):
    return jax.nn.sigmoid(x)

def _layernorm(x, axis=-1, eps=1e-05):
    m = jnp.mean(x, axis=axis, keepdims=True)
    v = jnp.var(x, axis=axis, keepdims=True)
    return (x - m) / jnp.sqrt(v + eps)

def _scatter_add(tgt, idx, src, axis=0):
    return tgt.at[idx].add(src)

def _segment_sum(src, seg, n):
    return jax.ops.segment_sum(src, seg, n)
kernel_name = 'mk_perceiver_d2_seqx_r2_ccc94d'

def setup_inputs(seed: int=0):
    np.random.seed(seed)
    _w = jnp.asarray

    def _rec_inputs():
        import jax
        import jax.numpy as jnp
        _rk = jax.random.key(seed)
        x = -0.000125 + 0.9999 * jax.random.normal(jax.random.fold_in(_rk, 1), (4, 128, 2048), jnp.float32)
        _lenS = 128 - jax.random.randint(jax.random.fold_in(_rk, 7), (4,), 0, max(1, 128 // 4) + 1, jnp.int32)
        _lenS2 = 2048 - jax.random.randint(jax.random.fold_in(_rk, 8), (4,), 0, max(1, 2048 // 4) + 1, jnp.int32)
        _ctx_4096P = jax.random.normal(jax.random.fold_in(_rk, 11), (4, 16, 2048), jnp.float32)
        _ctx_4096c = jax.random.dirichlet(jax.random.fold_in(_rk, 511), 0.3 * jnp.ones((16,), jnp.float32), (4, 2048))
        _ctx_4096t = jnp.einsum('bsk,bkd->bsd', _ctx_4096c, _ctx_4096P)
        _ctx_4096t = _ctx_4096t * jax.lax.rsqrt(jnp.mean(jnp.square(_ctx_4096t)) + 1e-12) * 0.953939
        ctx_4096 = -5.72187e-05 + 0.999849 * (_ctx_4096t + 0.3 * jax.random.normal(jax.random.fold_in(_rk, 611), (4, 2048, 2048), jnp.float32))
        return (x, ctx_4096)
    x, ctx_4096 = _rec_inputs()

    def _L0_xattn_setup():
        import jax, jax.numpy as jnp
        import numpy as np
        QMIN = 0.0
        QMAX = 255.0

        def fake_quant(x, scale, zp):
            s = scale.reshape(())
            z = zp.reshape(())
            q = jnp.clip(jnp.round(x / s + z), QMIN, QMAX)
            return (q - z) * s
        key = jax.random.key(seed)
        k1, k2 = jax.random.split(key)
        B, M, K, N = (4, 1024, 2048, 2048)
        x1 = jax.random.normal(k1, (B, M, K), dtype=jnp.float32)
        x2 = jax.random.normal(k2, (B, K, N), dtype=jnp.float32)
        x1_scale = jnp.full((1,), 8.0 / 255.0, dtype=jnp.float32)
        x1_zp = jnp.full((1,), 128.0, dtype=jnp.float32)
        x2_scale = jnp.full((1,), 8.0 / 255.0, dtype=jnp.float32)
        x2_zp = jnp.full((1,), 128.0, dtype=jnp.float32)
        return {'x1': x1, 'x2': x2, 'x1_scale': x1_scale, 'x1_zp': x1_zp, 'x2_scale': x2_scale, 'x2_zp': x2_zp}
    _L0_xattn_all = _L0_xattn_setup()
    _L0_xattn_in = {k: v for k, v in _L0_xattn_all.items() if k in ('x1_scale', 'x1_zp', 'x2_scale', 'x2_zp')}
    del _L0_xattn_all

    def _L0_attn_setup():
        import jax, jax.numpy as jnp
        import numpy as np
        H = 2048
        D = H // 4
        key = jax.random.key(seed)
        k1, k2, k3, k4, k5 = jax.random.split(key, 5)
        x = jax.random.normal(k1, (4, 2048, H), dtype=jnp.float32)
        s_in = 1.0 / np.sqrt(H)
        Wqkv = jax.random.normal(k2, (H, 3 * D), dtype=jnp.float32) * s_in
        bqkv = jax.random.normal(k3, (3 * D,), dtype=jnp.float32) * 0.01
        Wo = jax.random.normal(k4, (D, H), dtype=jnp.float32) * (1.0 / np.sqrt(D))
        bo = jax.random.normal(k5, (H,), dtype=jnp.float32) * 0.01
        return {'x': x, 'Wqkv': Wqkv, 'bqkv': bqkv, 'Wo': Wo, 'bo': bo}
    _L0_attn_all = _L0_attn_setup()
    _L0_attn_in = {k: v for k, v in _L0_attn_all.items() if k in ('Wqkv', 'bqkv', 'Wo', 'bo')}
    del _L0_attn_all

    def _L0_ffn_setup():
        import jax, jax.numpy as jnp
        import numpy as np
        R = 16
        NUM_EXPERTS = 8
        TOP_K = 2
        LORA_ALPHA = 32
        SCALING = LORA_ALPHA / R
        key = jax.random.key(seed)
        ks = jax.random.split(key, 6)
        d_in, d_out = (2048, 2048)
        x = jax.random.normal(ks[0], (4, 1024, d_in), dtype=jnp.float32)
        W_base = jax.random.normal(ks[1], (d_out, d_in), dtype=jnp.float32) * 0.02
        b_base = jax.random.normal(ks[2], (d_out,), dtype=jnp.float32) * 0.02
        W_router = jax.random.normal(ks[3], (NUM_EXPERTS, d_in), dtype=jnp.float32) * 0.01
        A = jax.random.normal(ks[4], (NUM_EXPERTS, R, d_in), dtype=jnp.float32) * 0.02
        B = jax.random.normal(ks[5], (NUM_EXPERTS, d_out, R), dtype=jnp.float32) * 0.02
        return {'x': x, 'W_base': W_base, 'b_base': b_base, 'W_router': W_router, 'A': A, 'B': B}
    _L0_ffn_all = _L0_ffn_setup()
    _L0_ffn_in = {k: v for k, v in _L0_ffn_all.items() if k in ('W_base', 'b_base', 'W_router', 'A', 'B')}
    del _L0_ffn_all

    def _L1_xattn_setup():
        import jax, jax.numpy as jnp
        import numpy as np
        key = jax.random.key(seed)
        k1, k2 = jax.random.split(key)
        B, Lq, Lk, D = (16, 512, 1024, 2048)
        query = jax.random.normal(k1, (B, Lq, D), dtype=jnp.float32)
        key_t = jax.random.normal(k2, (B, Lk, D), dtype=jnp.float32)
        return {'query': query, 'key': key_t}
    _L1_xattn_all = _L1_xattn_setup()
    _L1_xattn_in = {k: v for k, v in _L1_xattn_all.items() if k in ()}
    del _L1_xattn_all

    def _L1_attn_setup():
        import jax, jax.numpy as jnp
        import numpy as np
        B, T, H, S, F, G = (2, 1024, 2048, 512, 4992, 6)
        GRAD_ORDER_MIN = 4
        THD = 2.5
        key = jax.random.key(seed)
        ks = jax.random.split(key, 9)
        sc = 0.02
        hidden_states = jax.random.normal(ks[0], (B, T, H), jnp.float32)
        up_w = jax.random.normal(ks[1], (S, H), jnp.float32) * sc
        gate_w = jax.random.normal(ks[2], (S, H), jnp.float32) / np.sqrt(H)
        local_point = jax.random.normal(ks[3], (S,), jnp.float32)
        local_approx_output = jax.random.normal(ks[4], (H, S), jnp.float32) * sc
        fuse_weight = jax.random.normal(ks[5], (H, S, G), jnp.float32) * sc
        discount_factor = jnp.asarray(np.cumsum(np.log(np.arange(1, G + 1, dtype=np.float64))), jnp.float32)
        ffn_gate_w = jax.random.normal(ks[6], (F, H), jnp.float32) * sc
        ffn_up_w = jax.random.normal(ks[7], (F, H), jnp.float32) * sc
        ffn_down_w = jax.random.normal(ks[8], (H, F), jnp.float32) * sc
        return {'hidden_states': hidden_states, 'up_w': up_w, 'gate_w': gate_w, 'local_point': local_point, 'local_approx_output': local_approx_output, 'fuse_weight': fuse_weight, 'discount_factor': discount_factor, 'ffn_gate_w': ffn_gate_w, 'ffn_up_w': ffn_up_w, 'ffn_down_w': ffn_down_w}
    _L1_attn_all = _L1_attn_setup()
    _L1_attn_in = {k: v for k, v in _L1_attn_all.items() if k in ('up_w', 'gate_w', 'local_point', 'local_approx_output', 'fuse_weight', 'discount_factor', 'ffn_gate_w', 'ffn_up_w', 'ffn_down_w')}
    del _L1_attn_all

    def _L1_ffn_setup():
        import jax, jax.numpy as jnp
        import numpy as np
        NUM_EXPERTS = 8
        RANK = 32
        ALPHA = 16.0
        TOP_K = 2
        TEMPERATURE = 1.0
        GAMMA = 0.5
        SOFT_TOPK_TEMP = 0.5
        N_GRAM = 2
        EPS = 1e-06
        key = jax.random.key(seed)
        ks = jax.random.split(key, 6)
        d_in, d_out = (2048, 2048)
        Bsz, T = (4, 1024)
        x = jax.random.normal(ks[0], (Bsz, T, d_in), dtype=jnp.float32)
        W = jax.random.normal(ks[1], (d_out, d_in), dtype=jnp.float32) / np.sqrt(d_in)
        b = jax.random.normal(ks[2], (d_out,), dtype=jnp.float32) * 0.01
        A = jax.random.normal(ks[3], (d_in, RANK), dtype=jnp.float32) / np.sqrt(d_in)
        Bmat = jax.random.normal(ks[4], (RANK, d_out), dtype=jnp.float32) * 0.01
        LiMEs = jax.random.normal(ks[5], (NUM_EXPERTS, RANK), dtype=jnp.float32) * 0.1
        return {'x': x, 'W': W, 'b': b, 'A': A, 'Bmat': Bmat, 'LiMEs': LiMEs}
    _L1_ffn_all = _L1_ffn_setup()
    _L1_ffn_in = {k: v for k, v in _L1_ffn_all.items() if k in ('W', 'b', 'A', 'Bmat', 'LiMEs')}
    del _L1_ffn_all
    return {'x': x, 'ctx_4096': ctx_4096, 'L0_xattn_x1_scale': _L0_xattn_in['x1_scale'], 'L0_xattn_x1_zp': _L0_xattn_in['x1_zp'], 'L0_xattn_x2_scale': _L0_xattn_in['x2_scale'], 'L0_xattn_x2_zp': _L0_xattn_in['x2_zp'], 'L0_attn_Wqkv': _L0_attn_in['Wqkv'], 'L0_attn_bqkv': _L0_attn_in['bqkv'], 'L0_attn_Wo': _L0_attn_in['Wo'], 'L0_attn_bo': _L0_attn_in['bo'], 'L0_ffn_W_base': _L0_ffn_in['W_base'], 'L0_ffn_b_base': _L0_ffn_in['b_base'], 'L0_ffn_W_router': _L0_ffn_in['W_router'], 'L0_ffn_A': _L0_ffn_in['A'], 'L0_ffn_B': _L0_ffn_in['B'], 'L1_attn_up_w': _L1_attn_in['up_w'], 'L1_attn_gate_w': _L1_attn_in['gate_w'], 'L1_attn_local_point': _L1_attn_in['local_point'], 'L1_attn_local_approx_output': _L1_attn_in['local_approx_output'], 'L1_attn_fuse_weight': _L1_attn_in['fuse_weight'], 'L1_attn_discount_factor': _L1_attn_in['discount_factor'], 'L1_attn_ffn_gate_w': _L1_attn_in['ffn_gate_w'], 'L1_attn_ffn_up_w': _L1_attn_in['ffn_up_w'], 'L1_attn_ffn_down_w': _L1_attn_in['ffn_down_w'], 'L1_ffn_W': _L1_ffn_in['W'], 'L1_ffn_b': _L1_ffn_in['b'], 'L1_ffn_A': _L1_ffn_in['A'], 'L1_ffn_Bmat': _L1_ffn_in['Bmat'], 'L1_ffn_LiMEs': _L1_ffn_in['LiMEs']}

def reference(x, ctx_4096, L0_xattn_x1_scale, L0_xattn_x1_zp, L0_xattn_x2_scale, L0_xattn_x2_zp, L0_attn_Wqkv, L0_attn_bqkv, L0_attn_Wo, L0_attn_bo, L0_ffn_W_base, L0_ffn_b_base, L0_ffn_W_router, L0_ffn_A, L0_ffn_B, L1_attn_up_w, L1_attn_gate_w, L1_attn_local_point, L1_attn_local_approx_output, L1_attn_fuse_weight, L1_attn_discount_factor, L1_attn_ffn_gate_w, L1_attn_ffn_up_w, L1_attn_ffn_down_w, L1_ffn_W, L1_ffn_b, L1_ffn_A, L1_ffn_Bmat, L1_ffn_LiMEs):
    import jax
    import jax.numpy as jnp

    def _L0_xattn_ref(x1, x2, x1_scale, x1_zp, x2_scale, x2_zp):
        import jax, jax.numpy as jnp
        import numpy as np
        QMIN = 0.0
        QMAX = 255.0

        def fake_quant(x, scale, zp):
            s = scale.reshape(())
            z = zp.reshape(())
            q = jnp.clip(jnp.round(x / s + z), QMIN, QMAX)
            return (q - z) * s
        q1 = fake_quant(x1, x1_scale, x1_zp)
        q2 = fake_quant(x2, x2_scale, x2_zp)
        return jnp.matmul(q1, q2)

    def _L0_attn_ref(x, Wqkv, bqkv, Wo, bo):
        import jax, jax.numpy as jnp
        import numpy as np
        H = 2048
        D = H // 4
        B, S, C = x.shape
        d = C // 4
        qkv = jnp.einsum('bsc,cf->bsf', x, Wqkv) + bqkv
        qkv = qkv.reshape(B, S, 3, d)
        q, k, v = (qkv[:, :, 0], qkv[:, :, 1], qkv[:, :, 2])
        scale = 1.0 / jnp.sqrt(jnp.float32(d)).astype(x.dtype)
        attn = jnp.einsum('bqd,bkd->bqk', q, k) * scale
        attn = jax.nn.softmax(attn, axis=-1)
        out = jnp.einsum('bqk,bkd->bqd', attn, v)
        return jnp.einsum('bqd,dc->bqc', out, Wo) + bo

    def _L0_ffn_ref(x, W_base, b_base, W_router, A, B):
        import jax, jax.numpy as jnp
        import numpy as np
        R = 16
        NUM_EXPERTS = 8
        TOP_K = 2
        LORA_ALPHA = 32
        SCALING = LORA_ALPHA / R
        orig_shape = x.shape
        d_in = x.shape[-1]
        x_flat = x.reshape(-1, d_in)
        logits = x_flat @ W_router.T
        probs = jax.nn.softmax(logits, axis=-1)
        topk_probs, topk_idx = jax.lax.top_k(probs, TOP_K)
        topk_probs = topk_probs / jnp.sum(topk_probs, axis=-1, keepdims=True)
        onehot = jax.nn.one_hot(topk_idx, NUM_EXPERTS, dtype=x.dtype)
        combine = jnp.einsum('nk,nke->ne', topk_probs, onehot)
        h = jnp.einsum('nd,erd->ner', x_flat, A)
        hw = h * combine[:, :, None]
        expert_out = jnp.einsum('ner,eor->no', hw, B) * SCALING
        base_out = x_flat @ W_base.T + b_base
        out = base_out + expert_out
        return out.reshape(*orig_shape[:-1], W_base.shape[0])

    def _L1_xattn_ref(query, key):
        import jax, jax.numpy as jnp
        import numpy as np
        a = jnp.einsum('bqd,bkd->bqk', query, key)
        e = jax.nn.softmax(a, axis=-1)
        c = jnp.einsum('bqk,bkd->bqd', e, key)
        return c

    def _L1_attn_ref(hidden_states, up_w, gate_w, local_point, local_approx_output, fuse_weight, discount_factor, ffn_gate_w, ffn_up_w, ffn_down_w):
        import jax, jax.numpy as jnp
        import numpy as np
        B, T, H, S, F, G = (2, 1024, 2048, 512, 4992, 6)
        GRAD_ORDER_MIN = 4
        THD = 2.5
        approx_up = hidden_states @ up_w.T
        gate_pre = hidden_states @ gate_w.T
        delta = gate_pre - local_point
        neg_factor = jnp.where(delta > 0, 1.0, -1.0).astype(hidden_states.dtype)
        delta_abs = jnp.abs(delta)
        log_delta = jnp.log(delta_abs)
        keep = (delta_abs <= THD).astype(hidden_states.dtype)
        approx_out = approx_up @ local_approx_output.T
        for idx in range(G):
            m = idx + 1
            dterm = jnp.exp(log_delta * m - discount_factor[idx])
            if m % 2 == 1:
                dterm = dterm * neg_factor
            tmp = dterm * approx_up
            if m > GRAD_ORDER_MIN:
                tmp = tmp * keep
            approx_out = approx_out + tmp @ fuse_weight[:, :, idx].T
        ffn_out = jax.nn.silu(hidden_states @ ffn_gate_w.T) * (hidden_states @ ffn_up_w.T) @ ffn_down_w.T
        return approx_out + ffn_out

    def _L1_ffn_ref(x, W, b, A, Bmat, LiMEs):
        import jax, jax.numpy as jnp
        import numpy as np
        NUM_EXPERTS = 8
        RANK = 32
        ALPHA = 16.0
        TOP_K = 2
        TEMPERATURE = 1.0
        GAMMA = 0.5
        SOFT_TOPK_TEMP = 0.5
        N_GRAM = 2
        EPS = 1e-06
        Bsz, T, d_in = x.shape
        E = LiMEs.shape[0]
        scaling = ALPHA / RANK
        H = jnp.einsum('btd,od->bto', x, W) + b
        z = jnp.einsum('btd,dr->btr', x, A)
        anchors = jnp.arange(N_GRAM - 1, T, N_GRAM)
        H_slice = H[:, anchors, :E]
        delta_slice = jnp.einsum('bar,er->bae', z[:, anchors], LiMEs)
        H_scale = jnp.maximum(jnp.max(jnp.abs(H_slice)), EPS)
        d_scale = jnp.maximum(jnp.max(jnp.abs(delta_slice)), EPS)
        logits = ((1.0 - GAMMA) * (H_slice / H_scale) + GAMMA * (delta_slice / d_scale)) / TEMPERATURE
        probs = jax.nn.softmax(logits, axis=-1)
        topk_vals, _ = jax.lax.top_k(probs, TOP_K)
        thresh = topk_vals[..., -1:]
        mask = jax.nn.sigmoid((probs - thresh) / SOFT_TOPK_TEMP)
        weights = probs * mask
        weights = weights / (jnp.sum(weights, axis=-1, keepdims=True) + 1e-09)
        weights_full = jnp.repeat(weights, N_GRAM, axis=1)
        p_mix = jnp.einsum('bte,er->btr', weights_full, LiMEs)
        delta = jnp.einsum('btr,ro->bto', z * p_mix, Bmat) * scaling
        return H + delta
    x = x + _L0_xattn_ref(_layernorm(x, axis=-1), ctx_4096, L0_xattn_x1_scale, L0_xattn_x1_zp, L0_xattn_x2_scale, L0_xattn_x2_zp)
    x = x + _L0_attn_ref(_layernorm(x, axis=-1), L0_attn_Wqkv, L0_attn_bqkv, L0_attn_Wo, L0_attn_bo)
    x = x + _L0_ffn_ref(_layernorm(x, axis=-1), L0_ffn_W_base, L0_ffn_b_base, L0_ffn_W_router, L0_ffn_A, L0_ffn_B)
    x = x + _L1_xattn_ref(_layernorm(x, axis=-1), ctx_4096)
    x = x + _L1_attn_ref(_layernorm(x, axis=-1), L1_attn_up_w, L1_attn_gate_w, L1_attn_local_point, L1_attn_local_approx_output, L1_attn_fuse_weight, L1_attn_discount_factor, L1_attn_ffn_gate_w, L1_attn_ffn_up_w, L1_attn_ffn_down_w)
    x = x + _L1_ffn_ref(_layernorm(x, axis=-1), L1_ffn_W, L1_ffn_b, L1_ffn_A, L1_ffn_Bmat, L1_ffn_LiMEs)
    return x

_drawn_inputs = setup_inputs


def setup_inputs(seed=0):
    import zlib

    import numpy as np

    out = dict(_drawn_inputs(seed))
    spreads = {}
    factors = {'L0_attn_Wqkv': 8.0,
     'L0_attn_bqkv': 8.0,
     'L0_attn_Wo': 8.0,
     'L0_attn_bo': 200.0,
     'L0_ffn_b_base': 64.0,
     'L0_ffn_W_router': 8.0,
     'L0_ffn_A': 8.0,
     'L0_ffn_B': 8.0,
     'L1_attn_local_approx_output': 44.696,
     'L1_attn_ffn_gate_w': 3.539,
     'L1_attn_ffn_up_w': 3.345,
     'L1_attn_ffn_down_w': 3.357,
     'L1_ffn_b': 200.0,
     'L1_ffn_A': 64.0,
     'L1_ffn_Bmat': 64.0,
     'L1_ffn_LiMEs': 64.0,
     'L0_ffn_W_base': 4.342,
     'L1_attn_gate_w': 4.488,
     'L1_attn_local_point': 4.665,
     'L1_attn_fuse_weight': 3.532,
     'L1_ffn_W': 4.594}
    for name, (base, spread) in spreads.items():
        noise = np.random.default_rng([zlib.crc32(name.encode()), seed]).standard_normal(out[name].shape)
        drawn = base * np.exp(spread * noise) if base else spread * noise
        out[name] = jnp.asarray(drawn.astype(out[name].dtype))
    for name, factor in factors.items():
        out[name] = (out[name] * factor).astype(out[name].dtype)
    return out
```

```python
from collections import defaultdict
from contextlib import ExitStack, contextmanager

import numpy as np

import concourse.bass as bass
from concourse import mybir

F32 = mybir.dt.float32
F32R = mybir.dt.float32r
BF16 = mybir.dt.bfloat16
I32 = mybir.dt.int32
ALU = mybir.AluOpType
ACT = mybir.ActivationFunctionType
AX = mybir.AxisListType.X
RMAX = bass.bass_isa.ReduceOp.max
ds = bass.ds

P = 128
B = 4
TOK = B * P
D = 2048
KT = D // P
W = 512
NC = D // W
BLK = 1024
SLOTS = 4
LEAD = SLOTS
BANKS = 8

HD = D // 4
E0, R0 = 8, 16
SM0 = E0 + E0 * R0
KB0 = BLK // SM0
E1, R1 = 8, 32
SM1 = E1 + R1
S = 512
G = 6
F = 4992
FT = F // P
UNITS = FT // 2
LN_EPS = 1e-5
THD = 2.5
GRAD_ORDER_MIN = 4
MAGIC = 1.5 * 2.0 ** 23
QMAX = 255.0
QMID = 128.0

N_CTX = B * 2 * KT
N_BLOCKS = (N_CTX + 3 * KT // 2 + 2 * NC + -(-KT // KB0) + NC * KT // 2 + NC + 2 * N_CTX
            + KT + (G + 1) * 2 * NC + UNITS * (KT // 2 + NC) + KT // 4 + NC + 1 + NC * KT // 2 + NC)

C_S1, C_Z1, C_S2, C_Z2, C_BQK, C_LP, C_DF = 0, 1, 2, 3, 4, 12, 16
C_B8 = C_DF + G
C_LIM = C_B8 + E1
C_BV = C_LIM + E1 * R1
C_END = C_BV + HD


class Place:

    def __init__(self, engine):
        self.engine, self.n, self.turn, self.per_turn = engine, defaultdict(int), None, {}

    def next(self, name, k=1):
        self.n[name] += k
        return self.value(name)

    def value(self, name, back=0):
        n = self.n[name] - back
        step = self.per_turn.get(name, 0)
        return n if self.turn is None or step == 0 else self.turn * step + n

    @contextmanager
    def loop(self, turns, **per_turn):
        before = dict(self.n)
        with self.engine.Fori(0, turns) as turn:
            self.turn, self.per_turn = turn, per_turn
            yield turn
        for name in self.n:
            moved = self.n[name] - before.get(name, 0)
            assert moved == per_turn.get(name, 0), (name, moved)
        self.turn, self.per_turn = None, {}
        for name, k in per_turn.items():
            self.n[name] = before.get(name, 0) + turns * k


def build(nc, x_in, stream, biases, consts, out):
    ctx = ExitStack()
    at = [-(-nc.sbuf_base // 64) * 64]

    def place(name, shape, dtype, offset=None):
        size = int(np.prod(shape[1:])) * (2 if dtype == BF16 else 4)
        if offset is None:
            offset, at[0] = at[0], at[0] + -(-size // 64) * 64
        return nc.alloc_sbuf_tensor_at(name, shape, dtype, offset=offset)

    with ctx:
        x = place("x_res", [P, B * D], F32)
        raw = place("raw", [P, SLOTS, BLK], F32)
        hi = place("hi", [P, SLOTS, BLK], F32R)
        lo = place("lo", [P, SLOTS, BLK], F32R)
        xt_at = at[0]
        xt_hi = place("xt_hi", [P, KT, TOK], F32R)
        xt_lo = place("xt_lo", [P, KT, TOK], F32R)
        q1t = place("q1t", [P, B * D], BF16, offset=xt_at)
        q2 = place("q2", [P, SLOTS, BLK], BF16, offset=xt_at + 2 * B * D)
        th_hi = [place(f"th_hi{i}", [P, 4, TOK], F32R) for i in range(2)]
        th_lo = [place(f"th_lo{i}", [P, 4, TOK], F32R) for i in range(2)]
        wide = [place(f"wide{i}", [P, D], F32) for i in range(3)]
        cst = place("cst", [P, C_END], F32)
        ident = place("ident", [P, P], F32)
        pick = place("pick", [P, P], F32)
        ones = place("ones", [P, P], BF16)
        rank = place("rank", [P, B, E0], F32)
        stats = place("stats", [P, B * NC * 6], F32)
        sm = place("sm", [P, 448], F32)
        assert at[0] <= nc.sbuf_usable_end, (at[0], nc.sbuf_usable_end)
        psum = ctx.enter_context(nc.psum_tensor("psum", [P, BANKS, W], F32))

        used = [0]

        def cells(n):
            used[0] += n
            assert used[0] <= 448
            return sm[:, used[0] - n:used[0]]

        mv, var, rstd, nt1 = cells(2 * B), cells(B), cells(B), cells(B)
        quant, rows, row_now = cells(6), cells(B), cells(1)
        nmax, esum, rsum = cells(B), cells(B), cells(B)
        taylor, order_now, ediff = cells(2 * (G + 1)), cells(2), cells(G + 1)
        m1, m2, msum, gm, gmall = cells(B), cells(B), cells(B), cells(2), cells(2)
        pr, cand, oh1, oh2, t8 = (cells(B * E0) for _ in range(5))
        hd = cells(B * 2 * E1)
        lg = cells(B * 2 * E1)

        def sem(name):
            return ctx.enter_context(nc.semaphore(name))

        raw_full = [sem(f"raw_full{i}") for i in range(SLOTS)]
        x_loaded = [sem(f"x_loaded{i}") for i in range(B)]
        consts_loaded = sem("consts_loaded")
        tables_made = sem("tables_made")
        hi_ready = sem("hi_ready")
        lo_ready = sem("lo_ready")
        block_used = sem("block_used")
        bank_drained = sem("bank_drained")
        step_done = sem("step_done")
        ask_act = sem("ask_act")
        act_done = sem("act_done")
        ask_pe = sem("ask_pe")
        dve_step = sem("dve_step")
        bias_room = sem("bias_room")
        bias_loaded = sem("bias_loaded")
        ask_pool = sem("ask_pool")
        pool_done = sem("pool_done")
        stored = sem("stored")

        block = ctx.enter_context(nc.Block())

        def bank(p):
            return p.n["bank"] % BANKS

        def batch_of(tile, b):
            return tile[:, :, b * P:(b + 1) * P]

        @block.sync
        def _(sp):
            for n in range(SLOTS):
                sp.dma_start(raw[:, n, :], stream[n, :, :]).then_inc(raw_full[n], 16)
            with sp.Fori(1, N_BLOCKS // SLOTS) as turn:
                for s in range(SLOTS):
                    sp.wait_ge(lo_ready, turn * SLOTS + (s + 1 - SLOTS))
                    sp.dma_start(raw[:, s, :], stream[ds(turn * SLOTS + s, 1), :, :]
                                 .rearrange("a p n -> p (a n)")).then_inc(raw_full[s], 16)
            o = out.rearrange("b p n -> p b n")
            xv = x[:, :].rearrange("p (b n) -> p b n", b=B)
            for c in range(NC):
                sp.wait_ge(bank_drained, TOTAL_BANKS - 4 * (NC - 1 - c))
                sp.dma_start(o[:, :, c * W:(c + 1) * W], xv[:, :, c * W:(c + 1) * W]).then_inc(stored, 16)
            sp.wait_ge(stored, 16 * NC)

        @block.gpsimd
        def _(pool):
            pool.memset(ones[:, :], 1.0)
            for e in range(E0):
                pool.memset(rank[:, :, e:e + 1], float(E0 - e))
            pool.memset(ident[:, :], 0.0).then_inc(tables_made, 1)
            pool.wait_ge(tables_made, 1)
            pool.affine_select(out=ident[:, :], in_=ident[:, :], compare_op=ALU.not_equal, fill=1.0,
                               base=0, pattern=[[-1, P]], channel_multiplier=1).then_inc(tables_made, 1)
            pool.wait_ge(tables_made, 2)
            odd = ident[:, :].rearrange("p (j r) -> p j r", r=2)
            for r in range(2):
                last = pool.tensor_copy(pick[:, :].rearrange("p (j r) -> p j r", r=2)[:, :, r:r + 1],
                                        odd[:, :, 1:2])
            last.then_inc(tables_made, 1)
            for i in range(3):
                pool.wait_ge(bias_room, i + 1)
                pool.dma_start(wide[1][:, :], biases[i, :, :]).then_inc(bias_loaded, 16)
                if i == 2:
                    pool.wait_ge(bias_loaded, 48)
            pool.wait_ge(ask_pool, 1)
            pool.partition_all_reduce(gmall, gm, P, RMAX).then_inc(pool_done, 1)

        @block.scalar
        def _(act):
            p = Place(act)
            act.dma_start(cst[:, :], consts).then_inc(consts_loaded, 16)
            for b in range(B):
                act.dma_start(x[:, b * D:(b + 1) * D], x_in[b, :, :]).then_inc(x_loaded[b], 16)

            def slot_full():
                n = p.n["block"]
                turns = p.per_turn.get("block", 0)
                v = 16 * (n // SLOTS + 1)
                if p.turn is not None and turns:
                    v = p.turn * (16 * turns // SLOTS) + v
                act.wait_ge(raw_full[n % SLOTS], v)
                return n % SLOTS

            def split(k):
                for _ in range(k):
                    if p.n["block"] >= N_BLOCKS:
                        return
                    s = slot_full()
                    if p.n["block"] >= SLOTS:
                        act.wait_ge(block_used, p.value("block", SLOTS - 1))
                    nc.scalar.activation(hi[:, s, :], raw[:, s, :], ACT.Copy).then_inc(hi_ready, 1)
                    p.next("block")

            def scale_block(k):
                for _ in range(k):
                    s = slot_full()
                    nc.scalar.activation(raw[:, s, :], raw[:, s, :], ACT.Identity,
                                         bias=cst[:, C_Z2:C_Z2 + 1], scale=quant[:, 1:2]).then_inc(hi_ready, 1)
                    p.next("block")

            def answer(ins):
                ins.then_inc(act_done, 1)
                p.next("act_done")

            def transposed_hi(dst):
                for j in range(4):
                    act.wait_ge(step_done, p.next("step"))
                    answer(nc.scalar.activation(dst(j), psum[:, bank(p), :].rearrange("p (k t) -> p k t", t=P),
                                                ACT.Copy))
                    p.next("bank")

            def ln_hi():
                for b in range(B):
                    transposed_hi(lambda j: xt_hi[:, 4 * j:4 * j + 4, b * P:(b + 1) * P])

            def asked():
                act.wait_ge(ask_act, p.next("ask_act"))

            def skip(banks=0, steps=0):
                p.next("bank", banks)
                p.next("step", steps)

            asked()
            skip(16, 16)
            scale_block(LEAD)

            def correction(h):
                act.wait_ge(block_used, p.next("done", KT))
                act.wait_ge(bank_drained, p.value("bank"))
                k = bank(p)
                answer(nc.scalar.activation(wide[h][:, 0:BLK], psum[:, k + 2:k + 4, :], ACT.Copy,
                                            scale=quant[:, 2:3]))
                p.next("bank", 4)

            with p.loop(B - 1, block=2 * KT, bank=8, done=2 * KT, act_done=2):
                for h in range(2):
                    scale_block(KT)
                    correction(h)
            scale_block(KT)
            correction(0)
            scale_block(KT - LEAD)
            split(LEAD)
            correction(1)

            ln_hi()
            split(3 * KT // 2)
            skip(12)
            asked()
            k = bank(p)
            skip(4, 4)
            for b in range(B):
                answer(nc.scalar.activation(wide[0][:, b * P:(b + 1) * P], psum[:, k + b, 0:P], ACT.Exp,
                                            bias=nmax[:, b:b + 1], scale=HD ** -0.5, accum_out=esum[:, b:b + 1]))
            skip(4, 4)
            for j in range(4):
                act.wait_ge(step_done, p.next("step"))
                answer(nc.scalar.activation(th_hi[0][:, j, :], psum[:, bank(p), :], ACT.Copy))
                p.next("bank")
            split(2 * NC)
            skip(16)

            ln_hi()
            split(-(-KT // KB0))
            skip(4)
            asked()
            answer(nc.scalar.activation(pr, pr, ACT.Exp))
            with p.loop(2, block=KT, bank=8):
                split(KT)
                p.next("bank", 8)

            def lora_hi(rows_):
                for b in range(B):
                    act.wait_ge(step_done, p.next("step"))
                    answer(nc.scalar.activation(th_hi[0][0:rows_, 0, b * P:(b + 1) * P],
                                                psum[0:rows_, bank(p), 0:P], ACT.Copy))
                    p.next("bank")
                split(NC)
                skip(16)

            lora_hi(E0 * R0)

            def query_hi():
                transposed_hi(lambda j: xt_hi[:, 4 * j:4 * j + 4, 0:P])

            def exp_scores():
                asked()
                k = bank(p)
                answer(nc.scalar.activation(wide[0][:, :], psum[:, k:k + 4, :], ACT.Exp,
                                            bias=nmax[:, 0:1], accum_out=esum[:, 0:1]))
                p.next("bank", 4)

            def probs_hi():
                transposed_hi(lambda j: xt_hi[:, 4 * j:4 * j + 4, P:2 * P])

            query_hi()
            split(2 * KT)
            exp_scores()
            with p.loop(B - 1, block=4 * KT, bank=16, step=8, act_done=9, ask_act=1):
                query_hi()
                split(2 * KT)
                k = bank(p)
                p.next("bank", 4)
                probs_hi()
                asked()
                answer(nc.scalar.activation(wide[0][:, :], psum[:, k:k + 4, :], ACT.Exp,
                                            bias=nmax[:, 0:1], accum_out=esum[:, 0:1]))
                split(2 * KT)
                p.next("bank", 4)
            probs_hi()
            split(2 * KT)
            skip(4)

            asked()
            answer(nc.scalar.activation(taylor[:, 0:G + 1], ediff, ACT.Exp))
            ln_hi()
            split(KT)
            skip(8)

            def term_hi(i):
                asked()
                answer(nc.scalar.activation(th_hi[i][:, :, :], wide[0][:, :].rearrange("p (k t) -> p k t", k=4),
                                            ACT.Copy))

            term_hi(0)
            with p.loop(G // 2, block=4 * NC, bank=32, act_done=2, ask_act=2):
                for i in range(2):
                    term_hi(1 - i)
                    split(2 * NC)
                    p.next("bank", 16)
            split(2 * NC)
            skip(16)

            def gated(i, tiles):
                act.wait_ge(block_used, p.value("done"))
                k = bank(p)
                answer(nc.scalar.activation(wide[0][:, 0:tiles * W], psum[:, k:k + tiles, :], ACT.Sigmoid))
                asked()
                answer(nc.scalar.activation(th_hi[i][:, 0:tiles, :],
                                            wide[1][:, 0:tiles * W].rearrange("p (k t) -> p k t", t=TOK), ACT.Copy))
                p.next("bank", 2 * tiles)

            def down():
                split(NC)
                p.next("done", NC)
                p.next("bank", 4 * NC)

            p.n["done"] = p.n["block"] - LEAD
            split(KT // 2)
            p.next("done", KT // 2)
            gated(0, 2)
            with p.loop(UNITS // 2, block=2 * (KT // 2 + NC), done=2 * (KT // 2 + NC), bank=40, act_done=4, ask_act=2):
                for i in range(2):
                    split(KT // 2)
                    p.next("done", KT // 2)
                    gated(1 - i, 2)
                    down()
            split(KT // 4)
            p.next("done", KT // 4)
            gated(1, 1)
            down()
            down()

            ln_hi()
            split(1)
            skip(4)
            asked()
            skip(4, 4)
            answer(nc.scalar.activation(pr, pr, ACT.Exp))
            asked()
            answer(nc.scalar.activation(t8, t8, ACT.Sigmoid, scale=2.0))
            with p.loop(2, block=KT, bank=8):
                split(KT)
                p.next("bank", 8)
            lora_hi(R1)

        @block.vector
        def _(dve):
            p = Place(dve)
            v = nc.vector

            def link(ins):
                ins.then_inc(dve_step, 1)
                dve.wait_ge(dve_step, p.next("link"))

            def own_drains():
                dve.wait_ge(bank_drained, p.value("bank"))

            def split(k):
                for _ in range(k):
                    if p.n["block"] >= N_BLOCKS:
                        return
                    s = p.n["block"] % SLOTS
                    dve.wait_ge(hi_ready, p.next("block"))
                    v.tensor_tensor(lo[:, s, :], raw[:, s, :], hi[:, s, :].bitcast(F32), ALU.subtract)\
                     .then_inc(lo_ready, 1)

            def round_block(k):
                for _ in range(k):
                    s = p.n["block"] % SLOTS
                    dve.wait_ge(hi_ready, p.next("block"))
                    link(v.tensor_scalar(raw[:, s, :], raw[:, s, :], MAGIC, MAGIC, ALU.add, ALU.max))
                    if p.n["block"] > SLOTS:
                        dve.wait_ge(block_used, p.value("block", SLOTS))
                    v.tensor_scalar(q2[:, s, :], raw[:, s, :], MAGIC + QMAX, MAGIC + QMID, ALU.min, ALU.subtract)\
                     .then_inc(lo_ready, 1)

            def x_stats(b, c):
                return v.bn_stats(stats[:, (b * NC + c) * 6:(b * NC + c) * 6 + 6],
                                  x[:, b * D + c * W:b * D + (c + 1) * W])

            def chunk_stats(c):
                own_drains()
                for b in range(B):
                    last = x_stats(b, c)
                link(last)

            def rstd_all():
                st = stats[:, :].rearrange("p (b k) -> p b k", b=B)
                for b in range(B):
                    last = v.bn_aggr(mv[:, 2 * b:2 * b + 2], st[:, b, :])
                link(last)
                link(v.tensor_scalar(var, mv.rearrange("p (b k) -> p b k", k=2)[:, :, 1], LN_EPS, None, ALU.add))
                link(v.tensor_scalar(rstd.bitcast(I32), var.bitcast(I32), 1, None, ALU.logical_shift_right))
                link(v.tensor_scalar(rstd.bitcast(I32), rstd.bitcast(I32), -1.0, float(0x5F3759DF), ALU.mult, ALU.add))
                for _ in range(4):
                    link(v.scalar_tensor_tensor(nt1, rstd, -0.5, rstd, ALU.mult, ALU.mult))
                    link(v.tensor_tensor(nt1, nt1, var, ALU.mult))
                    link(v.scalar_tensor_tensor(rstd, nt1, 1.5, rstd, ALU.add, ALU.mult))

            def normalise(b, dst):
                return v.tensor_scalar(dst, x[:, b * D:(b + 1) * D], mv[:, 2 * b:2 * b + 1], rstd[:, b:b + 1],
                                       ALU.subtract, ALU.mult)

            def transposed_lo(hi_, lo_):
                for j in range(4):
                    dve.wait_ge(act_done, p.next("act_done"))
                    v.tensor_tensor(lo_(j), psum[:, bank(p), :].rearrange("p (k t) -> p k t", t=P),
                                    hi_(j).bitcast(F32), ALU.subtract).then_inc(bank_drained, 1)
                    p.next("bank")
                    p.next("step")

            def ln_lo(b):
                transposed_lo(lambda j: xt_hi[:, 4 * j:4 * j + 4, b * P:(b + 1) * P],
                              lambda j: xt_lo[:, 4 * j:4 * j + 4, b * P:(b + 1) * P])

            def layer_norm():
                rstd_all()
                for b in range(2):
                    normalise(b, wide[b][:, :]).then_inc(ask_pe, 1)
                for b in range(B):
                    ln_lo(b)
                    if b + 2 < B:
                        normalise(b + 2, wide[b][:, :]).then_inc(ask_pe, 1)

            def want_bias():
                own_drains()
                v.memset(nt1, 0.0).then_inc(bias_room, 1)

            def add_bias():
                dve.wait_ge(bias_loaded, 16 * p.next("bias"))
                for b in range(B):
                    last = v.tensor_tensor(x[:, b * D:(b + 1) * D], x[:, b * D:(b + 1) * D], wide[1][:, :], ALU.add)
                link(last)

            def epilogue(col, blocks):
                if blocks:
                    dve.wait_ge(block_used, p.next("done", blocks))
                own_drains()
                for b in range(B):
                    if isinstance(col, int):
                        xs = x[:, b * D + col * W:b * D + (col + 1) * W]
                    else:
                        xs = x[:, ds(col * W + b * D, W)]
                    v.tensor_tensor(xs, psum[:, bank(p), :], xs, ALU.add).then_inc(bank_drained, 1)
                    p.next("bank")

            def ask(ins):
                ins.then_inc(ask_act, 1)
                p.next("ask_act")

            def answered():
                dve.wait_ge(act_done, p.next("act_done"))

            def by_expert(t, n=E0):
                return t.rearrange("p (b e) -> p b e", b=B)

            def over(t, n=E0):
                return t.unsqueeze(2).to_broadcast([P, B, n])

            def top2():
                rk = rank[:, :, :]
                for m, oh, among in ((m1, oh1, pr), (m2, oh2, cand)):
                    link(v.tensor_reduce(m, by_expert(among), AX, ALU.max))
                    link(v.tensor_tensor(by_expert(t8), by_expert(among), over(m), ALU.is_equal))
                    link(v.tensor_tensor(by_expert(t8), by_expert(t8), rk, ALU.mult))
                    link(v.tensor_reduce(msum, by_expert(t8), AX, ALU.max))
                    link(v.tensor_tensor(by_expert(oh), rk, over(msum), ALU.is_equal))
                    if m is m1:
                        link(v.scalar_tensor_tensor(cand, oh, -2.0, pr, ALU.mult, ALU.add))

            def softmax8(lgv):
                link(v.tensor_reduce(m1, lgv, AX, ALU.max))
                ask(v.tensor_tensor(by_expert(pr), lgv, over(m1), ALU.subtract))
                answered()
                link(v.tensor_reduce(m1, by_expert(pr), AX, ALU.add))
                link(v.reciprocal(m1, m1))
                link(v.tensor_tensor(by_expert(pr), by_expert(pr), over(m1), ALU.mult))

            dve.wait_ge(tables_made, 3)
            dve.wait_ge(consts_loaded, 16)
            link(v.reciprocal(quant[:, 0:1], cst[:, C_S1:C_S1 + 1]))
            link(v.tensor_scalar(quant[:, 2:3], cst[:, C_Z1:C_Z1 + 1], -1.0, QMID, ALU.mult, ALU.add))
            link(v.tensor_scalar(quant[:, 3:4], cst[:, C_Z2:C_Z2 + 1], -1.0, QMID, ALU.mult, ALU.add))
            link(v.tensor_scalar(quant[:, 4:5], quant[:, 2:3], quant[:, 3:4], float(D), ALU.mult, ALU.mult))
            link(v.tensor_scalar(quant[:, 5:6], cst[:, C_S1:C_S1 + 1], cst[:, C_S2:C_S2 + 1], None, ALU.mult))
            ask(v.reciprocal(quant[:, 1:2], cst[:, C_S2:C_S2 + 1]))
            for b in range(B):
                dve.wait_ge(x_loaded[b], 16)
                for c in range(NC):
                    last = x_stats(b, c)
            link(last)
            rstd_all()

            def quantise(b):
                t = wide[b % 2][:, :]
                link(normalise(b, t))
                link(v.tensor_scalar(t, t, quant[:, 0:1], cst[:, C_Z1:C_Z1 + 1], ALU.mult, ALU.add))
                link(v.tensor_scalar(t, t, MAGIC, MAGIC, ALU.add, ALU.max))
                link(v.tensor_scalar(t, t, MAGIC + QMAX, MAGIC + QMID, ALU.min, ALU.subtract))
                v.tensor_reduce(rows[:, b:b + 1], t, AX, ALU.add).then_inc(ask_pe, 1)

            def q1_drain(b):
                for j in range(4):
                    dve.wait_ge(step_done, p.next("step"))
                    v.tensor_copy(q1t[:, b * D + j * W:b * D + (j + 1) * W], psum[:, bank(p), :])\
                     .then_inc(bank_drained, 1)
                    p.next("bank")

            quantise(0)
            quantise(1)
            for b in range(B):
                q1_drain(b)
                if b + 2 < B:
                    quantise(b + 2)
            link(v.tensor_scalar(rows, rows, quant[:, 3:4], quant[:, 4:5], ALU.mult, ALU.add))
            round_block(LEAD)

            def dequantise(b, h):
                answered()
                own_drains()
                k = bank(p)
                t = wide[h][:, 0:BLK]
                p.next("bank", 4)
                v.scalar_tensor_tensor(t, psum[:, k:k + 2, :].rearrange("p a n -> p (a n)"), row_now, t,
                                       ALU.add, ALU.add).then_inc(bank_drained, 4)
                own_drains()
                xs = x[:, ds(b * D + h * BLK, BLK)] if not isinstance(b, int) else \
                    x[:, b * D + h * BLK:b * D + (h + 1) * BLK]
                link(v.scalar_tensor_tensor(xs, t, quant[:, 5:6], xs, ALU.mult, ALU.add))

            with p.loop(B - 1, block=2 * KT, bank=8, act_done=2, link=2 * KT + 3) as b:
                link(v.tensor_copy(row_now, rows[:, ds(b, 1)]))
                for h in range(2):
                    round_block(KT)
                    dequantise(b, h)
            link(v.tensor_copy(row_now, rows[:, B - 1:B]))
            round_block(KT)
            dequantise(B - 1, 0)
            round_block(KT - LEAD)
            split(LEAD)
            dequantise(B - 1, 1)
            p.n["done"] = N_CTX

            for c in range(NC):
                chunk_stats(c)
            layer_norm()
            own_drains()
            for j, dst in ((0, wide[0]), (1, wide[1])):
                split(KT // 2)
                dve.wait_ge(block_used, p.next("done", KT // 2))
                for t in range(4):
                    v.tensor_scalar(dst[:, t * TOK:(t + 1) * TOK], psum[:, bank(p), :],
                                    cst[:, C_BQK + 4 * j + t:C_BQK + 4 * j + t + 1], None, ALU.add)\
                     .then_inc(bank_drained, 1)
                    p.next("bank")
            split(KT // 2)
            dve.wait_ge(block_used, p.next("done", KT // 2))
            for b in range(B):
                v.tensor_tensor(wide[2][:, b * HD:(b + 1) * HD], psum[:, bank(p), :], cst[:, C_BV:C_BV + HD],
                                ALU.add).then_inc(bank_drained, 1)
                p.next("bank")
            dve.wait_ge(step_done, p.next("step", 4))
            k = bank(p)
            link(v.tensor_reduce(nmax, psum[:, k:k + 4, 0:P], AX, ALU.max))
            ask(v.tensor_scalar(nmax, nmax, -HD ** -0.5, None, ALU.mult))
            dve.wait_ge(act_done, p.next("act_done", 4))
            p.next("bank", 4)
            v.reciprocal(rsum, esum).then_inc(bank_drained, 4)
            own_drains()
            for b in range(B):
                last = v.tensor_scalar(wide[0][:, b * P:(b + 1) * P], wide[0][:, b * P:(b + 1) * P], rsum[:, b:b + 1],
                                       None, ALU.mult)
            last.then_inc(ask_pe, 1)
            want_bias()
            for b in range(B):
                dve.wait_ge(step_done, p.next("step"))
                v.tensor_copy(wide[0][:, TOK + b * P:TOK + (b + 1) * P], psum[:, bank(p), 0:P])\
                 .then_inc(bank_drained, 1)
                p.next("bank")
            for j in range(4):
                answered()
                v.tensor_tensor(th_lo[0][:, j, :], psum[:, bank(p), :], th_hi[0][:, j, :].bitcast(F32),
                                ALU.subtract).then_inc(bank_drained, 1)
                p.next("bank")
                p.next("step")
            add_bias()
            for c in range(NC):
                split(2)
                epilogue(c, 2)
                chunk_stats(c)

            layer_norm()
            want_bias()
            split(-(-KT // KB0))
            smx = wide[2][:, 0:B * SM0].rearrange("p (b n) -> p b n", b=B)
            dve.wait_ge(block_used, p.next("done", -(-KT // KB0)))
            k = bank(p)
            p.next("bank", 4)
            v.tensor_copy(smx, psum[:, k:k + 4, 0:SM0]).then_inc(bank_drained, 4)
            own_drains()
            softmax8(smx[:, :, 0:E0])
            top2()
            link(v.tensor_tensor(msum, m1, m2, ALU.add))
            link(v.reciprocal(msum, msum))
            for m, oh in ((m1, oh1), (m2, oh2)):
                link(v.scalar_tensor_tensor(m, m, 2.0, msum, ALU.mult, ALU.mult))
                link(v.tensor_tensor(by_expert(oh), by_expert(oh), over(m), ALU.mult))
            link(v.tensor_tensor(oh1, oh1, oh2, ALU.add))
            hw = wide[2][:, 1024:1024 + B * E0 * R0]
            for b in range(B):
                last = v.tensor_tensor(
                    hw[:, b * P:(b + 1) * P].rearrange("p (e r) -> p e r", e=E0),
                    smx[:, b, E0:SM0].rearrange("p (e r) -> p e r", e=E0),
                    oh1[:, b * E0:(b + 1) * E0].unsqueeze(2).to_broadcast([P, E0, R0]), ALU.mult)
            last.then_inc(ask_pe, 1)
            add_bias()

            def chunk_pairs():
                with p.loop(2, block=KT, done=KT, bank=8) as t:
                    for i in range(2):
                        split(KT // 2)
                        epilogue(t * 2 + i, KT // 2)

            def lora(rows_, stat):
                for b in range(B):
                    answered()
                    v.tensor_tensor(th_lo[0][0:rows_, 0, b * P:(b + 1) * P], psum[0:rows_, bank(p), 0:P],
                                    th_hi[0][0:rows_, 0, b * P:(b + 1) * P].bitcast(F32),
                                    ALU.subtract).then_inc(bank_drained, 1)
                    p.next("bank")
                    p.next("step")
                for c in range(NC):
                    split(1)
                    epilogue(c, 1)
                    if stat:
                        chunk_stats(c)

            chunk_pairs()
            lora(E0 * R0, True)

            def query_lo(b):
                if isinstance(b, int):
                    normalise(b, wide[1][:, :]).then_inc(ask_pe, 1)
                else:
                    link(v.tensor_copy(order_now[:, 0:1], mv[:, ds(b * 2, 1)]))
                    link(v.tensor_copy(order_now[:, 1:2], rstd[:, ds(b, 1)]))
                    v.tensor_scalar(wide[1][:, :], x[:, ds(b * D, D)], order_now[:, 0:1], order_now[:, 1:2],
                                    ALU.subtract, ALU.mult).then_inc(ask_pe, 1)
                transposed_lo(lambda j: xt_hi[:, 4 * j:4 * j + 4, 0:P], lambda j: xt_lo[:, 4 * j:4 * j + 4, 0:P])

            def probs_lo():
                transposed_lo(lambda j: xt_hi[:, 4 * j:4 * j + 4, P:2 * P],
                              lambda j: xt_lo[:, 4 * j:4 * j + 4, P:2 * P])

            def score_max(k):
                dve.wait_ge(block_used, p.next("done", 2 * KT))
                link(v.tensor_reduce(m1[:, 0:1], psum[:, k:k + 4, :].rearrange("p a n -> p (a n)"), AX, ALU.max))
                ask(v.tensor_scalar(nmax[:, 0:1], m1[:, 0:1], -1.0, None, ALU.mult))

            def attended(b):
                dve.wait_ge(block_used, p.next("done", 2 * KT))
                own_drains()
                for c in range(NC):
                    xs = x[:, b * D + c * W:b * D + (c + 1) * W] if isinstance(b, int) else x[:, ds(b * D + c * W, W)]
                    v.scalar_tensor_tensor(xs, psum[:, bank(p), :], rsum[:, 0:1], xs, ALU.mult, ALU.add)\
                     .then_inc(bank_drained, 1)
                    p.next("bank")
                own_drains()
                for c in range(NC):
                    if isinstance(b, int):
                        last = x_stats(b, c)
                    else:
                        last = v.bn_stats(stats[:, ds(b * NC * 6 + c * 6, 6)], x[:, ds(b * D + c * W, W)])
                link(last)

            rstd_all()
            query_lo(0)
            split(2 * KT)
            score_max(bank(p))
            answered()
            p.next("bank", 4)
            v.reciprocal(rsum[:, 1:2], esum[:, 0:1]).then_inc(bank_drained, 4)
            own_drains()
            with p.loop(B - 1, block=4 * KT, done=4 * KT, bank=16, step=8, act_done=9, ask_act=1, link=5) as b:
                query_lo(b + 1)
                split(2 * KT)
                k = bank(p)
                p.next("bank", 4)
                score_max(k)
                link(v.tensor_copy(rsum[:, 0:1], rsum[:, 1:2]))
                for j in range(4):
                    answered()
                    kk = (bank(p) + j) % BANKS
                    last = v.tensor_tensor(xt_lo[:, 4 * j:4 * j + 4, P:2 * P],
                                           psum[:, kk, :].rearrange("p (k t) -> p k t", t=P),
                                           xt_hi[:, 4 * j:4 * j + 4, P:2 * P].bitcast(F32), ALU.subtract)
                    last.then_inc(ask_pe, 1)
                    p.next("step")
                answered()
                v.reciprocal(rsum[:, 1:2], esum[:, 0:1]).then_inc(bank_drained, 8)
                p.next("bank", 4)
                split(2 * KT)
                attended(b)
            probs_lo()
            link(v.tensor_copy(rsum[:, 0:1], rsum[:, 1:2]))
            split(2 * KT)
            attended(B - 1)

            link(v.memset(ediff, 0.0))
            link(v.tensor_scalar(ediff[:, 1:2], cst[:, C_DF:C_DF + 1], -1.0, None, ALU.mult))
            ask(v.tensor_tensor(ediff[:, 2:G + 1], cst[:, C_DF:C_DF + G - 1], cst[:, C_DF + 1:C_DF + G], ALU.subtract))
            link(v.memset(taylor[:, G + 1:G + 1 + GRAD_ORDER_MIN + 1], 1.0))
            link(v.memset(taylor[:, G + 2 + GRAD_ORDER_MIN:2 * (G + 1)], 0.0))
            answered()
            layer_norm()
            t_now, delta, keep = wide[0], wide[1], wide[2]
            split(KT // 2)
            dve.wait_ge(block_used, p.next("done", KT // 2))
            own_drains()
            for j in range(4):
                v.tensor_copy(t_now[:, j * TOK:(j + 1) * TOK], psum[:, bank(p), :]).then_inc(bank_drained, 1)
                p.next("bank")
            split(KT // 2)
            dve.wait_ge(block_used, p.next("done", KT // 2))
            for j in range(4):
                v.tensor_scalar(delta[:, j * TOK:(j + 1) * TOK], psum[:, bank(p), :],
                                cst[:, C_LP + j:C_LP + j + 1], None, ALU.subtract).then_inc(bank_drained, 1)
                p.next("bank")
            own_drains()
            link(v.tensor_scalar(keep[:, :], delta[:, :], -1.0, None, ALU.mult))
            link(v.tensor_tensor(keep[:, :], keep[:, :], delta[:, :], ALU.max))
            link(v.tensor_scalar(keep[:, :], keep[:, :], THD, None, ALU.is_le))

            def term_lo(i):
                answered()
                v.tensor_tensor(th_lo[i][:, :, :], t_now[:, :].rearrange("p (k t) -> p k t", k=4),
                                th_hi[i][:, :, :].bitcast(F32), ALU.subtract).then_inc(ask_pe, 1)

            def next_term(m):
                link(v.tensor_copy(order_now[:, 0:1], taylor[:, ds(m, 1)]))
                link(v.tensor_copy(order_now[:, 1:2], taylor[:, ds(m + (G + 1), 1)]))
                link(v.scalar_tensor_tensor(t_now[:, :], t_now[:, :], order_now[:, 0:1], delta[:, :],
                                            ALU.mult, ALU.mult))
                ask(v.scalar_tensor_tensor(t_now[:, :], keep[:, :], order_now[:, 1:2], t_now[:, :],
                                           ALU.max, ALU.mult))

            ask(v.tensor_copy(order_now[:, 0:1], taylor[:, 0:1]))
            term_lo(0)
            with p.loop(G // 2, block=4 * NC, done=4 * NC, bank=32, act_done=2, ask_act=2, link=6) as t:
                for i in range(2):
                    next_term(t * 2 + (i + 1))
                    term_lo(1 - i)
                    for c in range(NC):
                        split(2)
                        epilogue(c, 2)
            for c in range(NC):
                split(2)
                epilogue(c, 2)

            def gated(i, tiles, blocks):
                k = bank(p)
                n = tiles * W
                p.next("done", blocks)
                answered()
                link(v.tensor_tensor(wide[0][:, 0:n], wide[0][:, 0:n],
                                     psum[:, k:k + tiles, :].rearrange("p a n -> p (a n)"), ALU.mult))
                ask(v.tensor_tensor(wide[1][:, 0:n], wide[0][:, 0:n],
                                    psum[:, k + tiles:k + 2 * tiles, :].rearrange("p a n -> p (a n)"), ALU.mult))
                answered()
                p.next("bank", 2 * tiles)
                v.tensor_tensor(th_lo[i][:, 0:tiles, :], wide[1][:, 0:n].rearrange("p (k t) -> p k t", t=TOK),
                                th_hi[i][:, 0:tiles, :].bitcast(F32), ALU.subtract).then_inc(bank_drained, 2 * tiles)

            def down(stat=False):
                for c in range(NC):
                    split(1)
                    epilogue(c, 1)
                    if stat:
                        chunk_stats(c)

            split(KT // 2)
            gated(0, 2, KT // 2)
            with p.loop(UNITS // 2, block=2 * (KT // 2 + NC), done=2 * (KT // 2 + NC), bank=40, act_done=4,
                        ask_act=2, link=2):
                for i in range(2):
                    split(KT // 2)
                    gated(1 - i, 2, KT // 2)
                    down()
            split(KT // 4)
            gated(1, 1, KT // 4)
            down()
            down(stat=True)

            layer_norm()
            want_bias()
            split(1)
            dve.wait_ge(block_used, p.next("done", 1))
            k = bank(p)
            p.next("bank", 4)
            zc = wide[2][:, 0:B * SM1].rearrange("p (b n) -> p b n", b=B)
            for b in range(B):
                last = v.tensor_copy(wide[2][:, b * SM1:(b + 1) * SM1], psum[:, (k + b) % BANKS, 0:SM1])
            last.then_inc(bank_drained, 4)
            own_drains()
            z = zc[:, :, E1:SM1]
            hdv = hd.rearrange("p (b k e) -> p b k e", b=B, k=2)
            limes = cst[:, C_LIM:C_LIM + E1 * R1].rearrange("p (e r) -> p e r", e=E1)
            prod = wide[2][:, 512:512 + B * E1 * R1]
            link(v.tensor_tensor(hdv[:, :, 0, :], zc[:, :, 0:E1],
                                 cst[:, C_B8:C_B8 + E1].unsqueeze(1).to_broadcast([P, B, E1]), ALU.add))
            for b in range(B):
                last = v.tensor_tensor(prod[:, b * E1 * R1:(b + 1) * E1 * R1].rearrange("p (e r) -> p e r", e=E1),
                                       z[:, b, :].unsqueeze(1).to_broadcast([P, E1, R1]), limes, ALU.mult)
            link(last)
            v.tensor_reduce(hdv[:, :, 1, :], prod.rearrange("p (b e r) -> p b e r", b=B, e=E1), AX, ALU.add)\
             .then_inc(ask_pe, 1)
            dve.wait_ge(step_done, p.next("step", 4))
            k = bank(p)
            p.next("bank", 4)
            v.tensor_copy(lg, psum[:, k, 0:B * 2 * E1]).then_inc(bank_drained, 4)
            own_drains()
            lgv = lg.rearrange("p (b k e) -> p b k e", b=B, k=2)
            for i in range(2):
                link(v.tensor_scalar(by_expert(t8), lgv[:, :, i, :], -1.0, None, ALU.mult))
                link(v.tensor_tensor(by_expert(t8), by_expert(t8), lgv[:, :, i, :], ALU.max))
                last = v.tensor_reduce(gm[:, i:i + 1], t8, AX, ALU.max)
                if i == 0:
                    link(last)
            last.then_inc(ask_pool, 1)
            dve.wait_ge(pool_done, 1)
            link(v.tensor_scalar(gmall, gmall, 1e-6, None, ALU.max))
            link(v.reciprocal(gmall, gmall))
            link(v.tensor_scalar(gmall, gmall, 0.5, None, ALU.mult))
            link(v.tensor_scalar(lgv[:, :, 0, :], lgv[:, :, 0, :], gmall[:, 0:1], None, ALU.mult))
            link(v.scalar_tensor_tensor(by_expert(t8), lgv[:, :, 1, :], gmall[:, 1:2], lgv[:, :, 0, :],
                                        ALU.mult, ALU.add))
            softmax8(by_expert(t8))
            top2()
            ask(v.tensor_tensor(by_expert(t8), by_expert(pr), over(m2), ALU.subtract))
            answered()
            link(v.tensor_tensor(pr, pr, t8, ALU.mult))
            link(v.tensor_reduce(msum, by_expert(pr), AX, ALU.add))
            link(v.tensor_scalar(msum, msum, 1e-9, None, ALU.add))
            link(v.reciprocal(msum, msum))
            link(v.scalar_tensor_tensor(by_expert(pr), by_expert(pr), 0.5, over(msum), ALU.mult, ALU.mult))
            for b in range(B):
                last = v.tensor_tensor(
                    prod[:, b * E1 * R1:(b + 1) * E1 * R1].rearrange("p (r e) -> p r e", e=E1),
                    pr[:, b * E1:(b + 1) * E1].unsqueeze(1).to_broadcast([P, R1, E1]),
                    cst[:, C_LIM:C_LIM + E1 * R1].rearrange("p (e r) -> p r e", e=E1), ALU.mult)
            link(last)
            mix = wide[2][:, 1600:1600 + B * R1].rearrange("p (b r) -> p b r", b=B)
            link(v.tensor_reduce(mix, prod.rearrange("p (b r e) -> p b r e", b=B, e=E1), AX, ALU.add))
            v.tensor_tensor(mix, mix, z, ALU.mult).then_inc(ask_pe, 1)
            add_bias()
            chunk_pairs()
            lora(R1, False)

        @block.tensor
        def _(pe):
            p = Place(pe)
            mm = nc.tensor.matmul

            def free_bank():
                k = bank(p)
                if p.n["bank"] >= BANKS:
                    pe.wait_ge(bank_drained, p.value("bank", BANKS - 1))
                p.next("bank")
                return k

            def all_drained():
                pe.wait_ge(bank_drained, p.value("bank"))

            def asked(k=1):
                pe.wait_ge(ask_pe, p.next("ask_pe", k))

            def three(dst, st, mv_, first, last):
                (sh, sl), (mh, ml) = st, mv_
                mm(dst, sh, mh, start=first, stop=False)
                mm(dst, sh, ml, start=False, stop=False)
                return mm(dst, sl, mh, start=False, stop=last)

            def transposes(src, rows_=P):
                for j in range(4):
                    k = free_bank()
                    for i, tile in enumerate(src(j)):
                        last = nc.tensor.transpose(psum[0:rows_, k, i * P:(i + 1) * P], tile, ident[:, :])
                    last.then_inc(step_done, 1)

            def tiles4(t):
                return lambda j: [t[:, (4 * j + i) * P:(4 * j + i + 1) * P] for i in range(4)]

            def ln_transposes():
                for b in range(B):
                    asked()
                    transposes(tiles4(wide[b % 2]))
                all_drained()

            def blocks(n, products):
                banks = None
                for i in range(n):
                    s = p.n["block"] % SLOTS
                    pe.wait_ge(lo_ready, p.next("block"))
                    todo = products(i, s)
                    if banks is None:
                        banks = {}
                    for j, st, mv_, width, first, last in todo:
                        if j not in banks:
                            banks[j] = free_bank()
                        ins = three(psum[:, banks[j], 0:width], st, mv_, first, last)
                    ins.then_inc(block_used, 1)

            def part(s, a, n, rows_=P):
                return (hi[0:rows_, s, a:a + n], lo[0:rows_, s, a:a + n])

            def tokens(t, k, b, rows_=P):
                return (t[0][0:rows_, k, b * P:(b + 1) * P], t[1][0:rows_, k, b * P:(b + 1) * P])

            xt = (xt_hi, xt_lo)
            th = list(zip(th_hi, th_lo))

            def token_major(t, n_kt, per_block, width, rows_=P):
                def products(i, s):
                    return [(b, tokens(t, k, b, rows_), part(s, (k - i * per_block) * width, width, rows_), width,
                             k == 0, k == n_kt - 1)
                            for k in range(i * per_block, min(n_kt, (i + 1) * per_block)) for b in range(B)]
                blocks(-(-n_kt // per_block), products)

            def feature_major(tiles=4):
                per_block = BLK // (tiles * P)

                def products(i, s):
                    return [(j, part(s, ((k - i * per_block) * tiles + j) * P, P), (xt_hi[:, k, :], xt_lo[:, k, :]),
                             TOK, k == 0, k == KT - 1)
                            for k in range(i * per_block, (i + 1) * per_block) for j in range(tiles)]
                blocks(KT // per_block, products)

            pe.wait_ge(tables_made, 3)
            for b in range(B):
                asked()
                transposes(tiles4(wide[b % 2]))
            all_drained()
            with p.loop(B, block=2 * KT, bank=8) as b:
                for h in range(2):
                    ks = [free_bank() for _ in range(4)]
                    for i in range(KT):
                        s = p.n["block"] % SLOTS
                        pe.wait_ge(lo_ready, p.next("block"))
                        for j in range(2):
                            mm(psum[:, ks[j], :], q1t[:, ds(b * D + i * P, P)], q2[:, s, j * W:(j + 1) * W],
                               start=i == 0, stop=i == KT - 1)
                        for j in range(2):
                            ins = mm(psum[:, ks[2 + j], :], ones[:, :], q2[:, s, j * W:(j + 1) * W],
                                     start=i == 0, stop=i == KT - 1)
                        ins.then_inc(block_used, 1)

            ln_transposes()
            feature_major()
            feature_major()
            token_major(xt, KT, 2, W)
            all_drained()
            for b in range(B):
                k = free_bank()
                for j in range(4):
                    last = mm(psum[:, k, 0:P], wide[0][:, j * TOK + b * P:j * TOK + (b + 1) * P],
                              wide[1][:, j * TOK + b * P:j * TOK + (b + 1) * P], start=j == 0, stop=j == 3)
                last.then_inc(step_done, 1)
            asked()
            for b in range(B):
                nc.tensor.transpose(psum[:, free_bank(), 0:P], wide[0][:, b * P:(b + 1) * P], ident[:, :])\
                  .then_inc(step_done, 1)
            all_drained()
            for j in range(4):
                k = free_bank()
                for b in range(B):
                    last = mm(psum[:, k, b * P:(b + 1) * P], wide[2][:, b * HD + j * P:b * HD + (j + 1) * P],
                              wide[0][:, TOK + b * P:TOK + (b + 1) * P], start=True, stop=True)
                last.then_inc(step_done, 1)
            all_drained()
            for c in range(NC):
                token_major(th[0], 4, 2, W)

            def chunk_pairs():
                with p.loop(2, block=KT, bank=8):
                    for _ in range(2):
                        token_major(xt, KT, 2, W)

            ln_transposes()
            token_major(xt, KT, KB0, SM0)
            chunk_pairs()
            asked()
            for b in range(B):
                nc.tensor.transpose(psum[:, free_bank(), 0:P], wide[2][:, 1024 + b * P:1024 + (b + 1) * P], ident[:, :])\
                  .then_inc(step_done, 1)
            all_drained()
            for c in range(NC):
                token_major(th[0], 1, 1, W)

            def rows_major(col):
                def products(i, s):
                    k, half = i // 2, i % 2
                    st = (xt_hi[:, k, col:col + P], xt_lo[:, k, col:col + P])
                    return [(2 * half + j, st, part(s, j * W, W), W, k == 0, k == KT - 1) for j in range(2)]
                blocks(2 * KT, products)

            def scores():
                asked()
                transposes(tiles4(wide[1]))
                all_drained()
                rows_major(0)

            scores()
            with p.loop(B - 1, block=4 * KT, bank=16, ask_pe=5):
                asked()
                transposes(tiles4(wide[1]))
                all_drained()
                rows_major(0)
                transposes(tiles4(wide[0]))
                asked(4)
                rows_major(P)
            all_drained()
            transposes(tiles4(wide[0]))
            all_drained()
            rows_major(P)

            ln_transposes()
            feature_major()
            feature_major()
            with p.loop(G // 2, block=4 * NC, bank=32, ask_pe=2):
                for i in range(2):
                    asked()
                    for c in range(NC):
                        token_major(th[i], 4, 2, W)
            asked()
            for c in range(NC):
                token_major(th[0], 4, 2, W)

            feature_major()
            with p.loop(UNITS // 2, block=2 * (KT // 2 + NC), bank=40):
                for i in range(2):
                    feature_major()
                    for c in range(NC):
                        token_major(th[i], 2, 2, W)
            feature_major(tiles=2)
            for i, kt in ((0, 2), (1, 1)):
                for c in range(NC):
                    token_major(th[i], kt, 2, W)

            ln_transposes()
            token_major(xt, KT, KT, SM1)
            asked()
            k = free_bank()
            for _ in range(3):
                free_bank()
            mm(psum[:, k, 0:B * 2 * E1], pick[:, :], hd, start=True, stop=True).then_inc(step_done, 4)
            chunk_pairs()
            asked()
            for b in range(B):
                nc.tensor.transpose(psum[0:R1, free_bank(), 0:P], wide[2][:, 1600 + b * R1:1600 + (b + 1) * R1],
                                    ident[:, :]).then_inc(step_done, 1)
            all_drained()
            for c in range(NC):
                token_major(th[0], 1, 1, W, R1)
            assert p.n["bank"] == TOTAL_BANKS and p.n["block"] == N_BLOCKS, (p.n["bank"], p.n["block"], N_BLOCKS)


TOTAL_BANKS = (16 + 8 * B) + (16 + 12 + 12 + 16) + (16 + 4 + 16 + 4 + 16) + 16 * B \
    + (16 + 8 + 16 * (G + 1) + 20 * UNITS + 2 + 16) + (16 + 4 + 4 + 16 + 4 + 16)


def tiled(w, tiles_per_block=2):
    k, n = w.shape
    kt = k // P
    nb = -(-kt // tiles_per_block)
    out = np.zeros((nb, P, BLK), np.float32)
    for i in range(nb):
        part = w[i * tiles_per_block * P:(i + 1) * tiles_per_block * P]
        m = part.shape[0] // P
        out[i, :, :m * n] = part.reshape(m, P, n).transpose(1, 0, 2).reshape(P, m * n)
    return out


def chunks(w, tiles_per_block=2):
    return [tiled(w[:, c * W:(c + 1) * W], tiles_per_block) for c in range(NC)]


def halves(w):
    return w.reshape(KT, P, 2, BLK).transpose(2, 0, 1, 3)


def kernel(x, ctx_4096, L0_xattn_x1_scale, L0_xattn_x1_zp, L0_xattn_x2_scale, L0_xattn_x2_zp, L0_attn_Wqkv,
           L0_attn_bqkv, L0_attn_Wo, L0_attn_bo, L0_ffn_W_base, L0_ffn_b_base, L0_ffn_W_router, L0_ffn_A, L0_ffn_B,
           L1_attn_up_w, L1_attn_gate_w, L1_attn_local_point, L1_attn_local_approx_output, L1_attn_fuse_weight,
           L1_attn_discount_factor, L1_attn_ffn_gate_w, L1_attn_ffn_up_w, L1_attn_ffn_down_w, L1_ffn_W, L1_ffn_b,
           L1_ffn_A, L1_ffn_Bmat, L1_ffn_LiMEs):
    import concourse.bacc as bacc
    from concourse.bass_utils import run_bass_kernel_spmd

    c = np.asarray(ctx_4096)
    parts = [halves(c[b]).reshape(-1, P, BLK) for b in range(B)]
    wqkv = np.asarray(L0_attn_Wqkv)
    parts += [tiled(wqkv[:, i * HD:(i + 1) * HD]) for i in range(3)]
    parts += chunks(np.asarray(L0_attn_Wo))
    lora_a = np.asarray(L0_ffn_A).reshape(E0 * R0, D)
    parts += [tiled(np.concatenate([np.asarray(L0_ffn_W_router), lora_a]).T, KB0)]
    parts += chunks(np.asarray(L0_ffn_W_base).T)
    parts += chunks(np.asarray(L0_ffn_B).transpose(0, 2, 1).reshape(E0 * R0, D), 1)

    def rows(w):
        return halves(w).transpose(1, 0, 2, 3).reshape(-1, P, BLK)

    parts += [rows(c[0].T)]
    for b in range(1, B):
        parts += [rows(c[b].T), rows(c[b - 1])]
    parts += [rows(c[B - 1])]
    parts += [tiled(np.asarray(w).T) for w in (L1_attn_up_w, L1_attn_gate_w)]
    parts += chunks(np.asarray(L1_attn_local_approx_output).T)
    fuse = np.asarray(L1_attn_fuse_weight)
    for m in range(G):
        parts += chunks(fuse[:, :, m].T)
    gate, up, down = (np.asarray(w).T for w in (L1_attn_ffn_gate_w, L1_attn_ffn_up_w, L1_attn_ffn_down_w))

    def gate_up(j, tiles=2):
        f = slice(2 * j * P, (2 * j + tiles) * P)
        return tiled(np.concatenate([gate[:, f], up[:, f]], axis=1), BLK // (2 * tiles * P))

    def down_rows(j, tiles=2):
        return chunks(down[2 * j * P:(2 * j + tiles) * P])

    parts += [gate_up(0)]
    for j in range(1, UNITS):
        parts += [gate_up(j)] + down_rows(j - 1)
    parts += [gate_up(UNITS, 1)] + down_rows(UNITS - 1) + down_rows(UNITS, 1)
    w1 = np.asarray(L1_ffn_W).T
    parts += [tiled(np.concatenate([w1[:, :E1], np.asarray(L1_ffn_A)], axis=1), KT)]
    parts += chunks(w1)
    bmat = np.zeros((P, D), np.float32)
    bmat[:R1] = np.asarray(L1_ffn_Bmat)
    parts += chunks(bmat, 1)
    stream = np.concatenate(parts)
    assert stream.shape == (N_BLOCKS, P, BLK), stream.shape

    def wide_row(a):
        a = np.asarray(a).reshape(-1)
        return np.broadcast_to(a, (P, a.size))

    b1 = np.asarray(L1_ffn_b)
    bqkv = np.asarray(L0_attn_bqkv)
    consts = np.concatenate(
        [wide_row(a) for a in (L0_xattn_x1_scale, L0_xattn_x1_zp, L0_xattn_x2_scale, L0_xattn_x2_zp)]
        + [bqkv[:2 * HD].reshape(8, P).T, np.asarray(L1_attn_local_point).reshape(4, P).T]
        + [wide_row(a) for a in (L1_attn_discount_factor, b1[:E1], L1_ffn_LiMEs, bqkv[2 * HD:])], axis=1)
    assert consts.shape == (P, C_END)
    biases = np.stack([wide_row(a) for a in (L0_attn_bo, L0_ffn_b_base, b1)])

    arrays = {"x_in": np.asarray(x), "stream": stream, "biases": biases, "consts": consts}
    arrays = {k: np.ascontiguousarray(a) for k, a in arrays.items()}
    nc = bacc.Bacc("TRN2", target_bir_lowering=False, num_devices=1)
    args = [nc.dram_tensor(k, a.shape, F32, kind="ExternalInput").ap() for k, a in arrays.items()]
    out = nc.dram_tensor("x_out", (B, P, D), F32, kind="ExternalOutput").ap()
    build(nc, *args, out)
    return run_bass_kernel_spmd(nc, [arrays], core_ids=[0]).results[0]["x_out"]
```

```python
from collections import defaultdict
from contextlib import ExitStack, contextmanager

import numpy as np

import concourse.bass as bass
from concourse import mybir

F32 = mybir.dt.float32
F32R = mybir.dt.float32r
BF16 = mybir.dt.bfloat16
I32 = mybir.dt.int32
ALU = mybir.AluOpType
ACT = mybir.ActivationFunctionType
AX = mybir.AxisListType.X
RMAX = bass.bass_isa.ReduceOp.max
ds = bass.ds

P = 128
B = 4
TOK = B * P
D = 2048
KT = D // P
W = 512
NC = D // W
BLK = 1024
SLOTS = 4
LEAD = SLOTS
CTX_SLOTS = 8
CTX_LEAD = 7
BANKS = 8

HD = D // 4
E0, R0 = 8, 16
E1, R1 = 8, 32
SM1 = E1 + R1
S = 512
G = 6
F = 4992
FT = F // P
UNITS = FT // 2
LN_EPS = 1e-5
THD = 2.5
GRAD_ORDER_MIN = 4
MAGIC = 1.5 * 2.0 ** 23
QMAX = 255.0
QMID = 128.0

N_CTX = B * 2 * KT
N_BLOCKS = (N_CTX + 3 * KT // 2 + 2 * NC + KT // 4 + NC * KT // 2 + NC + 2 * N_CTX
            + KT + (G + 1) * 2 * NC + UNITS * (KT // 2 + NC) + KT // 4 + NC + KT // 8 + NC * KT // 2 + NC)

C_S1, C_Z1, C_S2, C_Z2, C_BQK, C_LP, C_DF = 0, 1, 2, 3, 4, 12, 16
C_B8 = C_DF + G
C_LIM = C_B8 + E1
C_BV = C_LIM + E1 * R1
C_END = C_BV + HD


class Place:

    def __init__(self, engine):
        self.engine, self.n, self.turn, self.per_turn = engine, defaultdict(int), None, {}

    def next(self, name, k=1):
        self.n[name] += k
        return self.value(name)

    def value(self, name, back=0):
        n = self.n[name] - back
        step = self.per_turn.get(name, 0)
        return n if self.turn is None or step == 0 else self.turn * step + n

    @contextmanager
    def loop(self, turns, **per_turn):
        before = dict(self.n)
        with self.engine.Fori(0, turns) as turn:
            self.turn, self.per_turn = turn, per_turn
            yield turn
        for name in self.n:
            moved = self.n[name] - before.get(name, 0)
            assert moved == per_turn.get(name, 0), (name, moved)
        self.turn, self.per_turn = None, {}
        for name, k in per_turn.items():
            self.n[name] = before.get(name, 0) + turns * k


def build(nc, x_in, stream, biases, consts, out):
    ctx = ExitStack()
    at = [-(-nc.sbuf_base // 64) * 64]

    def place(name, shape, dtype, offset=None):
        size = int(np.prod(shape[1:])) * (2 if dtype == BF16 else 4)
        if offset is None:
            offset, at[0] = at[0], at[0] + -(-size // 64) * 64
        return nc.alloc_sbuf_tensor_at(name, shape, dtype, offset=offset)

    with ctx:
        x = place("x_res", [P, B * D], F32)
        raw = place("raw", [P, SLOTS, BLK], F32)
        hi = place("hi", [P, SLOTS, BLK], F32R)
        lo = place("lo", [P, SLOTS, BLK], F32R)
        xt_at = at[0]
        xt_hi = place("xt_hi", [P, KT, TOK], F32R)
        xt_lo = place("xt_lo", [P, KT, TOK], F32R)
        ctx_raw = place("ctx_raw", [P, CTX_SLOTS, BLK], F32, offset=xt_at)
        q2 = place("q2", [P, SLOTS, BLK], BF16, offset=xt_at + 4 * CTX_SLOTS * BLK)
        q1t = place("q1t", [P, D], BF16, offset=xt_at + 4 * CTX_SLOTS * BLK + 2 * SLOTS * BLK)
        th_hi = [place(f"th_hi{i}", [P, 4, TOK], F32R) for i in range(2)]
        th_lo = [place(f"th_lo{i}", [P, 4, TOK], F32R) for i in range(2)]
        wide = [place(f"wide{i}", [P, D], F32) for i in range(3)]
        cst = place("cst", [P, C_END], F32)
        ident = place("ident", [P, P], F32)
        pick = place("pick", [P, P], F32)
        ones = place("ones", [P, P], BF16)
        rank = place("rank", [P, B, E0], F32)
        stats = place("stats", [P, B * NC * 6], F32)
        sm = place("sm", [P, 448], F32)
        assert at[0] <= nc.sbuf_usable_end, (at[0], nc.sbuf_usable_end)
        psum = ctx.enter_context(nc.psum_tensor("psum", [P, BANKS, W], F32))

        used = [0]

        def cells(n):
            used[0] += n
            assert used[0] <= 448
            return sm[:, used[0] - n:used[0]]

        mv, var, rstd, nt1 = cells(2 * B), cells(B), cells(B), cells(B)
        quant, row_next, row_now = cells(6), cells(1), cells(1)
        nmax, esum, rsum = cells(B), cells(B), cells(B)
        taylor, order_now, ediff = cells(2 * (G + 1)), cells(2), cells(G + 1)
        m1, m2, msum, gm, gmall = cells(B), cells(B), cells(B), cells(2), cells(2)
        pr, cand, oh1, oh2, t8 = (cells(B * E0) for _ in range(5))
        hd = cells(B * 2 * E1)
        lg = cells(B * 2 * E1)

        def sem(name):
            return ctx.enter_context(nc.semaphore(name))

        ctx_full = [sem(f"ctx_full{i}") for i in range(CTX_SLOTS)]
        raw_full = [sem(f"raw_full{i}") for i in range(SLOTS)]
        x_loaded = [sem(f"x_loaded{i}") for i in range(B)]
        consts_loaded = sem("consts_loaded")
        tables_made = sem("tables_made")
        hi_ready = sem("hi_ready")
        lo_ready = sem("lo_ready")
        block_used = sem("block_used")
        bank_drained = sem("bank_drained")
        step_done = sem("step_done")
        ask_act = sem("ask_act")
        act_done = sem("act_done")
        ask_pe = sem("ask_pe")
        dve_step = sem("dve_step")
        bias_room = sem("bias_room")
        bias_loaded = sem("bias_loaded")
        ask_pool = sem("ask_pool")
        pool_done = sem("pool_done")
        stored = sem("stored")

        block = ctx.enter_context(nc.Block())

        def bank(p):
            return p.n["bank"] % BANKS

        def batch_of(tile, b):
            return tile[:, :, b * P:(b + 1) * P]

        @block.sync
        def _(sp):
            def load(dst, n, landed):
                sp.dma_start(dst, stream[n, :, :] if isinstance(n, int) else
                             stream[ds(n, 1), :, :].rearrange("a p n -> p (a n)")).then_inc(landed, 16)

            for s in range(CTX_SLOTS):
                load(ctx_raw[:, s, :], s, ctx_full[s])
            with sp.Fori(1, N_CTX // CTX_SLOTS) as turn:
                for s in range(CTX_SLOTS):
                    sp.wait_ge(lo_ready, turn * CTX_SLOTS + (s + 1 - CTX_SLOTS))
                    load(ctx_raw[:, s, :], turn * CTX_SLOTS + s, ctx_full[s])
            for s in range(SLOTS):
                load(raw[:, s, :], N_CTX + s, raw_full[s])
            turns, rest = divmod(N_BLOCKS - N_CTX, SLOTS)
            with sp.Fori(1, turns) as turn:
                for s in range(SLOTS):
                    sp.wait_ge(lo_ready, turn * SLOTS + (N_CTX + s + 1 - SLOTS))
                    load(raw[:, s, :], turn * SLOTS + (N_CTX + s), raw_full[s])
            for s in range(rest):
                n = N_BLOCKS - rest + s
                sp.wait_ge(lo_ready, n + 1 - SLOTS)
                load(raw[:, s, :], n, raw_full[s])
            o = out.rearrange("b p n -> p b n")
            xv = x[:, :].rearrange("p (b n) -> p b n", b=B)
            for c in range(NC):
                sp.wait_ge(bank_drained, TOTAL_BANKS - 4 * (NC - 1 - c))
                sp.dma_start(o[:, :, c * W:(c + 1) * W], xv[:, :, c * W:(c + 1) * W]).then_inc(stored, 16)
            sp.wait_ge(stored, 16 * NC)

        @block.gpsimd
        def _(pool):
            pool.memset(ones[:, :], 1.0)
            for e in range(E0):
                pool.memset(rank[:, :, e:e + 1], float(E0 - e))
            pool.memset(ident[:, :], 0.0).then_inc(tables_made, 1)
            pool.wait_ge(tables_made, 1)
            pool.affine_select(out=ident[:, :], in_=ident[:, :], compare_op=ALU.not_equal, fill=1.0,
                               base=0, pattern=[[-1, P]], channel_multiplier=1).then_inc(tables_made, 1)
            pool.wait_ge(tables_made, 2)
            odd = ident[:, :].rearrange("p (j r) -> p j r", r=2)
            for r in range(2):
                last = pool.tensor_copy(pick[:, :].rearrange("p (j r) -> p j r", r=2)[:, :, r:r + 1],
                                        odd[:, :, 1:2])
            last.then_inc(tables_made, 1)
            for i in range(3):
                pool.wait_ge(bias_room, i + 1)
                pool.dma_start(wide[1][:, :], biases[i, :, :]).then_inc(bias_loaded, 16)
                if i == 2:
                    pool.wait_ge(bias_loaded, 48)
            pool.wait_ge(ask_pool, 1)
            pool.partition_all_reduce(gmall, gm, P, RMAX).then_inc(pool_done, 1)

        @block.scalar
        def _(act):
            p = Place(act)
            act.dma_start(cst[:, :], consts).then_inc(consts_loaded, 16)
            for b in range(B):
                act.dma_start(x[:, b * D:(b + 1) * D], x_in[b, :, :]).then_inc(x_loaded[b], 16)
                if b == 0:
                    act.wait_ge(x_loaded[0], 16)

            def landed(full, n):
                slots, turns = len(full), p.per_turn.get("block", 0)
                v = 16 * (n // slots + 1)
                if p.turn is not None and turns:
                    v = p.turn * (16 * turns // slots) + v
                act.wait_ge(full[n % slots], v)
                return n % slots

            def split(k):
                for _ in range(k):
                    if p.n["block"] >= N_BLOCKS:
                        return
                    s = landed(raw_full, p.n["block"] - N_CTX)
                    act.wait_ge(block_used, p.value("block", SLOTS - 1))
                    nc.scalar.activation(hi[:, s, :], raw[:, s, :], ACT.Copy).then_inc(hi_ready, 1)
                    p.next("block")

            def scale_block(k):
                for _ in range(k):
                    s = landed(ctx_full, p.n["block"])
                    nc.scalar.activation(ctx_raw[:, s, :], ctx_raw[:, s, :], ACT.Identity,
                                         bias=cst[:, C_Z2:C_Z2 + 1], scale=quant[:, 1:2]).then_inc(hi_ready, 1)
                    p.next("block")

            def answer(ins):
                ins.then_inc(act_done, 1)
                p.next("act_done")

            def transposed_hi(dst):
                for j in range(4):
                    act.wait_ge(step_done, p.next("step"))
                    answer(nc.scalar.activation(dst(j), psum[:, bank(p), :].rearrange("p (k t) -> p k t", t=P),
                                                ACT.Copy))
                    p.next("bank")

            def ln_hi():
                for b in range(B):
                    transposed_hi(lambda j: xt_hi[:, 4 * j:4 * j + 4, b * P:(b + 1) * P])

            def early_ln_hi():
                for b in range(B):
                    transposed_hi(lambda j: xt_hi[:, 4 * j:4 * j + 4, b * P:(b + 1) * P])
                    if b < B - 1:
                        p.next("bank", 4)

            def asked():
                act.wait_ge(ask_act, p.next("ask_act"))

            def skip(banks=0, steps=0):
                p.next("bank", banks)
                p.next("step", steps)

            def q1_copy():
                for j in range(4):
                    act.wait_ge(step_done, p.next("step"))
                    answer(nc.scalar.activation(q1t[:, j * W:(j + 1) * W], psum[:, bank(p), :], ACT.Copy))
                    p.next("bank")
                p.next("bank", 4)

            def correction(h):
                act.wait_ge(block_used, p.next("done", KT))
                act.wait_ge(bank_drained, p.value("bank"))
                k = bank(p)
                answer(nc.scalar.activation(wide[h][:, 0:BLK], psum[:, k + 2:k + 4, :], ACT.Copy,
                                            scale=quant[:, 2:3]))
                p.next("bank", 4)

            asked()
            scale_block(CTX_LEAD)
            with p.loop(B - 1, block=2 * KT, bank=16, done=2 * KT, act_done=6, step=4):
                q1_copy()
                for h in range(2):
                    scale_block(KT)
                    correction(h)
            q1_copy()
            scale_block(KT)
            correction(0)
            scale_block(KT - CTX_LEAD)
            split(LEAD)
            correction(1)

            early_ln_hi()
            split(3 * KT // 2)
            skip(12)
            asked()
            k = bank(p)
            skip(4, 4)
            for b in range(B):
                answer(nc.scalar.activation(wide[0][:, b * P:(b + 1) * P], psum[:, k + b, 0:P], ACT.Exp,
                                            bias=nmax[:, b:b + 1], scale=HD ** -0.5, accum_out=esum[:, b:b + 1]))
            skip(4, 4)
            for j in range(4):
                act.wait_ge(step_done, p.next("step"))
                answer(nc.scalar.activation(th_hi[0][:, j, :], psum[:, bank(p), :], ACT.Copy))
                p.next("bank")
            split(2 * NC)
            skip(16)

            def lora_hi(rows_):
                skip(4, 4)
                act.wait_ge(bank_drained, p.value("bank"))
                answer(nc.scalar.activation(th_hi[0][0:rows_, 0, :], wide[2][0:rows_, 3 * W:4 * W], ACT.Copy))
                split(NC - 1)
                split(KT // 2 + 1)
                skip(16)

            early_ln_hi()
            split(KT // 2)
            split(KT // 4)
            skip(4 + 4 + 4, 4)
            asked()
            answer(nc.scalar.activation(pr, pr, ACT.Exp))
            split(KT // 2)
            split(KT // 2)
            skip(8)
            lora_hi(E0 * R0)

            def query_hi():
                transposed_hi(lambda j: xt_hi[:, 4 * j:4 * j + 4, 0:P])

            def exp_scores():
                asked()
                k = bank(p)
                answer(nc.scalar.activation(wide[0][:, :], psum[:, k:k + 4, :], ACT.Exp,
                                            bias=nmax[:, 0:1], accum_out=esum[:, 0:1]))
                p.next("bank", 4)

            def probs_hi():
                transposed_hi(lambda j: xt_hi[:, 4 * j:4 * j + 4, P:2 * P])

            query_hi()
            split(2 * KT)
            exp_scores()
            query_hi()
            probs_hi()
            with p.loop(B - 2, block=4 * KT, bank=16, step=8, act_done=9, ask_act=1):
                split(2 * KT)
                exp_scores()
                split(2 * KT)
                p.next("bank", 4)
                query_hi()
                probs_hi()
            split(2 * KT)
            exp_scores()
            split(2 * KT)
            skip(4)
            probs_hi()
            split(2 * KT)
            skip(4)

            asked()
            answer(nc.scalar.activation(taylor[:, 0:G + 1], ediff, ACT.Exp))
            ln_hi()
            split(KT)
            skip(8)

            def term_hi(i):
                asked()
                answer(nc.scalar.activation(th_hi[i][:, :, :], wide[0][:, :].rearrange("p (k t) -> p k t", k=4),
                                            ACT.Copy))

            term_hi(0)
            with p.loop(G // 2, block=4 * NC, bank=32, act_done=2, ask_act=2):
                for i in range(2):
                    term_hi(1 - i)
                    split(2 * NC)
                    p.next("bank", 16)
            split(2 * NC)
            skip(16)

            def gated(i, tiles):
                act.wait_ge(block_used, p.value("done"))
                k = bank(p)
                answer(nc.scalar.activation(wide[0][:, 0:tiles * W], psum[:, k:k + tiles, :], ACT.Sigmoid))
                p.next("bank", 2 * tiles)
                act.wait_ge(bank_drained, p.value("bank"))
                answer(nc.scalar.activation(th_hi[i][:, 0:tiles, :],
                                            wide[1][:, 0:tiles * W].rearrange("p (k t) -> p k t", t=TOK), ACT.Copy))

            def down():
                split(NC)
                p.next("done", NC)
                p.next("bank", 4 * NC)

            p.n["done"] = p.n["block"] - LEAD
            split(KT // 2)
            p.next("done", KT // 2)
            gated(0, 2)
            with p.loop(UNITS // 2, block=2 * (KT // 2 + NC), done=2 * (KT // 2 + NC), bank=40, act_done=4):
                for i in range(2):
                    split(KT // 2)
                    p.next("done", KT // 2)
                    gated(1 - i, 2)
                    down()
            split(KT // 4)
            p.next("done", KT // 4)
            gated(1, 1)
            down()
            down()

            early_ln_hi()
            split(KT // 2)
            split(KT // 8)
            skip(4 + 4 + 4, 4)
            split(KT // 2)
            skip(4 + 4, 4)
            asked()
            answer(nc.scalar.activation(pr, pr, ACT.Exp))
            asked()
            answer(nc.scalar.activation(t8, t8, ACT.Sigmoid, scale=2.0))
            split(KT // 2)
            skip(4)
            lora_hi(R1)

        @block.vector
        def _(dve):
            p = Place(dve)
            v = nc.vector

            def link(ins):
                ins.then_inc(dve_step, 1)
                dve.wait_ge(dve_step, p.next("link"))

            def own_drains():
                dve.wait_ge(bank_drained, p.value("bank"))

            def split(k):
                for _ in range(k):
                    if p.n["block"] >= N_BLOCKS:
                        return
                    s = p.n["block"] % SLOTS
                    dve.wait_ge(hi_ready, p.next("block"))
                    v.tensor_tensor(lo[:, s, :], raw[:, s, :], hi[:, s, :].bitcast(F32), ALU.subtract)\
                     .then_inc(lo_ready, 1)

            def round_block(k):
                for _ in range(k):
                    s = p.n["block"] % SLOTS
                    dve.wait_ge(hi_ready, p.next("block"))
                    c = (p.n["block"] - 1) % CTX_SLOTS
                    link(v.tensor_scalar(ctx_raw[:, c, :], ctx_raw[:, c, :], MAGIC, MAGIC, ALU.add, ALU.max))
                    if p.n["block"] > SLOTS:
                        dve.wait_ge(block_used, p.value("block", SLOTS))
                    v.tensor_scalar(q2[:, s, :], ctx_raw[:, c, :], MAGIC + QMAX, MAGIC + QMID, ALU.min, ALU.subtract)\
                     .then_inc(lo_ready, 1)

            def x_stats(b, c):
                return v.bn_stats(stats[:, (b * NC + c) * 6:(b * NC + c) * 6 + 6],
                                  x[:, b * D + c * W:b * D + (c + 1) * W])

            def chunk_stats(c):
                own_drains()
                for b in range(B):
                    last = x_stats(b, c)
                link(last)

            def rstd_of(a=0, n=B):
                st = stats[:, :].rearrange("p (b k) -> p b k", b=B)
                va, rs, nt = var[:, a:n], rstd[:, a:n], nt1[:, a:n]
                for b in range(a, n):
                    last = v.bn_aggr(mv[:, 2 * b:2 * b + 2], st[:, b, :])
                link(last)
                link(v.tensor_scalar(va, mv.rearrange("p (b k) -> p b k", k=2)[:, a:n, 1], LN_EPS, None, ALU.add))
                link(v.tensor_scalar(rs.bitcast(I32), va.bitcast(I32), 1, None, ALU.logical_shift_right))
                link(v.tensor_scalar(rs.bitcast(I32), rs.bitcast(I32), -1.0, float(0x5F3759DF), ALU.mult, ALU.add))
                for _ in range(4):
                    link(v.scalar_tensor_tensor(nt, rs, -0.5, rs, ALU.mult, ALU.mult))
                    link(v.tensor_tensor(nt, nt, va, ALU.mult))
                    link(v.scalar_tensor_tensor(rs, nt, 1.5, rs, ALU.add, ALU.mult))

            def normalise(b, dst):
                return v.tensor_scalar(dst, x[:, b * D:(b + 1) * D], mv[:, 2 * b:2 * b + 1], rstd[:, b:b + 1],
                                       ALU.subtract, ALU.mult)

            def transposed_lo(hi_, lo_, unused=0):
                for j in range(4):
                    dve.wait_ge(act_done, p.next("act_done"))
                    v.tensor_tensor(lo_(j), psum[:, bank(p), :].rearrange("p (k t) -> p k t", t=P),
                                    hi_(j).bitcast(F32), ALU.subtract)\
                     .then_inc(bank_drained, 1 + (unused if j == 3 else 0))
                    p.next("bank")
                    p.next("step")
                p.next("bank", unused)

            def ln_lo(b, unused):
                transposed_lo(lambda j: xt_hi[:, 4 * j:4 * j + 4, b * P:(b + 1) * P],
                              lambda j: xt_lo[:, 4 * j:4 * j + 4, b * P:(b + 1) * P], unused)

            def layer_norm(early=False):
                rstd_of()
                for b in range(2):
                    normalise(b, wide[b][:, :]).then_inc(ask_pe, 1)
                for b in range(B):
                    ln_lo(b, 4 if early and b < B - 1 else 0)
                    if b + 2 < B:
                        normalise(b + 2, wide[b][:, :]).then_inc(ask_pe, 1)

            def want_bias():
                own_drains()
                v.memset(nt1, 0.0).then_inc(bias_room, 1)

            def add_bias():
                dve.wait_ge(bias_loaded, 16 * p.next("bias"))
                for b in range(B):
                    last = v.tensor_tensor(x[:, b * D:(b + 1) * D], x[:, b * D:(b + 1) * D], wide[1][:, :], ALU.add)
                link(last)

            def epilogue(col, blocks):
                if blocks:
                    dve.wait_ge(block_used, p.next("done", blocks))
                own_drains()
                for b in range(B):
                    if isinstance(col, int):
                        xs = x[:, b * D + col * W:b * D + (col + 1) * W]
                    else:
                        xs = x[:, ds(col * W + b * D, W)]
                    v.tensor_tensor(xs, psum[:, bank(p), :], xs, ALU.add).then_inc(bank_drained, 1)
                    p.next("bank")

            def ask(ins):
                ins.then_inc(ask_act, 1)
                p.next("ask_act")

            def answered():
                dve.wait_ge(act_done, p.next("act_done"))

            def by_expert(t, n=E0):
                return t.rearrange("p (b e) -> p b e", b=B)

            def over(t, n=E0):
                return t.unsqueeze(2).to_broadcast([P, B, n])

            def top2():
                rk = rank[:, :, :]
                for m, oh, among in ((m1, oh1, pr), (m2, oh2, cand)):
                    link(v.tensor_reduce(m, by_expert(among), AX, ALU.max))
                    link(v.tensor_tensor(by_expert(t8), by_expert(among), over(m), ALU.is_equal))
                    link(v.tensor_tensor(by_expert(t8), by_expert(t8), rk, ALU.mult))
                    link(v.tensor_reduce(msum, by_expert(t8), AX, ALU.max))
                    link(v.tensor_tensor(by_expert(oh), rk, over(msum), ALU.is_equal))
                    if m is m1:
                        link(v.scalar_tensor_tensor(cand, oh, -2.0, pr, ALU.mult, ALU.add))

            def softmax8(lgv):
                link(v.tensor_reduce(m1, lgv, AX, ALU.max))
                ask(v.tensor_tensor(by_expert(pr), lgv, over(m1), ALU.subtract))
                answered()
                link(v.tensor_reduce(m1, by_expert(pr), AX, ALU.add))
                link(v.reciprocal(m1, m1))
                link(v.tensor_tensor(by_expert(pr), by_expert(pr), over(m1), ALU.mult))

            def quantise(b):
                t = wide[2][:, :]
                if isinstance(b, int):
                    link(normalise(b, t))
                else:
                    link(v.tensor_copy(order_now[:, 0:1], mv[:, ds(b * 2, 1)]))
                    link(v.tensor_copy(order_now[:, 1:2], rstd[:, ds(b, 1)]))
                    link(v.tensor_scalar(t, x[:, ds(b * D, D)], order_now[:, 0:1], order_now[:, 1:2],
                                         ALU.subtract, ALU.mult))
                link(v.tensor_scalar(t, t, quant[:, 0:1], cst[:, C_Z1:C_Z1 + 1], ALU.mult, ALU.add))
                link(v.tensor_scalar(t, t, MAGIC, MAGIC, ALU.add, ALU.max))
                link(v.tensor_scalar(t, t, MAGIC + QMAX, MAGIC + QMID, ALU.min, ALU.subtract))
                link(v.tensor_reduce(row_next, t, AX, ALU.add))
                v.tensor_scalar(row_next, row_next, quant[:, 3:4], quant[:, 4:5], ALU.mult, ALU.add).then_inc(ask_pe, 1)

            dve.wait_ge(tables_made, 3)
            dve.wait_ge(consts_loaded, 16)
            link(v.reciprocal(quant[:, 0:1], cst[:, C_S1:C_S1 + 1]))
            link(v.tensor_scalar(quant[:, 2:3], cst[:, C_Z1:C_Z1 + 1], -1.0, QMID, ALU.mult, ALU.add))
            link(v.tensor_scalar(quant[:, 3:4], cst[:, C_Z2:C_Z2 + 1], -1.0, QMID, ALU.mult, ALU.add))
            link(v.tensor_scalar(quant[:, 4:5], quant[:, 2:3], quant[:, 3:4], float(D), ALU.mult, ALU.mult))
            link(v.tensor_scalar(quant[:, 5:6], cst[:, C_S1:C_S1 + 1], cst[:, C_S2:C_S2 + 1], None, ALU.mult))
            ask(v.reciprocal(quant[:, 1:2], cst[:, C_S2:C_S2 + 1]))
            for b in range(B):
                dve.wait_ge(x_loaded[b], 16)
                for c in range(NC):
                    last = x_stats(b, c)
                if b == 0:
                    link(last)
                    rstd_of(0, 1)
                    quantise(0)
                    round_block(LEAD)
            link(last)
            rstd_of(1, B)

            def q1_drained():
                dve.wait_ge(act_done, p.next("act_done", 4))
                p.next("bank", 8)
                link(v.tensor_copy(row_now, row_next))
                v.tensor_copy(nt1[:, 0:1], row_next).then_inc(bank_drained, 8)

            def dequantise(b, h):
                answered()
                own_drains()
                k = bank(p)
                t = wide[h][:, 0:BLK]
                p.next("bank", 4)
                v.scalar_tensor_tensor(t, psum[:, k:k + 2, :].rearrange("p a n -> p (a n)"), row_now, t,
                                       ALU.add, ALU.add).then_inc(bank_drained, 4)
                own_drains()
                xs = x[:, ds(b * D + h * BLK, BLK)] if not isinstance(b, int) else \
                    x[:, b * D + h * BLK:b * D + (h + 1) * BLK]
                link(v.scalar_tensor_tensor(xs, t, quant[:, 5:6], xs, ALU.mult, ALU.add))

            with p.loop(B - 1, block=2 * KT, bank=16, act_done=6, link=2 * KT + 10) as b:
                q1_drained()
                round_block(KT)
                dequantise(b, 0)
                quantise(b + 1)
                round_block(KT)
                dequantise(b, 1)
            q1_drained()
            round_block(KT)
            dequantise(B - 1, 0)
            round_block(KT - LEAD)
            split(LEAD)
            dequantise(B - 1, 1)
            p.n["done"] = N_CTX
            p.n["step"] = 4 * B

            for c in range(NC):
                chunk_stats(c)
            layer_norm(early=True)
            split(KT // 2)
            dve.wait_ge(block_used, p.next("done", KT // 2))
            for b in range(B):
                v.tensor_tensor(wide[2][:, b * HD:(b + 1) * HD], psum[:, bank(p), :], cst[:, C_BV:C_BV + HD],
                                ALU.add).then_inc(bank_drained, 1)
                p.next("bank")
            for j, dst in ((0, wide[0]), (1, wide[1])):
                split(KT // 2)
                dve.wait_ge(block_used, p.next("done", KT // 2))
                for t in range(4):
                    v.tensor_scalar(dst[:, t * TOK:(t + 1) * TOK], psum[:, bank(p), :],
                                    cst[:, C_BQK + 4 * j + t:C_BQK + 4 * j + t + 1], None, ALU.add)\
                     .then_inc(bank_drained, 1)
                    p.next("bank")
            dve.wait_ge(step_done, p.next("step", 4))
            k = bank(p)
            link(v.tensor_reduce(nmax, psum[:, k:k + 4, 0:P], AX, ALU.max))
            ask(v.tensor_scalar(nmax, nmax, -HD ** -0.5, None, ALU.mult))
            dve.wait_ge(act_done, p.next("act_done", 4))
            p.next("bank", 4)
            v.reciprocal(rsum, esum).then_inc(bank_drained, 4)
            own_drains()
            for b in range(B):
                last = v.tensor_scalar(wide[0][:, b * P:(b + 1) * P], wide[0][:, b * P:(b + 1) * P], rsum[:, b:b + 1],
                                       None, ALU.mult)
            last.then_inc(ask_pe, 1)
            want_bias()
            for b in range(B):
                dve.wait_ge(step_done, p.next("step"))
                v.tensor_copy(wide[0][:, TOK + b * P:TOK + (b + 1) * P], psum[:, bank(p), 0:P])\
                 .then_inc(bank_drained, 1)
                p.next("bank")
            for j in range(4):
                answered()
                v.tensor_tensor(th_lo[0][:, j, :], psum[:, bank(p), :], th_hi[0][:, j, :].bitcast(F32),
                                ALU.subtract).then_inc(bank_drained, 1)
                p.next("bank")
                p.next("step")
            add_bias()
            for c in range(NC):
                split(2)
                epilogue(c, 2)
                chunk_stats(c)

            def small_drained(blocks, tiles):
                split(blocks)
                dve.wait_ge(block_used, p.next("done", blocks))
                k = bank(p)
                p.next("bank", 4)
                for j in range(tiles):
                    last = v.tensor_copy(wide[2][:, j * TOK:(j + 1) * TOK], psum[:, k + j, :])
                last.then_inc(bank_drained, 4)

            def token_rows(dst, n):
                dve.wait_ge(step_done, p.next("step", 4))
                k = bank(p)
                p.next("bank", 4)
                v.tensor_copy(dst, psum[:, k, 0:n]).then_inc(bank_drained, 4)
                own_drains()

            def lora(rows_, factor, stat):
                for b in range(B):
                    dve.wait_ge(step_done, p.next("step"))
                    dst = wide[2][0:rows_, 3 * W + b * P:3 * W + (b + 1) * P]
                    if factor is None:
                        ins = v.tensor_copy(dst, psum[0:rows_, bank(p), 0:P])
                    else:
                        ins = v.tensor_tensor(dst, psum[0:rows_, bank(p), 0:P], factor[:, b * P:(b + 1) * P], ALU.mult)
                    ins.then_inc(bank_drained, 1)
                    p.next("bank")
                answered()
                v.tensor_tensor(th_lo[0][0:rows_, 0, :], wide[2][0:rows_, 3 * W:4 * W],
                                th_hi[0][0:rows_, 0, :].bitcast(F32), ALU.subtract).then_inc(ask_pe, 1)
                for c in range(NC - 1):
                    split(1)
                    epilogue(c, 1)
                    if stat:
                        chunk_stats(c)
                split(KT // 2 + 1)
                epilogue(NC - 1, KT // 2 + 1)
                if stat:
                    chunk_stats(NC - 1)

            layer_norm(early=True)
            want_bias()
            split(KT // 2)
            epilogue(0, KT // 2)
            small_drained(KT // 4, 2)
            token_rows(lg[:, 0:B * E0], B * E0)
            softmax8(by_expert(lg[:, 0:B * E0]))
            top2()
            link(v.tensor_tensor(msum, m1, m2, ALU.add))
            link(v.reciprocal(msum, msum))
            for m, oh in ((m1, oh1), (m2, oh2)):
                link(v.scalar_tensor_tensor(m, m, 2.0, msum, ALU.mult, ALU.mult))
                link(v.tensor_tensor(by_expert(oh), by_expert(oh), over(m), ALU.mult))
            link(v.tensor_tensor(oh1, oh1, oh2, ALU.add))
            spread = wide[2][:, 2 * W:3 * W]
            v.tensor_copy(spread.rearrange("p (k r) -> p k r", r=R0),
                          oh1.unsqueeze(2).to_broadcast([P, B * E0, R0])).then_inc(ask_pe, 1)
            add_bias()
            for c in range(1, 3):
                split(KT // 2)
                epilogue(c, KT // 2)
            lora(E0 * R0, wide[2][:, 0:TOK], True)

            def query(b):
                if isinstance(b, int):
                    normalise(b, wide[1][:, :]).then_inc(ask_pe, 1)
                else:
                    link(v.tensor_copy(order_now[:, 0:1], mv[:, ds(b * 2, 1)]))
                    link(v.tensor_copy(order_now[:, 1:2], rstd[:, ds(b, 1)]))
                    v.tensor_scalar(wide[1][:, :], x[:, ds(b * D, D)], order_now[:, 0:1], order_now[:, 1:2],
                                    ALU.subtract, ALU.mult).then_inc(ask_pe, 1)

            def query_lo():
                transposed_lo(lambda j: xt_hi[:, 4 * j:4 * j + 4, 0:P], lambda j: xt_lo[:, 4 * j:4 * j + 4, 0:P])

            def probs_lo():
                transposed_lo(lambda j: xt_hi[:, 4 * j:4 * j + 4, P:2 * P],
                              lambda j: xt_lo[:, 4 * j:4 * j + 4, P:2 * P])

            def softmax():
                split(2 * KT)
                dve.wait_ge(block_used, p.next("done", 2 * KT))
                k = bank(p)
                link(v.tensor_reduce(m1[:, 0:1], psum[:, k:k + 4, :].rearrange("p a n -> p (a n)"), AX, ALU.max))
                ask(v.tensor_scalar(nmax[:, 0:1], m1[:, 0:1], -1.0, None, ALU.mult))
                answered()
                p.next("bank", 4)
                v.reciprocal(rsum[:, 1:2], esum[:, 0:1]).then_inc(bank_drained, 4)

            def attended(b):
                dve.wait_ge(block_used, p.next("done", 2 * KT))
                own_drains()
                for c in range(NC):
                    xs = x[:, b * D + c * W:b * D + (c + 1) * W] if isinstance(b, int) else x[:, ds(b * D + c * W, W)]
                    v.scalar_tensor_tensor(xs, psum[:, bank(p), :], rsum[:, 0:1], xs, ALU.mult, ALU.add)\
                     .then_inc(bank_drained, 1)
                    p.next("bank")
                own_drains()
                link(v.tensor_copy(rsum[:, 0:1], rsum[:, 1:2]))

            def batch_stats(b):
                own_drains()
                for c in range(NC):
                    last = x_stats(b, c) if isinstance(b, int) else \
                        v.bn_stats(stats[:, ds(b * NC * 6 + c * 6, 6)], x[:, ds(b * D + c * W, W)])
                link(last)

            rstd_of()
            query(0)
            query_lo()
            query(1)
            softmax()
            own_drains()
            link(v.tensor_copy(rsum[:, 0:1], rsum[:, 1:2]))
            query_lo()
            probs_lo()
            with p.loop(B - 2, block=4 * KT, done=4 * KT, bank=16, step=8, act_done=9, ask_act=1, link=5) as b:
                softmax()
                query(b + 2)
                split(2 * KT)
                attended(b)
                query_lo()
                probs_lo()
                batch_stats(b)
            softmax()
            split(2 * KT)
            attended(B - 2)
            probs_lo()
            batch_stats(B - 2)
            split(2 * KT)
            attended(B - 1)
            own_drains()
            batch_stats(B - 1)

            link(v.memset(ediff, 0.0))
            link(v.tensor_scalar(ediff[:, 1:2], cst[:, C_DF:C_DF + 1], -1.0, None, ALU.mult))
            ask(v.tensor_tensor(ediff[:, 2:G + 1], cst[:, C_DF:C_DF + G - 1], cst[:, C_DF + 1:C_DF + G], ALU.subtract))
            link(v.memset(taylor[:, G + 1:G + 1 + GRAD_ORDER_MIN + 1], 1.0))
            link(v.memset(taylor[:, G + 2 + GRAD_ORDER_MIN:2 * (G + 1)], 0.0))
            answered()
            layer_norm()
            t_now, delta, keep = wide[0], wide[1], wide[2]
            split(KT // 2)
            dve.wait_ge(block_used, p.next("done", KT // 2))
            own_drains()
            for j in range(4):
                v.tensor_copy(t_now[:, j * TOK:(j + 1) * TOK], psum[:, bank(p), :]).then_inc(bank_drained, 1)
                p.next("bank")
            split(KT // 2)
            dve.wait_ge(block_used, p.next("done", KT // 2))
            for j in range(4):
                v.tensor_scalar(delta[:, j * TOK:(j + 1) * TOK], psum[:, bank(p), :],
                                cst[:, C_LP + j:C_LP + j + 1], None, ALU.subtract).then_inc(bank_drained, 1)
                p.next("bank")
            own_drains()
            link(v.tensor_scalar(keep[:, :], delta[:, :], -1.0, None, ALU.mult))
            link(v.tensor_tensor(keep[:, :], keep[:, :], delta[:, :], ALU.max))
            link(v.tensor_scalar(keep[:, :], keep[:, :], THD, None, ALU.is_le))

            def term_lo(i):
                answered()
                v.tensor_tensor(th_lo[i][:, :, :], t_now[:, :].rearrange("p (k t) -> p k t", k=4),
                                th_hi[i][:, :, :].bitcast(F32), ALU.subtract).then_inc(ask_pe, 1)

            def next_term(m):
                link(v.tensor_copy(order_now[:, 0:1], taylor[:, ds(m, 1)]))
                link(v.tensor_copy(order_now[:, 1:2], taylor[:, ds(m + (G + 1), 1)]))
                link(v.scalar_tensor_tensor(t_now[:, :], t_now[:, :], order_now[:, 0:1], delta[:, :],
                                            ALU.mult, ALU.mult))
                ask(v.scalar_tensor_tensor(t_now[:, :], keep[:, :], order_now[:, 1:2], t_now[:, :],
                                           ALU.max, ALU.mult))

            ask(v.tensor_copy(order_now[:, 0:1], taylor[:, 0:1]))
            term_lo(0)
            with p.loop(G // 2, block=4 * NC, done=4 * NC, bank=32, act_done=2, ask_act=2, link=6) as t:
                for i in range(2):
                    next_term(t * 2 + (i + 1))
                    term_lo(1 - i)
                    for c in range(NC):
                        split(2)
                        epilogue(c, 2)
            for c in range(NC):
                split(2)
                epilogue(c, 2)

            def gated(i, tiles, blocks):
                k = bank(p)
                n = tiles * W
                p.next("done", blocks)
                answered()
                link(v.tensor_tensor(wide[0][:, 0:n], wide[0][:, 0:n],
                                     psum[:, k:k + tiles, :].rearrange("p a n -> p (a n)"), ALU.mult))
                v.tensor_tensor(wide[1][:, 0:n], wide[0][:, 0:n],
                                psum[:, k + tiles:k + 2 * tiles, :].rearrange("p a n -> p (a n)"),
                                ALU.mult).then_inc(bank_drained, 2 * tiles)
                p.next("bank", 2 * tiles)
                answered()
                v.tensor_tensor(th_lo[i][:, 0:tiles, :], wide[1][:, 0:n].rearrange("p (k t) -> p k t", t=TOK),
                                th_hi[i][:, 0:tiles, :].bitcast(F32), ALU.subtract).then_inc(ask_pe, 1)

            def down(stat=False):
                for c in range(NC):
                    split(1)
                    epilogue(c, 1)
                    if stat:
                        chunk_stats(c)

            split(KT // 2)
            gated(0, 2, KT // 2)
            with p.loop(UNITS // 2, block=2 * (KT // 2 + NC), done=2 * (KT // 2 + NC), bank=40, act_done=4,
                        link=2):
                for i in range(2):
                    split(KT // 2)
                    gated(1 - i, 2, KT // 2)
                    down()
            split(KT // 4)
            gated(1, 1, KT // 4)
            down()
            down(stat=True)

            layer_norm(early=True)
            want_bias()
            split(KT // 2)
            epilogue(0, KT // 2)
            small_drained(KT // 8, 1)
            token_rows(wide[2][:, 1728:1728 + B * SM1], B * SM1)
            zc = wide[2][:, 1728:1728 + B * SM1].rearrange("p (b n) -> p b n", b=B)
            z = zc[:, :, E1:SM1]
            hdv = hd.rearrange("p (b k e) -> p b k e", b=B, k=2)
            limes = cst[:, C_LIM:C_LIM + E1 * R1].rearrange("p (e r) -> p e r", e=E1)
            prod = wide[2][:, 512:512 + B * E1 * R1]
            link(v.tensor_tensor(hdv[:, :, 0, :], zc[:, :, 0:E1],
                                 cst[:, C_B8:C_B8 + E1].unsqueeze(1).to_broadcast([P, B, E1]), ALU.add))
            for b in range(B):
                last = v.tensor_tensor(prod[:, b * E1 * R1:(b + 1) * E1 * R1].rearrange("p (e r) -> p e r", e=E1),
                                       z[:, b, :].unsqueeze(1).to_broadcast([P, E1, R1]), limes, ALU.mult)
            link(last)
            v.tensor_reduce(hdv[:, :, 1, :], prod.rearrange("p (b e r) -> p b e r", b=B, e=E1), AX, ALU.add)\
             .then_inc(ask_pe, 1)
            add_bias()
            split(KT // 2)
            epilogue(1, KT // 2)
            token_rows(lg, B * 2 * E1)
            lgv = lg.rearrange("p (b k e) -> p b k e", b=B, k=2)
            for i in range(2):
                link(v.tensor_scalar(by_expert(t8), lgv[:, :, i, :], -1.0, None, ALU.mult))
                link(v.tensor_tensor(by_expert(t8), by_expert(t8), lgv[:, :, i, :], ALU.max))
                last = v.tensor_reduce(gm[:, i:i + 1], t8, AX, ALU.max)
                if i == 0:
                    link(last)
            last.then_inc(ask_pool, 1)
            dve.wait_ge(pool_done, 1)
            link(v.tensor_scalar(gmall, gmall, 1e-6, None, ALU.max))
            link(v.reciprocal(gmall, gmall))
            link(v.tensor_scalar(gmall, gmall, 0.5, None, ALU.mult))
            link(v.tensor_scalar(lgv[:, :, 0, :], lgv[:, :, 0, :], gmall[:, 0:1], None, ALU.mult))
            link(v.scalar_tensor_tensor(by_expert(t8), lgv[:, :, 1, :], gmall[:, 1:2], lgv[:, :, 0, :],
                                        ALU.mult, ALU.add))
            softmax8(by_expert(t8))
            top2()
            ask(v.tensor_tensor(by_expert(t8), by_expert(pr), over(m2), ALU.subtract))
            answered()
            link(v.tensor_tensor(pr, pr, t8, ALU.mult))
            link(v.tensor_reduce(msum, by_expert(pr), AX, ALU.add))
            link(v.tensor_scalar(msum, msum, 1e-9, None, ALU.add))
            link(v.reciprocal(msum, msum))
            link(v.scalar_tensor_tensor(by_expert(pr), by_expert(pr), 0.5, over(msum), ALU.mult, ALU.mult))
            for b in range(B):
                last = v.tensor_tensor(
                    prod[:, b * E1 * R1:(b + 1) * E1 * R1].rearrange("p (r e) -> p r e", e=E1),
                    pr[:, b * E1:(b + 1) * E1].unsqueeze(1).to_broadcast([P, R1, E1]),
                    cst[:, C_LIM:C_LIM + E1 * R1].rearrange("p (e r) -> p r e", e=E1), ALU.mult)
            link(last)
            mix = wide[2][:, 1536:1536 + B * R1].rearrange("p (b r) -> p b r", b=B)
            link(v.tensor_reduce(mix, prod.rearrange("p (b r e) -> p b r e", b=B, e=E1), AX, ALU.add))
            v.tensor_tensor(wide[2][:, 0:B * R1].rearrange("p (b r) -> p b r", b=B), mix, z, ALU.mult)\
             .then_inc(ask_pe, 1)
            split(KT // 2)
            epilogue(2, KT // 2)
            lora(R1, None, False)

        @block.tensor
        def _(pe):
            p = Place(pe)
            mm = nc.tensor.matmul

            def free_bank():
                k = bank(p)
                if p.n["bank"] >= BANKS:
                    pe.wait_ge(bank_drained, p.value("bank", BANKS - 1))
                p.next("bank")
                return k

            def all_drained():
                pe.wait_ge(bank_drained, p.value("bank"))

            def asked(k=1):
                pe.wait_ge(ask_pe, p.next("ask_pe", k))

            def three(dst, st, mv_, first, last):
                (sh, sl), (mh, ml) = st, mv_
                mm(dst, sh, mh, start=first, stop=False)
                mm(dst, sh, ml, start=False, stop=False)
                return mm(dst, sl, mh, start=False, stop=last)

            def transposes(src, rows_=P):
                for j in range(4):
                    k = free_bank()
                    for i, tile in enumerate(src(j)):
                        last = nc.tensor.transpose(psum[0:rows_, k, i * P:(i + 1) * P], tile, ident[:, :])
                    last.then_inc(step_done, 1)

            def tiles4(t):
                return lambda j: [t[:, (4 * j + i) * P:(4 * j + i + 1) * P] for i in range(4)]

            def ln_transposes():
                for b in range(B):
                    asked()
                    transposes(tiles4(wide[b % 2]))
                all_drained()

            def blocks(n, products):
                banks = None
                for i in range(n):
                    s = p.n["block"] % SLOTS
                    pe.wait_ge(lo_ready, p.next("block"))
                    todo = products(i, s)
                    if banks is None:
                        banks = {}
                    for j, st, mv_, width, first, last in todo:
                        if j not in banks:
                            banks[j] = free_bank()
                        ins = three(psum[:, banks[j], 0:width], st, mv_, first, last)
                    ins.then_inc(block_used, 1)

            def part(s, a, n, rows_=P):
                return (hi[0:rows_, s, a:a + n], lo[0:rows_, s, a:a + n])

            def tokens(t, k, b, rows_=P):
                return (t[0][0:rows_, k, b * P:(b + 1) * P], t[1][0:rows_, k, b * P:(b + 1) * P])

            xt = (xt_hi, xt_lo)
            th = list(zip(th_hi, th_lo))

            def token_major(t, n_kt, per_block, width, rows_=P):
                def products(i, s):
                    return [(b, tokens(t, k, b, rows_), part(s, (k - i * per_block) * width, width, rows_), width,
                             k == 0, k == n_kt - 1)
                            for k in range(i * per_block, min(n_kt, (i + 1) * per_block)) for b in range(B)]
                blocks(-(-n_kt // per_block), products)

            def feature_major(tiles=4):
                per_block = BLK // (tiles * P)

                def products(i, s):
                    return [(j, part(s, ((k - i * per_block) * tiles + j) * P, P), (xt_hi[:, k, :], xt_lo[:, k, :]),
                             TOK, k == 0, k == KT - 1)
                            for k in range(i * per_block, (i + 1) * per_block) for j in range(tiles)]
                blocks(KT // per_block, products)

            def ln_and_first_product():
                base = p.n["bank"]
                early, per_block = min(LEAD, KT // 2), 2

                def token_tile(b):
                    asked()
                    assert p.n["bank"] == base + 8 * b
                    transposes(tiles4(wide[b % 2]))
                    p.next("bank", 4 if b < B - 1 else 0)

                def product(b, i):
                    for k in range(i * per_block, (i + 1) * per_block):
                        ins = three(psum[:, (base + 4 + b) % BANKS, :], tokens(xt, k, b),
                                    part((n0 + i) % SLOTS, (k - i * per_block) * W, W), k == 0, k == KT - 1)
                    return ins

                n0 = p.n["block"]
                token_tile(0)
                token_tile(1)
                pe.wait_ge(bank_drained, base)
                pe.wait_ge(lo_ready, p.value("block") + early)
                for b in range(B):
                    pe.wait_ge(bank_drained, base + 8 * b + 4)
                    for i in range(early):
                        ins = product(b, i)
                        if b == B - 1:
                            ins.then_inc(block_used, 1)
                    if b + 2 < B:
                        token_tile(b + 2)
                p.next("block", early)
                for i in range(early, KT // per_block):
                    pe.wait_ge(lo_ready, p.next("block"))
                    for b in range(B):
                        ins = product(b, i)
                    ins.then_inc(block_used, 1)
                p.next("bank", 4)

            pe.wait_ge(tables_made, 3)
            with p.loop(B, block=2 * KT, bank=16, ask_pe=1):
                asked()
                transposes(tiles4(wide[2]))
                p.next("bank", 4)
                all_drained()
                for h in range(2):
                    ks = [free_bank() for _ in range(4)]
                    for i in range(KT):
                        s = p.n["block"] % SLOTS
                        pe.wait_ge(lo_ready, p.next("block"))
                        for j in range(2):
                            mm(psum[:, ks[j], :], q1t[:, i * P:(i + 1) * P], q2[:, s, j * W:(j + 1) * W],
                               start=i == 0, stop=i == KT - 1)
                        for j in range(2):
                            ins = mm(psum[:, ks[2 + j], :], ones[:, :], q2[:, s, j * W:(j + 1) * W],
                                     start=i == 0, stop=i == KT - 1)
                        ins.then_inc(block_used, 1)

            ln_and_first_product()
            feature_major()
            feature_major()
            all_drained()
            for b in range(B):
                k = free_bank()
                for j in range(4):
                    last = mm(psum[:, k, 0:P], wide[0][:, j * TOK + b * P:j * TOK + (b + 1) * P],
                              wide[1][:, j * TOK + b * P:j * TOK + (b + 1) * P], start=j == 0, stop=j == 3)
                last.then_inc(step_done, 1)
            asked()
            for b in range(B):
                nc.tensor.transpose(psum[:, free_bank(), 0:P], wide[0][:, b * P:(b + 1) * P], ident[:, :])\
                  .then_inc(step_done, 1)
            all_drained()
            for j in range(4):
                k = free_bank()
                for b in range(B):
                    last = mm(psum[:, k, b * P:(b + 1) * P], wide[2][:, b * HD + j * P:b * HD + (j + 1) * P],
                              wide[0][:, TOK + b * P:TOK + (b + 1) * P], start=True, stop=True)
                last.then_inc(step_done, 1)
            all_drained()
            for c in range(NC):
                token_major(th[0], 4, 2, W)

            def narrow(tiles, width):
                kept = p.n["bank"]
                feature_major(tiles)
                p.next("bank", kept + 4 - p.n["bank"])
                all_drained()
                k = free_bank()
                p.next("bank", 3)
                n, src = width
                for b in range(B):
                    last = nc.tensor.transpose(psum[:, k, b * n:(b + 1) * n],
                                               wide[2][0:n, src + b * P:src + (b + 1) * P], ident[0:n, 0:n])
                last.then_inc(step_done, 4)

            def lora(tile, rows_):
                asked()
                for b in range(B):
                    nc.tensor.transpose(psum[0:rows_, free_bank(), 0:P], tile(b), ident[:, :]).then_inc(step_done, 1)
                asked()
                for c in range(NC - 1):
                    token_major(th[0], 1, 1, W, rows_)

                def products(i, s):
                    if i == KT // 2:
                        return [(b, tokens(th[0], 0, b, rows_), part(s, 0, W, rows_), W, False, True) for b in range(B)]
                    return [(b, tokens(xt, k, b), part(s, (k - 2 * i) * W, W), W, k == 0, False)
                            for k in (2 * i, 2 * i + 1) for b in range(B)]
                blocks(KT // 2 + 1, products)

            ln_and_first_product()
            narrow(2, (E0, TOK))
            token_major(xt, KT, 2, W)
            token_major(xt, KT, 2, W)
            lora(lambda b: wide[2][:, 2 * W + b * P:2 * W + (b + 1) * P], E0 * R0)

            def rows_major(col):
                def products(i, s):
                    k, half = i // 2, i % 2
                    st = (xt_hi[:, k, col:col + P], xt_lo[:, k, col:col + P])
                    return [(2 * half + j, st, part(s, j * W, W), W, k == 0, k == KT - 1) for j in range(2)]
                blocks(2 * KT, products)

            def query():
                asked()
                transposes(tiles4(wide[1]))

            def probs():
                transposes(tiles4(wide[0]))

            def scores():
                rows_major(0)

            def values():
                rows_major(P)

            query()
            all_drained()
            scores()
            query()
            probs()
            all_drained()
            with p.loop(B - 2, block=4 * KT, bank=16, ask_pe=1):
                scores()
                values()
                query()
                probs()
            scores()
            values()
            probs()
            all_drained()
            values()

            ln_transposes()
            feature_major()
            feature_major()
            with p.loop(G // 2, block=4 * NC, bank=32, ask_pe=2):
                for i in range(2):
                    asked()
                    for c in range(NC):
                        token_major(th[i], 4, 2, W)
            asked()
            for c in range(NC):
                token_major(th[0], 4, 2, W)

            feature_major()
            with p.loop(UNITS // 2, block=2 * (KT // 2 + NC), bank=40, ask_pe=2):
                for i in range(2):
                    feature_major()
                    asked()
                    for c in range(NC):
                        token_major(th[i], 2, 2, W)
            feature_major(tiles=2)
            for i, kt in ((0, 2), (1, 1)):
                asked()
                for c in range(NC):
                    token_major(th[i], kt, 2, W)

            ln_and_first_product()
            narrow(1, (SM1, 0))
            token_major(xt, KT, 2, W)
            asked()
            k = free_bank()
            p.next("bank", 3)
            mm(psum[:, k, 0:B * 2 * E1], pick[:, :], hd, start=True, stop=True).then_inc(step_done, 4)
            token_major(xt, KT, 2, W)
            lora(lambda b: wide[2][:, b * R1:(b + 1) * R1], R1)
            assert p.n["bank"] == TOTAL_BANKS and p.n["block"] == N_BLOCKS, (p.n["bank"], p.n["block"], N_BLOCKS)


TOTAL_BANKS = (16 * B) + (32 + 8 + 12 + 16) + (32 + 8 + 8 + 4 + 16) + 16 * B \
    + (16 + 8 + 16 * (G + 1) + 20 * UNITS + 2 + 16) + (32 + 8 + 8 + 4 + 4 + 16)


def tiled(w, tiles_per_block=2):
    k, n = w.shape
    kt = k // P
    nb = -(-kt // tiles_per_block)
    out = np.zeros((nb, P, BLK), np.float32)
    for i in range(nb):
        part = w[i * tiles_per_block * P:(i + 1) * tiles_per_block * P]
        m = part.shape[0] // P
        out[i, :, :m * n] = part.reshape(m, P, n).transpose(1, 0, 2).reshape(P, m * n)
    return out


def chunks(w, tiles_per_block=2):
    return [tiled(w[:, c * W:(c + 1) * W], tiles_per_block) for c in range(NC)]


def halves(w):
    return w.reshape(KT, P, 2, BLK).transpose(2, 0, 1, 3)


def kernel(x, ctx_4096, L0_xattn_x1_scale, L0_xattn_x1_zp, L0_xattn_x2_scale, L0_xattn_x2_zp, L0_attn_Wqkv,
           L0_attn_bqkv, L0_attn_Wo, L0_attn_bo, L0_ffn_W_base, L0_ffn_b_base, L0_ffn_W_router, L0_ffn_A, L0_ffn_B,
           L1_attn_up_w, L1_attn_gate_w, L1_attn_local_point, L1_attn_local_approx_output, L1_attn_fuse_weight,
           L1_attn_discount_factor, L1_attn_ffn_gate_w, L1_attn_ffn_up_w, L1_attn_ffn_down_w, L1_ffn_W, L1_ffn_b,
           L1_ffn_A, L1_ffn_Bmat, L1_ffn_LiMEs):
    import concourse.bacc as bacc
    from concourse.bass_utils import run_bass_kernel_spmd

    c = np.asarray(ctx_4096)
    parts = [halves(c[b]).reshape(-1, P, BLK) for b in range(B)]
    wqkv = np.asarray(L0_attn_Wqkv)
    parts += [tiled(wqkv[:, i * HD:(i + 1) * HD]) for i in (2, 0, 1)]
    parts += chunks(np.asarray(L0_attn_Wo))
    lora_a = np.asarray(L0_ffn_A).reshape(E0 * R0, D)
    router = np.concatenate([np.asarray(L0_ffn_W_router), np.zeros((P - E0, D), np.float32)])
    base = chunks(np.asarray(L0_ffn_W_base).T)
    lora_b = chunks(np.asarray(L0_ffn_B).transpose(0, 2, 1).reshape(E0 * R0, D), 1)
    parts += [base[0], tiled(np.concatenate([lora_a, router]).T, 4), base[1], base[2]] + lora_b[:3] \
        + [base[3], lora_b[3]]

    def rows(w):
        return halves(w).transpose(1, 0, 2, 3).reshape(-1, P, BLK)

    parts += [rows(c[0].T)]
    for b in range(1, B):
        parts += [rows(c[b].T), rows(c[b - 1])]
    parts += [rows(c[B - 1])]
    parts += [tiled(np.asarray(w).T) for w in (L1_attn_up_w, L1_attn_gate_w)]
    parts += chunks(np.asarray(L1_attn_local_approx_output).T)
    fuse = np.asarray(L1_attn_fuse_weight)
    for m in range(G):
        parts += chunks(fuse[:, :, m].T)
    gate, up, down = (np.asarray(w).T for w in (L1_attn_ffn_gate_w, L1_attn_ffn_up_w, L1_attn_ffn_down_w))

    def gate_up(j, tiles=2):
        f = slice(2 * j * P, (2 * j + tiles) * P)
        return tiled(np.concatenate([gate[:, f], up[:, f]], axis=1), BLK // (2 * tiles * P))

    def down_rows(j, tiles=2):
        return chunks(down[2 * j * P:(2 * j + tiles) * P])

    parts += [gate_up(0)]
    for j in range(1, UNITS):
        parts += [gate_up(j)] + down_rows(j - 1)
    parts += [gate_up(UNITS, 1)] + down_rows(UNITS - 1) + down_rows(UNITS, 1)
    w1 = np.asarray(L1_ffn_W).T
    first = np.concatenate([w1[:, :E1], np.asarray(L1_ffn_A), np.zeros((D, P - SM1), np.float32)], axis=1)
    bmat = np.zeros((P, D), np.float32)
    bmat[:R1] = np.asarray(L1_ffn_Bmat)
    base, lora_b = chunks(w1), chunks(bmat, 1)
    parts += [base[0], tiled(first, 8), base[1], base[2]] + lora_b[:3] + [base[3], lora_b[3]]
    stream = np.concatenate(parts)
    assert stream.shape == (N_BLOCKS, P, BLK), stream.shape

    def wide_row(a):
        a = np.asarray(a).reshape(-1)
        return np.broadcast_to(a, (P, a.size))

    b1 = np.asarray(L1_ffn_b)
    bqkv = np.asarray(L0_attn_bqkv)
    consts = np.concatenate(
        [wide_row(a) for a in (L0_xattn_x1_scale, L0_xattn_x1_zp, L0_xattn_x2_scale, L0_xattn_x2_zp)]
        + [bqkv[:2 * HD].reshape(8, P).T, np.asarray(L1_attn_local_point).reshape(4, P).T]
        + [wide_row(a) for a in (L1_attn_discount_factor, b1[:E1], L1_ffn_LiMEs, bqkv[2 * HD:])], axis=1)
    assert consts.shape == (P, C_END)
    biases = np.stack([wide_row(a) for a in (L0_attn_bo, L0_ffn_b_base, b1)])

    arrays = {"x_in": np.asarray(x), "stream": stream, "biases": biases, "consts": consts}
    arrays = {k: np.ascontiguousarray(a) for k, a in arrays.items()}
    nc = bacc.Bacc("TRN2", target_bir_lowering=False, num_devices=1)
    args = [nc.dram_tensor(k, a.shape, F32, kind="ExternalInput").ap() for k, a in arrays.items()]
    out = nc.dram_tensor("x_out", (B, P, D), F32, kind="ExternalOutput").ap()
    build(nc, *args, out)
    return run_bass_kernel_spmd(nc, [arrays], core_ids=[0]).results[0]["x_out"]
```

```python
from collections import defaultdict
from contextlib import ExitStack, contextmanager

import numpy as np

import concourse.bass as bass
from concourse import mybir

F32 = mybir.dt.float32
F32R = mybir.dt.float32r
BF16 = mybir.dt.bfloat16
I32 = mybir.dt.int32
ALU = mybir.AluOpType
ACT = mybir.ActivationFunctionType
AX = mybir.AxisListType.X
RMAX = bass.bass_isa.ReduceOp.max
ds = bass.ds

P = 128
B = 4
TOK = B * P
D = 2048
KT = D // P
W = 512
NC = D // W
BLK = 1024
SLOTS = 4
LEAD = SLOTS
CTX_SLOTS = 8
Q_SLOTS = 8
CTX_LEAD = 4
Q_LEAD = 4
BANKS = 8
WIDE_SLOTS = 8

HD = D // 4
E0, R0 = 8, 16
E1, R1 = 8, 32
SM1 = E1 + R1
S = 512
G = 6
F = 4992
FT = F // P
UNITS = FT // 2
LN_EPS = 1e-5
THD = 2.5
GRAD_ORDER_MIN = 4
MAGIC = 1.5 * 2.0 ** 23
QMAX = 255.0
QMID = 128.0

N_CTX = B * 2 * KT
N_BLOCKS = (N_CTX + 3 * KT // 2 + 2 * NC + KT // 4 + NC * KT // 2 + NC + 2 * N_CTX
            + KT + (G + 1) * 2 * NC + UNITS * (KT // 2 + NC) + KT // 4 + NC + KT // 8 + NC * KT // 2 + NC)

N_WIDE = 3 * KT // 2 + 2 * NC + KT // 4 + NC * KT // 2 + NC + 2 * N_CTX
assert N_WIDE % WIDE_SLOTS == 0

C_S1, C_Z1, C_S2, C_Z2, C_BQK, C_LP, C_DF = 0, 1, 2, 3, 4, 12, 16
C_B8 = C_DF + G
C_LIM = C_B8 + E1
C_BV = C_LIM + E1 * R1
C_END = C_BV + HD


class Place:

    def __init__(self, engine):
        self.engine, self.n, self.turn, self.per_turn = engine, defaultdict(int), None, {}

    def next(self, name, k=1):
        self.n[name] += k
        return self.value(name)

    def value(self, name, back=0):
        n = self.n[name] - back
        step = self.per_turn.get(name, 0)
        return n if self.turn is None or step == 0 else self.turn * step + n

    @contextmanager
    def loop(self, turns, **per_turn):
        before = dict(self.n)
        with self.engine.Fori(0, turns) as turn:
            self.turn, self.per_turn = turn, per_turn
            yield turn
        for name in self.n:
            moved = self.n[name] - before.get(name, 0)
            assert moved == per_turn.get(name, 0), (name, moved)
        self.turn, self.per_turn = None, {}
        for name, k in per_turn.items():
            self.n[name] = before.get(name, 0) + turns * k


def build(nc, x_in, stream, biases, consts, out):
    ctx = ExitStack()
    at = [-(-nc.sbuf_base // 64) * 64]

    def place(name, shape, dtype, offset=None):
        size = int(np.prod(shape[1:])) * (2 if dtype == BF16 else 4)
        if offset is None:
            offset, at[0] = at[0], at[0] + -(-size // 64) * 64
        return nc.alloc_sbuf_tensor_at(name, shape, dtype, offset=offset)

    with ctx:
        x = place("x_res", [P, B * D], F32)
        raw = place("raw", [P, SLOTS, BLK], F32)
        hi = place("hi", [P, SLOTS, BLK], F32R)
        lo = place("lo", [P, SLOTS, BLK], F32R)
        xt_at = at[0]
        xt_hi = place("xt_hi", [P, KT, TOK], F32R)
        xt_lo = place("xt_lo", [P, KT, TOK], F32R)
        ctx_raw = place("ctx_raw", [P, CTX_SLOTS, BLK], F32, offset=xt_at)
        q2 = place("q2", [P, Q_SLOTS, BLK], BF16, offset=xt_at + 4 * CTX_SLOTS * BLK)
        q1t = place("q1t", [P, D], BF16, offset=xt_at + 4 * CTX_SLOTS * BLK + 2 * Q_SLOTS * BLK)
        th_at = at[0]
        th_hi = [place(f"th_hi{i}", [P, 4, TOK], F32R) for i in range(2)]
        th_lo = [place(f"th_lo{i}", [P, 4, TOK], F32R) for i in range(2)]
        more_raw = [place(f"more_raw{i}", [P, 2, BLK], F32, offset=th_at + (2 * i + 1) * 16 * TOK) for i in range(2)]
        wide = [place(f"wide{i}", [P, D], F32) for i in range(3)]
        cst = place("cst", [P, C_END], F32)
        ident = place("ident", [P, P], F32)
        pick = place("pick", [P, P], F32)
        ones = place("ones", [P, P], BF16)
        rank = place("rank", [P, B, E0], F32)
        stats = place("stats", [P, B * NC * 6], F32)
        sm = place("sm", [P, 448], F32)
        assert at[0] <= nc.sbuf_usable_end, (at[0], nc.sbuf_usable_end)
        psum = ctx.enter_context(nc.psum_tensor("psum", [P, BANKS, W], F32))

        used = [0]

        def cells(n):
            used[0] += n
            assert used[0] <= 448
            return sm[:, used[0] - n:used[0]]

        mv, var, rstd, nt1 = cells(2 * B), cells(B), cells(B), cells(B)
        quant, row_next, row_now = cells(6), cells(1), cells(1)
        nmax, esum, rsum = cells(B), cells(B), cells(B)
        taylor, order_now, ediff = cells(2 * (G + 1)), cells(2), cells(G + 1)
        m1, m2, msum, gm, gmall = cells(B), cells(B), cells(B), cells(2), cells(2)
        pr, cand, oh1, oh2, t8 = (cells(B * E0) for _ in range(5))
        hd = cells(B * 2 * E1)
        lg = cells(B * 2 * E1)

        def sem(name):
            return ctx.enter_context(nc.semaphore(name))

        ctx_full = [sem(f"ctx_full{i}") for i in range(CTX_SLOTS)]
        raw_full = [sem(f"raw_full{i}") for i in range(WIDE_SLOTS)]
        x0_loaded = [sem(f"x0_loaded{c}") for c in range(NC)]
        x_loaded = [sem(f"x_loaded{b}") for b in range(1, B)]
        consts_loaded = sem("consts_loaded")
        tables_made = sem("tables_made")
        hi_ready = sem("hi_ready")
        lo_ready = sem("lo_ready")
        block_used = sem("block_used")
        bank_drained = sem("bank_drained")
        step_done = sem("step_done")
        correction_ready = sem("correction_ready")
        half_done = sem("half_done")
        norms_ready = sem("norms_ready")
        tokens_ready = sem("tokens_ready")
        pool_step = sem("pool_step")
        ask_act = sem("ask_act")
        act_done = sem("act_done")
        ask_pe = sem("ask_pe")
        dve_step = sem("dve_step")
        bias_room = sem("bias_room")
        bias_loaded = sem("bias_loaded")
        ask_pool = sem("ask_pool")
        pool_done = sem("pool_done")
        stored = sem("stored")

        quantising = ((quant[:, 0:1], cst[:, C_Z1:C_Z1 + 1], ALU.mult, ALU.add),
                      (MAGIC, MAGIC, ALU.add, ALU.max),
                      (MAGIC + QMAX, MAGIC + QMID, ALU.min, ALU.subtract))

        block = ctx.enter_context(nc.Block())

        def raw_at(m):
            s = m % (WIDE_SLOTS if m < N_WIDE else SLOTS)
            return raw[:, s, :] if s < SLOTS else more_raw[(s - SLOTS) // 2][:, s % 2, :]

        def bank(p):
            return p.n["bank"] % BANKS

        def batch_of(tile, b):
            return tile[:, :, b * P:(b + 1) * P]

        @block.sync
        def _(sp):
            def load(dst, n, landed):
                sp.dma_start(dst, stream[n, :, :] if isinstance(n, int) else
                             stream[ds(n, 1), :, :].rearrange("a p n -> p (a n)")).then_inc(landed, 16)

            for c in range(NC):
                sp.dma_start(x[:, c * W:(c + 1) * W], x_in[0, :, c * W:(c + 1) * W]).then_inc(x0_loaded[c], 16)
            for s in range(CTX_SLOTS):
                load(ctx_raw[:, s, :], s, ctx_full[s])
            with sp.Fori(1, N_CTX // CTX_SLOTS) as turn:
                for s in range(CTX_SLOTS):
                    sp.wait_ge(lo_ready, turn * CTX_SLOTS + (s + 1 - CTX_SLOTS))
                    load(ctx_raw[:, s, :], turn * CTX_SLOTS + s, ctx_full[s])
            for s in range(WIDE_SLOTS):
                load(raw_at(s), N_CTX + s, raw_full[s])
            with sp.Fori(1, N_WIDE // WIDE_SLOTS) as turn:
                for s in range(WIDE_SLOTS):
                    sp.wait_ge(lo_ready, turn * WIDE_SLOTS + (N_CTX + s + 1 - WIDE_SLOTS))
                    load(raw_at(s), turn * WIDE_SLOTS + (N_CTX + s), raw_full[s])
            first = N_CTX + N_WIDE
            for s in range(SLOTS):
                sp.wait_ge(lo_ready, first + s + 1 - WIDE_SLOTS)
                load(raw[:, s, :], first + s, raw_full[s])
            turns, rest = divmod(N_BLOCKS - first, SLOTS)
            with sp.Fori(1, turns) as turn:
                for s in range(SLOTS):
                    sp.wait_ge(lo_ready, turn * SLOTS + (first + s + 1 - SLOTS))
                    load(raw[:, s, :], turn * SLOTS + (first + s), raw_full[s])
            for s in range(rest):
                n = N_BLOCKS - rest + s
                sp.wait_ge(lo_ready, n + 1 - SLOTS)
                load(raw[:, s, :], n, raw_full[s])
            o = out.rearrange("b p n -> p b n")
            xv = x[:, :].rearrange("p (b n) -> p b n", b=B)
            for c in range(NC - 1):
                sp.wait_ge(bank_drained, TOTAL_BANKS - B * (NC - 1 - c))
                sp.dma_start(o[:, :, c * W:(c + 1) * W], xv[:, :, c * W:(c + 1) * W]).then_inc(stored, 16)
            for b in range(B):
                sp.wait_ge(bank_drained, TOTAL_BANKS - (B - 1 - b))
                sp.dma_start(o[:, b, (NC - 1) * W:], xv[:, b, (NC - 1) * W:]).then_inc(stored, 16)
            sp.wait_ge(stored, 16 * (NC - 1 + B))

        @block.gpsimd
        def _(pool):
            pool.memset(ones[:, :], 1.0)
            for e in range(E0):
                pool.memset(rank[:, :, e:e + 1], float(E0 - e))
            pool.memset(ident[:, :], 0.0).then_inc(tables_made, 1)
            pool.wait_ge(tables_made, 1)
            pool.affine_select(out=ident[:, :], in_=ident[:, :], compare_op=ALU.not_equal, fill=1.0,
                               base=0, pattern=[[-1, P]], channel_multiplier=1).then_inc(tables_made, 1)
            pool.wait_ge(tables_made, 2)
            odd = ident[:, :].rearrange("p (j r) -> p j r", r=2)
            for r in range(2):
                last = pool.tensor_copy(pick[:, :].rearrange("p (j r) -> p j r", r=2)[:, :, r:r + 1],
                                        odd[:, :, 1:2])
            last.then_inc(tables_made, 1)
            t = wide[2][:, :]
            pool.wait_ge(norms_ready, 1)
            for b in range(1, B):
                pool.wait_ge(bank_drained, 16 * (b - 1) + 8)
                pool.tensor_scalar(t, x[:, b * D:(b + 1) * D], mv[:, 2 * b:2 * b + 1], rstd[:, b:b + 1],
                                   ALU.subtract, ALU.mult).then_inc(pool_step, 1)
                for i, (c1, c2, op1, op2) in enumerate(quantising):
                    pool.wait_ge(pool_step, 3 * (b - 1) + i + 1)
                    pool.tensor_scalar(t, t, c1, c2, op1, op2)\
                        .then_inc(*((tokens_ready, 1) if i == 2 else (pool_step, 1)))
            for i in range(3):
                pool.wait_ge(bias_room, i + 1)
                pool.dma_start(wide[1][:, :], biases[i, :, :]).then_inc(bias_loaded, 16)
                if i == 2:
                    pool.wait_ge(bias_loaded, 48)
            pool.wait_ge(ask_pool, 1)
            pool.partition_all_reduce(gmall, gm, P, RMAX).then_inc(pool_done, 1)

        @block.scalar
        def _(act):
            p = Place(act)
            act.dma_start(cst[:, :], consts).then_inc(consts_loaded, 16)
            act.wait_ge(x0_loaded[NC - 1], 16)
            for b in range(1, B):
                act.dma_start(x[:, b * D:(b + 1) * D], x_in[b, :, :]).then_inc(x_loaded[b - 1], 16)

            def landed(full, n, before=0):
                slots, turns = len(full), p.per_turn.get("block", 0)
                v = 16 * (before + n // slots + 1)
                if p.turn is not None and turns:
                    v = p.turn * (16 * turns // slots) + v
                act.wait_ge(full[n % slots], v)
                return n % slots

            def split(k):
                for _ in range(k):
                    if p.n["block"] >= N_BLOCKS:
                        return
                    s, m = p.n["block"] % SLOTS, p.n["block"] - N_CTX
                    if m < N_WIDE:
                        landed(raw_full, m)
                    else:
                        landed(raw_full[:SLOTS], m - N_WIDE, N_WIDE // WIDE_SLOTS)
                    if p.turn is not None or p.n["block"] >= N_CTX + SLOTS:
                        act.wait_ge(block_used, p.value("block", SLOTS - 1))
                    nc.scalar.activation(hi[:, s, :], raw_at(m), ACT.Copy).then_inc(hi_ready, 1)
                    p.next("block")

            def scale_block(k):
                for _ in range(k):
                    s = landed(ctx_full, p.n["block"])
                    nc.scalar.activation(ctx_raw[:, s, :], ctx_raw[:, s, :], ACT.Identity,
                                         bias=cst[:, C_Z2:C_Z2 + 1], scale=quant[:, 1:2]).then_inc(hi_ready, 1)
                    p.next("block")

            def answer(ins):
                ins.then_inc(act_done, 1)
                p.next("act_done")

            def transposed_hi(dst, *js):
                for j in js or range(4):
                    act.wait_ge(step_done, p.next("step"))
                    answer(nc.scalar.activation(dst(j), psum[:, bank(p), :].rearrange("p (k t) -> p k t", t=P),
                                                ACT.Copy))
                    p.next("bank")

            def ln_hi():
                for b in range(B):
                    transposed_hi(lambda j: xt_hi[:, 4 * j:4 * j + 4, b * P:(b + 1) * P])
                    if b == 1:
                        split(2)

            def early_ln_hi():
                for b in range(B):
                    transposed_hi(lambda j: xt_hi[:, 4 * j:4 * j + 4, b * P:(b + 1) * P])
                    if b < B - 1:
                        p.next("bank", 4)

            def asked():
                act.wait_ge(ask_act, p.next("ask_act"))

            def skip(banks=0, steps=0):
                p.next("bank", banks)
                p.next("step", steps)

            def q1_copy():
                for j in range(4):
                    act.wait_ge(step_done, p.next("step"))
                    answer(nc.scalar.activation(q1t[:, j * W:(j + 1) * W], psum[:, bank(p), :], ACT.Copy))
                    p.next("bank")
                p.next("bank", 4)

            def correction(h):
                act.wait_ge(block_used, p.next("done", KT))
                act.wait_ge(bank_drained, p.value("bank"))
                k = bank(p)
                nc.scalar.activation(wide[h][:, 0:BLK], psum[:, k + 2:k + 4, :], ACT.Identity, bias=row_now,
                                     scale=quant[:, 2:3]).then_inc(correction_ready, 1)
                p.next("bank", 4)

            def row_sums():
                act.wait_ge(tokens_ready, p.next("tokens"))
                answer(nc.scalar.activation(hi[:, 0:2, :], wide[2][:, :].rearrange("p (s n) -> p s n", s=2), ACT.Copy,
                                            accum_out=row_next))

            asked()
            scale_block(CTX_LEAD)
            row_sums()
            q1_copy()
            with p.loop(B - 1, block=2 * KT, bank=16, done=2 * KT, act_done=5, step=4, tokens=1):
                scale_block(KT)
                correction(0)
                scale_block(KT)
                correction(1)
                row_sums()
                q1_copy()
            scale_block(KT)
            correction(0)
            scale_block(KT - CTX_LEAD)
            split(LEAD)
            correction(1)

            early_ln_hi()
            split(3 * KT // 2)
            skip(12)
            asked()
            k = bank(p)
            skip(4, 4)
            for b in range(B):
                answer(nc.scalar.activation(wide[0][:, b * P:(b + 1) * P], psum[:, k + b, 0:P], ACT.Exp,
                                            bias=nmax[:, b:b + 1], scale=HD ** -0.5, accum_out=esum[:, b:b + 1]))
            skip(4, 4)
            for j in range(4):
                act.wait_ge(step_done, p.next("step"))
                answer(nc.scalar.activation(th_hi[0][:, j, :], psum[:, bank(p), :], ACT.Copy))
                p.next("bank")
            split(2 * NC)
            skip(16)

            def lora_hi(rows_):
                split(4)
                skip(4, 4)
                act.wait_ge(bank_drained, p.value("bank"))
                answer(nc.scalar.activation(th_hi[0][0:rows_, 0, :], wide[2][0:rows_, 3 * W:4 * W], ACT.Copy))
                split(KT // 2 - 4)
                split(NC - 1)
                split(KT // 2 + 1)
                skip(4 + 16)

            early_ln_hi()
            split(KT // 2)
            split(KT // 4)
            skip(4 + 4 + 4, 4)
            asked()
            answer(nc.scalar.activation(pr, pr, ACT.Exp))
            split(KT // 2)
            skip(4)
            lora_hi(E0 * R0)

            def query_hi():
                transposed_hi(lambda j: xt_hi[:, 4 * j:4 * j + 4, 0:P])

            def exp_scores():
                asked()
                k = bank(p)
                answer(nc.scalar.activation(wide[0][:, :], psum[:, k:k + 4, :], ACT.Exp,
                                            bias=nmax[:, 0:1], accum_out=esum[:, 0:1]))
                p.next("bank", 4)

            def query_and_values():
                for j in range(4):
                    transposed_hi(lambda j: xt_hi[:, 4 * j:4 * j + 4, 0:P], j)
                    split(1)

            def probs_and_scores(last=False):
                for j in range(4):
                    transposed_hi(lambda j: xt_hi[:, 4 * j:4 * j + 4, P:2 * P], j)
                    split(0 if last else 1)
                split(10 if last else 6)

            query_hi()
            split(2 * KT - 2)
            exp_scores()
            query_hi()
            probs_and_scores()
            with p.loop(B - 2, block=4 * KT, bank=16, step=8, act_done=9, ask_act=1):
                split(2 * KT - 10)
                exp_scores()
                query_and_values()
                split(2 * KT - 4)
                p.next("bank", 4)
                probs_and_scores()
            asked()
            answer(nc.scalar.activation(taylor[:, 0:G + 1], ediff, ACT.Exp))
            split(2 * KT - 10)
            exp_scores()
            split(2 * KT)
            skip(4)
            probs_and_scores(last=True)
            split(2 * KT - 10)
            skip(4)

            def term_hi(i):
                asked()
                answer(nc.scalar.activation(th_hi[i][:, :, :], wide[0][:, :].rearrange("p (k t) -> p k t", k=4),
                                            ACT.Copy))

            ln_hi()
            split(KT // 2)
            term_hi(0)
            split(KT // 2)
            skip(8)

            with p.loop(G // 2, block=4 * NC, bank=32, act_done=2, ask_act=2):
                for i in range(2):
                    term_hi(1 - i)
                    split(2 * NC)
                    p.next("bank", 16)
            split(2 * NC)
            skip(16)

            def gated(i, tiles):
                act.wait_ge(block_used, p.value("done"))
                k = bank(p)
                answer(nc.scalar.activation(wide[0][:, 0:tiles * W], psum[:, k:k + tiles, :], ACT.Sigmoid))
                p.next("bank", 2 * tiles)
                act.wait_ge(bank_drained, p.value("bank"))
                answer(nc.scalar.activation(th_hi[i][:, 0:tiles, :],
                                            wide[1][:, 0:tiles * W].rearrange("p (k t) -> p k t", t=TOK), ACT.Copy))

            def down():
                split(NC)
                p.next("done", NC)
                p.next("bank", 4 * NC)

            p.n["done"] = p.n["block"] - LEAD
            split(KT // 2)
            p.next("done", KT // 2)
            gated(0, 2)
            with p.loop(UNITS // 2, block=2 * (KT // 2 + NC), done=2 * (KT // 2 + NC), bank=40, act_done=4):
                for i in range(2):
                    split(KT // 2)
                    p.next("done", KT // 2)
                    gated(1 - i, 2)
                    down()
            split(KT // 4)
            p.next("done", KT // 4)
            gated(1, 1)
            split(2 * NC)
            skip(4 * NC)

            early_ln_hi()
            split(KT // 2)
            split(KT // 8)
            skip(4 + 4 + 4, 4)
            split(KT // 2)
            skip(4 + 4, 4)
            asked()
            answer(nc.scalar.activation(pr, pr, ACT.Exp))
            asked()
            answer(nc.scalar.activation(t8, t8, ACT.Sigmoid, scale=2.0))
            lora_hi(R1)

        @block.vector
        def _(dve):
            p = Place(dve)
            v = nc.vector

            def link(ins):
                ins.then_inc(dve_step, 1)
                dve.wait_ge(dve_step, p.next("link"))

            def own_drains():
                dve.wait_ge(bank_drained, p.value("bank"))

            def split(k):
                for _ in range(k):
                    if p.n["block"] >= N_BLOCKS:
                        return
                    s, m = p.n["block"] % SLOTS, p.n["block"] - N_CTX
                    dve.wait_ge(hi_ready, p.next("block"))
                    v.tensor_tensor(lo[:, s, :], raw_at(m), hi[:, s, :].bitcast(F32), ALU.subtract)\
                     .then_inc(lo_ready, 1)

            def round_blocks(k):
                for _ in range(k):
                    c, s = p.n["block"] % CTX_SLOTS, p.n["block"] % Q_SLOTS
                    dve.wait_ge(hi_ready, p.next("block"))
                    link(v.tensor_scalar(ctx_raw[:, c, :], ctx_raw[:, c, :], MAGIC, MAGIC, ALU.add, ALU.max))
                    if p.n["block"] > Q_SLOTS:
                        dve.wait_ge(block_used, p.value("block", Q_SLOTS))
                    v.tensor_scalar(q2[:, s, :], ctx_raw[:, c, :], MAGIC + QMAX, MAGIC + QMID,
                                    ALU.min, ALU.subtract).then_inc(lo_ready, 1)

            def x_stats(b, c):
                if isinstance(b, int):
                    return v.bn_stats(stats[:, (b * NC + c) * 6:(b * NC + c) * 6 + 6],
                                      x[:, b * D + c * W:b * D + (c + 1) * W])
                return v.bn_stats(stats[:, ds(b * NC * 6 + c * 6, 6)], x[:, ds(b * D + c * W, W)])

            def chunk_stats(c):
                own_drains()
                for b in range(B):
                    last = x_stats(b, c)
                link(last)

            def rstd_of(a=0, n=B):
                st = stats[:, :].rearrange("p (b k) -> p b k", b=B)
                va, rs, nt = var[:, a:n], rstd[:, a:n], nt1[:, a:n]
                for b in range(a, n):
                    last = v.bn_aggr(mv[:, 2 * b:2 * b + 2], st[:, b, :])
                link(last)
                link(v.tensor_scalar(va, mv.rearrange("p (b k) -> p b k", k=2)[:, a:n, 1], LN_EPS, None, ALU.add))
                link(v.tensor_scalar(rs.bitcast(I32), va.bitcast(I32), 1, None, ALU.logical_shift_right))
                link(v.tensor_scalar(rs.bitcast(I32), rs.bitcast(I32), -1.0, float(0x5F3759DF), ALU.mult, ALU.add))
                for _ in range(3):
                    link(v.scalar_tensor_tensor(nt, rs, -0.5, rs, ALU.mult, ALU.mult))
                    link(v.tensor_tensor(nt, nt, va, ALU.mult))
                    link(v.scalar_tensor_tensor(rs, nt, 1.5, rs, ALU.add, ALU.mult))

            def normalise(b, dst):
                return v.tensor_scalar(dst, x[:, b * D:(b + 1) * D], mv[:, 2 * b:2 * b + 1], rstd[:, b:b + 1],
                                       ALU.subtract, ALU.mult)

            def transposed_lo(hi_, lo_, *js, unused=0):
                for j in js or range(4):
                    dve.wait_ge(act_done, p.next("act_done"))
                    v.tensor_tensor(lo_(j), psum[:, bank(p), :].rearrange("p (k t) -> p k t", t=P),
                                    hi_(j).bitcast(F32), ALU.subtract)\
                     .then_inc(bank_drained, 1 + (unused if j == 3 else 0))
                    p.next("bank")
                    p.next("step")
                p.next("bank", unused)

            def ln_lo(b, unused):
                transposed_lo(lambda j: xt_hi[:, 4 * j:4 * j + 4, b * P:(b + 1) * P],
                              lambda j: xt_lo[:, 4 * j:4 * j + 4, b * P:(b + 1) * P], unused=unused)

            def layer_norm():
                ln_lo(0, 4)
                other_norms()
                normalise(1, wide[1][:, :]).then_inc(ask_pe, 1)
                normalise(2, wide[0][:, :]).then_inc(ask_pe, 1)
                ln_lo(1, 4)
                normalise(3, wide[1][:, :]).then_inc(ask_pe, 1)
                ln_lo(2, 4)
                ln_lo(3, 0)

            def want_bias():
                own_drains()
                v.memset(nt1, 0.0).then_inc(bias_room, 1)

            def add_bias():
                dve.wait_ge(bias_loaded, 16 * p.next("bias"))
                for b in range(B):
                    last = v.tensor_tensor(x[:, b * D:(b + 1) * D], x[:, b * D:(b + 1) * D], wide[1][:, :], ALU.add)
                link(last)

            def add_chunk(col, batches):
                own_drains()
                for b in batches:
                    if isinstance(col, int):
                        xs = x[:, b * D + col * W:b * D + (col + 1) * W]
                    else:
                        xs = x[:, ds(col * W + b * D, W)]
                    v.tensor_tensor(xs, psum[:, bank(p), :], xs, ALU.add).then_inc(bank_drained, 1)
                    p.next("bank")

            def epilogue(col, blocks):
                if blocks:
                    dve.wait_ge(block_used, p.next("done", blocks))
                add_chunk(col, range(B))

            def closing(blocks, first_tokens):
                dve.wait_ge(block_used, p.next("done", blocks))
                add_chunk(NC - 1, [0])
                own_drains()
                link(x_stats(0, NC - 1))
                rstd_of(0, 1)
                normalise(0, first_tokens[:, :]).then_inc(ask_pe, 1)
                add_chunk(NC - 1, range(1, B))
                split(1)

            def other_norms():
                own_drains()
                for b in range(1, B):
                    last = x_stats(b, NC - 1)
                link(last)
                rstd_of(1, B)

            def ask(ins):
                ins.then_inc(ask_act, 1)
                p.next("ask_act")

            def answered():
                dve.wait_ge(act_done, p.next("act_done"))

            def by_expert(t, n=E0):
                return t.rearrange("p (b e) -> p b e", b=B)

            def over(t, n=E0):
                return t.unsqueeze(2).to_broadcast([P, B, n])

            def top2():
                rk = rank[:, :, :]
                for m, oh, among in ((m1, oh1, pr), (m2, oh2, cand)):
                    link(v.tensor_reduce(m, by_expert(among), AX, ALU.max))
                    link(v.tensor_tensor(by_expert(t8), by_expert(among), over(m), ALU.is_equal))
                    link(v.tensor_tensor(by_expert(t8), by_expert(t8), rk, ALU.mult))
                    link(v.tensor_reduce(msum, by_expert(t8), AX, ALU.max))
                    link(v.tensor_tensor(by_expert(oh), rk, over(msum), ALU.is_equal))
                    if m is m1:
                        link(v.scalar_tensor_tensor(cand, oh, -2.0, pr, ALU.mult, ALU.add))

            def softmax8(lgv):
                link(v.tensor_reduce(m1, lgv, AX, ALU.max))
                ask(v.tensor_tensor(by_expert(pr), lgv, over(m1), ALU.subtract))
                answered()
                link(v.tensor_reduce(m1, by_expert(pr), AX, ALU.add))
                link(v.reciprocal(m1, m1))
                link(v.tensor_tensor(by_expert(pr), by_expert(pr), over(m1), ALU.mult))

            def row_term():
                answered()
                link(v.tensor_scalar(row_next, row_next, quant[:, 3:4], quant[:, 4:5], ALU.mult, ALU.add))

            def q1_drained():
                dve.wait_ge(act_done, p.next("act_done", 4))
                p.next("bank", 8)
                link(v.tensor_copy(row_now, row_next))
                v.tensor_copy(nt1[:, 0:1], row_next).then_inc(bank_drained, 8)

            dve.wait_ge(tables_made, 3)
            dve.wait_ge(consts_loaded, 16)
            link(v.reciprocal(quant[:, 0:1], cst[:, C_S1:C_S1 + 1]))
            link(v.tensor_scalar(quant[:, 2:3], cst[:, C_Z1:C_Z1 + 1], -1.0, QMID, ALU.mult, ALU.add))
            link(v.tensor_scalar(quant[:, 3:4], cst[:, C_Z2:C_Z2 + 1], -1.0, QMID, ALU.mult, ALU.add))
            link(v.tensor_scalar(quant[:, 4:5], quant[:, 2:3], quant[:, 3:4], float(D), ALU.mult, ALU.mult))
            link(v.tensor_scalar(quant[:, 5:6], cst[:, C_S1:C_S1 + 1], cst[:, C_S2:C_S2 + 1], None, ALU.mult))
            ask(v.reciprocal(quant[:, 1:2], cst[:, C_S2:C_S2 + 1]))
            for b in range(B):
                if b:
                    dve.wait_ge(x_loaded[b - 1], 16)
                for c in range(NC):
                    if b == 0:
                        dve.wait_ge(x0_loaded[c], 16)
                    last = x_stats(b, c)
                if b == 0:
                    link(last)
                    rstd_of(0, 1)
                    link(normalise(0, wide[2][:, :]))
                    for i, (c1, c2, op1, op2) in enumerate(quantising):
                        last = v.tensor_scalar(wide[2][:, :], wide[2][:, :], c1, c2, op1, op2)
                        if i < 2:
                            link(last)
                    last.then_inc(tokens_ready, 1)
                    round_blocks(Q_LEAD)
                    row_term()
                elif b == 1:
                    q1_drained()
            link(last)
            rstd_of(1, B)
            v.memset(nt1, 0.0).then_inc(norms_ready, 1)

            def dequantise(b, h):
                dve.wait_ge(half_done, p.next("half"))
                k = bank(p)
                p.next("bank", 4)
                xs = x[:, ds(b * D + h * BLK, BLK)] if not isinstance(b, int) else \
                    x[:, b * D + h * BLK:b * D + (h + 1) * BLK]
                v.scalar_tensor_tensor(xs, psum[:, k:k + 2, :].rearrange("p a n -> p (a n)"), quant[:, 5:6], xs,
                                       ALU.mult, ALU.add).then_inc(bank_drained, 4)
                own_drains()

            def half_stats(b, h):
                for c in range(h * NC // 2, (h + 1) * NC // 2):
                    last = x_stats(b, c)
                return last

            def last_batch_norm(unused, chunks, to_split=0):
                for b in range(B):
                    ln_lo(b, unused if b < B - 1 else 0)
                    if b == 0:
                        normalise(2, wide[0][:, :]).then_inc(ask_pe, 1)
                        for c in chunks:
                            last = x_stats(B - 1, c)
                        link(last)
                        rstd_of(B - 1, B)
                    elif b == 1:
                        normalise(3, wide[1][:, :]).then_inc(ask_pe, 1)
                        split(to_split)

            with p.loop(B - 1, block=2 * KT, bank=16, act_done=5, half=2, link=2 * KT + 2) as b:
                round_blocks(KT)
                dequantise(b, 0)
                half_stats(b, 0)
                round_blocks(KT)
                dequantise(b, 1)
                half_stats(b, 1)
                row_term()
                q1_drained()
            round_blocks(KT)
            dequantise(B - 1, 0)
            rstd_of(0, B - 1)
            normalise(0, wide[0][:, :]).then_inc(ask_pe, 1)
            half_stats(B - 1, 0)
            round_blocks(KT - Q_LEAD)
            split(LEAD)
            dequantise(B - 1, 1)
            normalise(1, wide[1][:, :]).then_inc(ask_pe, 1)
            p.n["done"] = N_CTX
            p.n["step"] = 4 * B

            last_batch_norm(4, range(NC // 2, NC))
            split(KT // 2)
            dve.wait_ge(block_used, p.next("done", KT // 2))
            for b in range(B):
                v.tensor_tensor(wide[2][:, b * HD:(b + 1) * HD], psum[:, bank(p), :], cst[:, C_BV:C_BV + HD],
                                ALU.add).then_inc(bank_drained, 1)
                p.next("bank")
            for j, dst in ((0, wide[0]), (1, wide[1])):
                split(KT // 2)
                dve.wait_ge(block_used, p.next("done", KT // 2))
                for t in range(4):
                    v.tensor_scalar(dst[:, t * TOK:(t + 1) * TOK], psum[:, bank(p), :],
                                    cst[:, C_BQK + 4 * j + t:C_BQK + 4 * j + t + 1], None, ALU.add)\
                     .then_inc(bank_drained, 1)
                    p.next("bank")
            dve.wait_ge(step_done, p.next("step", 4))
            k = bank(p)
            link(v.tensor_reduce(nmax, psum[:, k:k + 4, 0:P], AX, ALU.max))
            ask(v.tensor_scalar(nmax, nmax, -HD ** -0.5, None, ALU.mult))
            dve.wait_ge(act_done, p.next("act_done", 4))
            p.next("bank", 4)
            v.reciprocal(rsum, esum).then_inc(bank_drained, 4)
            own_drains()
            for b in range(B):
                last = v.tensor_scalar(wide[0][:, b * P:(b + 1) * P], wide[0][:, b * P:(b + 1) * P], rsum[:, b:b + 1],
                                       None, ALU.mult)
            last.then_inc(ask_pe, 1)
            want_bias()
            for b in range(B):
                dve.wait_ge(step_done, p.next("step"))
                v.tensor_copy(wide[0][:, TOK + b * P:TOK + (b + 1) * P], psum[:, bank(p), 0:P])\
                 .then_inc(bank_drained, 1)
                p.next("bank")
            for j in range(4):
                answered()
                v.tensor_tensor(th_lo[0][:, j, :], psum[:, bank(p), :], th_hi[0][:, j, :].bitcast(F32),
                                ALU.subtract).then_inc(bank_drained, 1)
                p.next("bank")
                p.next("step")
            add_bias()
            for c in range(NC - 1):
                split(2)
                epilogue(c, 2)
                chunk_stats(c)
            split(1)
            closing(2, wide[0])

            def small_drained(blocks, tiles):
                split(blocks)
                dve.wait_ge(block_used, p.next("done", blocks))
                k = bank(p)
                p.next("bank", 4)
                for j in range(tiles):
                    last = v.tensor_copy(wide[2][:, j * TOK:(j + 1) * TOK], psum[:, k + j, :])
                last.then_inc(bank_drained, 4)

            def token_rows(dst, n):
                dve.wait_ge(step_done, p.next("step", 4))
                k = bank(p)
                p.next("bank", 4)
                v.tensor_copy(dst, psum[:, k, 0:n]).then_inc(bank_drained, 4)
                own_drains()

            def lora_states(rows_, factor):
                for b in range(B):
                    dve.wait_ge(step_done, p.next("step"))
                    dst = wide[2][0:rows_, 3 * W + b * P:3 * W + (b + 1) * P]
                    if factor is None:
                        ins = v.tensor_copy(dst, psum[0:rows_, bank(p), 0:P])
                    else:
                        ins = v.tensor_tensor(dst, psum[0:rows_, bank(p), 0:P], factor[:, b * P:(b + 1) * P], ALU.mult)
                    ins.then_inc(bank_drained, 1)
                    p.next("bank")
                answered()
                v.tensor_tensor(th_lo[0][0:rows_, 0, :], wide[2][0:rows_, 3 * W:4 * W],
                                th_hi[0][0:rows_, 0, :].bitcast(F32), ALU.subtract).then_inc(ask_pe, 1)

            def lora(rows_, factor, stat):
                split(4)
                lora_states(rows_, factor)
                split(KT // 2 - 4)
                epilogue(2, KT // 2)
                for c in range(NC - 1):
                    split(1)
                    epilogue(c, 1)
                    if stat:
                        chunk_stats(c)
                split(KT // 2)

            layer_norm()
            want_bias()
            split(KT // 2)
            epilogue(0, KT // 2)
            small_drained(KT // 4, 2)
            token_rows(lg[:, 0:B * E0], B * E0)
            softmax8(by_expert(lg[:, 0:B * E0]))
            top2()
            link(v.tensor_tensor(msum, m1, m2, ALU.add))
            link(v.reciprocal(msum, msum))
            for m, oh in ((m1, oh1), (m2, oh2)):
                link(v.scalar_tensor_tensor(m, m, 2.0, msum, ALU.mult, ALU.mult))
                link(v.tensor_tensor(by_expert(oh), by_expert(oh), over(m), ALU.mult))
            link(v.tensor_tensor(oh1, oh1, oh2, ALU.add))
            spread = wide[2][:, 2 * W:3 * W]
            v.tensor_copy(spread.rearrange("p (k r) -> p k r", r=R0),
                          oh1.unsqueeze(2).to_broadcast([P, B * E0, R0])).then_inc(ask_pe, 1)
            add_bias()
            split(KT // 2)
            epilogue(1, KT // 2)
            lora(E0 * R0, wide[2][:, 0:TOK], True)
            closing(KT // 2 + 1, wide[1])

            def query(b):
                if isinstance(b, int):
                    normalise(b, wide[1][:, :]).then_inc(ask_pe, 1)
                else:
                    link(v.tensor_copy(order_now[:, 0:1], mv[:, ds(b * 2, 1)]))
                    link(v.tensor_copy(order_now[:, 1:2], rstd[:, ds(b, 1)]))
                    v.tensor_scalar(wide[1][:, :], x[:, ds(b * D, D)], order_now[:, 0:1], order_now[:, 1:2],
                                    ALU.subtract, ALU.mult).then_inc(ask_pe, 1)

            def query_lo(*js):
                transposed_lo(lambda j: xt_hi[:, 4 * j:4 * j + 4, 0:P], lambda j: xt_lo[:, 4 * j:4 * j + 4, 0:P], *js)

            def probs_lo(j):
                transposed_lo(lambda j: xt_hi[:, 4 * j:4 * j + 4, P:2 * P],
                              lambda j: xt_lo[:, 4 * j:4 * j + 4, P:2 * P], j)

            def softmax():
                dve.wait_ge(block_used, p.next("done", 2 * KT))
                k = bank(p)
                link(v.tensor_reduce(m1[:, 0:1], psum[:, k:k + 4, :].rearrange("p a n -> p (a n)"), AX, ALU.max))
                ask(v.tensor_scalar(nmax[:, 0:1], m1[:, 0:1], -1.0, None, ALU.mult))
                split(1)
                answered()
                p.next("bank", 4)
                v.reciprocal(rsum[:, 1:2], esum[:, 0:1]).then_inc(bank_drained, 4)

            def attended(b):
                dve.wait_ge(block_used, p.next("done", 2 * KT))
                own_drains()
                for c in range(NC):
                    xs = x[:, b * D + c * W:b * D + (c + 1) * W] if isinstance(b, int) else x[:, ds(b * D + c * W, W)]
                    v.scalar_tensor_tensor(xs, psum[:, bank(p), :], rsum[:, 0:1], xs, ALU.mult, ALU.add)\
                     .then_inc(bank_drained, 1)
                    p.next("bank")
                own_drains()
                link(v.tensor_copy(rsum[:, 0:1], rsum[:, 1:2]))

            def probs_and_scores(b=None, last=False):
                for j in range(4):
                    probs_lo(j)
                    split(0 if last else 1)
                split(4 if last else 0)
                for c in range(NC):
                    if b is not None:
                        x_stats(b, c)
                    split(1)
                split(2)
                link(v.tensor_copy(nt1[:, 0:1], rsum[:, 0:1]))

            query_lo()
            other_norms()
            query(1)
            split(2 * KT - 3)
            softmax()
            own_drains()
            link(v.tensor_copy(rsum[:, 0:1], rsum[:, 1:2]))
            query_lo()
            probs_and_scores()
            with p.loop(B - 2, block=4 * KT, done=4 * KT, bank=16, step=8, act_done=9, ask_act=1, link=5) as b:
                query(b + 2)
                split(2 * KT - 11)
                softmax()
                for j in range(4):
                    query_lo(j)
                    split(1)
                split(2 * KT - 5)
                attended(b)
                split(1)
                probs_and_scores(b)
            link(v.memset(ediff, 0.0))
            link(v.tensor_scalar(ediff[:, 1:2], cst[:, C_DF:C_DF + 1], -1.0, None, ALU.mult))
            ask(v.tensor_tensor(ediff[:, 2:G + 1], cst[:, C_DF:C_DF + G - 1], cst[:, C_DF + 1:C_DF + G], ALU.subtract))
            link(v.memset(taylor[:, G + 1:G + 1 + GRAD_ORDER_MIN + 1], 1.0))
            link(v.memset(taylor[:, G + 2 + GRAD_ORDER_MIN:2 * (G + 1)], 0.0))
            answered()
            split(2 * KT - 11)
            softmax()
            split(2 * KT - 1)
            attended(B - 2)
            split(1)
            probs_and_scores(B - 2, last=True)
            split(6)
            rstd_of(0, B - 1)
            for b in range(2):
                split(4)
                normalise(b, wide[b][:, :]).then_inc(ask_pe, 1)
            split(2 * KT - 8 - 6 - 2 * 4 - 3)
            attended(B - 1)
            last_batch_norm(0, range(NC), to_split=3)

            t_now, delta, keep = wide[0], wide[1], wide[2]

            def term_lo(i):
                answered()
                v.tensor_tensor(th_lo[i][:, :, :], t_now[:, :].rearrange("p (k t) -> p k t", k=4),
                                th_hi[i][:, :, :].bitcast(F32), ALU.subtract).then_inc(ask_pe, 1)

            split(KT // 2)
            dve.wait_ge(block_used, p.next("done", KT // 2))
            own_drains()
            for j in range(4):
                v.tensor_copy(t_now[:, j * TOK:(j + 1) * TOK], psum[:, bank(p), :]).then_inc(bank_drained, 1)
                p.next("bank")
            own_drains()
            ask(v.tensor_copy(order_now[:, 0:1], taylor[:, 0:1]))
            split(2)
            term_lo(0)
            split(KT // 2 - 2)
            dve.wait_ge(block_used, p.next("done", KT // 2))
            for j in range(4):
                v.tensor_scalar(delta[:, j * TOK:(j + 1) * TOK], psum[:, bank(p), :],
                                cst[:, C_LP + j:C_LP + j + 1], None, ALU.subtract).then_inc(bank_drained, 1)
                p.next("bank")
            own_drains()
            link(v.tensor_scalar(keep[:, :], delta[:, :], -1.0, None, ALU.mult))
            link(v.tensor_tensor(keep[:, :], keep[:, :], delta[:, :], ALU.max))
            link(v.tensor_scalar(keep[:, :], keep[:, :], THD, None, ALU.is_le))

            def next_term(m):
                link(v.tensor_copy(order_now[:, 0:1], taylor[:, ds(m, 1)]))
                link(v.tensor_copy(order_now[:, 1:2], taylor[:, ds(m + (G + 1), 1)]))
                link(v.scalar_tensor_tensor(t_now[:, :], t_now[:, :], order_now[:, 0:1], delta[:, :],
                                            ALU.mult, ALU.mult))
                ask(v.scalar_tensor_tensor(t_now[:, :], keep[:, :], order_now[:, 1:2], t_now[:, :],
                                           ALU.max, ALU.mult))

            with p.loop(G // 2, block=4 * NC, done=4 * NC, bank=32, act_done=2, ask_act=2, link=6) as t:
                for i in range(2):
                    next_term(t * 2 + (i + 1))
                    term_lo(1 - i)
                    for c in range(NC):
                        split(2)
                        epilogue(c, 2)
            for c in range(NC):
                split(2)
                epilogue(c, 2)

            def gated(i, tiles, blocks):
                k = bank(p)
                n = tiles * W
                p.next("done", blocks)
                answered()
                link(v.tensor_tensor(wide[0][:, 0:n], wide[0][:, 0:n],
                                     psum[:, k:k + tiles, :].rearrange("p a n -> p (a n)"), ALU.mult))
                v.tensor_tensor(wide[1][:, 0:n], wide[0][:, 0:n],
                                psum[:, k + tiles:k + 2 * tiles, :].rearrange("p a n -> p (a n)"),
                                ALU.mult).then_inc(bank_drained, 2 * tiles)
                p.next("bank", 2 * tiles)
                answered()
                v.tensor_tensor(th_lo[i][:, 0:tiles, :], wide[1][:, 0:n].rearrange("p (k t) -> p k t", t=TOK),
                                th_hi[i][:, 0:tiles, :].bitcast(F32), ALU.subtract).then_inc(ask_pe, 1)

            def down():
                for c in range(NC):
                    split(1)
                    epilogue(c, 1)

            split(KT // 2)
            gated(0, 2, KT // 2)
            with p.loop(UNITS // 2, block=2 * (KT // 2 + NC), done=2 * (KT // 2 + NC), bank=40, act_done=4,
                        link=2):
                for i in range(2):
                    split(KT // 2)
                    gated(1 - i, 2, KT // 2)
                    down()
            split(KT // 4)
            gated(1, 1, KT // 4)
            for c in range(NC - 1):
                split(2)
                epilogue(c, 2)
                chunk_stats(c)
            split(1)
            closing(2, wide[0])

            layer_norm()
            want_bias()
            split(KT // 2)
            epilogue(0, KT // 2)
            small_drained(KT // 8, 1)
            token_rows(wide[2][:, 1728:1728 + B * SM1], B * SM1)
            zc = wide[2][:, 1728:1728 + B * SM1].rearrange("p (b n) -> p b n", b=B)
            z = zc[:, :, E1:SM1]
            hdv = hd.rearrange("p (b k e) -> p b k e", b=B, k=2)
            limes = cst[:, C_LIM:C_LIM + E1 * R1].rearrange("p (e r) -> p e r", e=E1)
            prod = wide[2][:, 512:512 + B * E1 * R1]
            link(v.tensor_tensor(hdv[:, :, 0, :], zc[:, :, 0:E1],
                                 cst[:, C_B8:C_B8 + E1].unsqueeze(1).to_broadcast([P, B, E1]), ALU.add))
            for b in range(B):
                last = v.tensor_tensor(prod[:, b * E1 * R1:(b + 1) * E1 * R1].rearrange("p (e r) -> p e r", e=E1),
                                       z[:, b, :].unsqueeze(1).to_broadcast([P, E1, R1]), limes, ALU.mult)
            link(last)
            v.tensor_reduce(hdv[:, :, 1, :], prod.rearrange("p (b e r) -> p b e r", b=B, e=E1), AX, ALU.add)\
             .then_inc(ask_pe, 1)
            add_bias()
            split(KT // 2)
            epilogue(1, KT // 2)
            token_rows(lg, B * 2 * E1)
            lgv = lg.rearrange("p (b k e) -> p b k e", b=B, k=2)
            for i in range(2):
                link(v.tensor_scalar(by_expert(t8), lgv[:, :, i, :], -1.0, None, ALU.mult))
                link(v.tensor_tensor(by_expert(t8), by_expert(t8), lgv[:, :, i, :], ALU.max))
                last = v.tensor_reduce(gm[:, i:i + 1], t8, AX, ALU.max)
                if i == 0:
                    link(last)
            last.then_inc(ask_pool, 1)
            dve.wait_ge(pool_done, 1)
            link(v.tensor_scalar(gmall, gmall, 1e-6, None, ALU.max))
            link(v.reciprocal(gmall, gmall))
            link(v.tensor_scalar(gmall, gmall, 0.5, None, ALU.mult))
            link(v.tensor_scalar(lgv[:, :, 0, :], lgv[:, :, 0, :], gmall[:, 0:1], None, ALU.mult))
            link(v.scalar_tensor_tensor(by_expert(t8), lgv[:, :, 1, :], gmall[:, 1:2], lgv[:, :, 0, :],
                                        ALU.mult, ALU.add))
            softmax8(by_expert(t8))
            top2()
            ask(v.tensor_tensor(by_expert(t8), by_expert(pr), over(m2), ALU.subtract))
            answered()
            link(v.tensor_tensor(pr, pr, t8, ALU.mult))
            link(v.tensor_reduce(msum, by_expert(pr), AX, ALU.add))
            link(v.tensor_scalar(msum, msum, 1e-9, None, ALU.add))
            link(v.reciprocal(msum, msum))
            link(v.scalar_tensor_tensor(by_expert(pr), by_expert(pr), 0.5, over(msum), ALU.mult, ALU.mult))
            for b in range(B):
                last = v.tensor_tensor(
                    prod[:, b * E1 * R1:(b + 1) * E1 * R1].rearrange("p (r e) -> p r e", e=E1),
                    pr[:, b * E1:(b + 1) * E1].unsqueeze(1).to_broadcast([P, R1, E1]),
                    cst[:, C_LIM:C_LIM + E1 * R1].rearrange("p (e r) -> p r e", e=E1), ALU.mult)
            link(last)
            mix = wide[2][:, 1536:1536 + B * R1].rearrange("p (b r) -> p b r", b=B)
            link(v.tensor_reduce(mix, prod.rearrange("p (b r e) -> p b r e", b=B, e=E1), AX, ALU.add))
            v.tensor_tensor(wide[2][:, 0:B * R1].rearrange("p (b r) -> p b r", b=B), mix, z, ALU.mult)\
             .then_inc(ask_pe, 1)
            lora(R1, None, False)
            epilogue(NC - 1, KT // 2 + 1)

        @block.tensor
        def _(pe):
            p = Place(pe)
            mm = nc.tensor.matmul

            def free_bank():
                k = bank(p)
                if p.n["bank"] >= BANKS:
                    pe.wait_ge(bank_drained, p.value("bank", BANKS - 1))
                p.next("bank")
                return k

            def all_drained():
                pe.wait_ge(bank_drained, p.value("bank"))

            def asked(k=1):
                pe.wait_ge(ask_pe, p.next("ask_pe", k))

            def three(dst, st, mv_, first, last):
                (sh, sl), (mh, ml) = st, mv_
                mm(dst, sh, mh, start=first, stop=False)
                mm(dst, sh, ml, start=False, stop=False)
                return mm(dst, sl, mh, start=False, stop=last)

            def transposes(src, rows_=P):
                for j in range(4):
                    k = free_bank()
                    for i, tile in enumerate(src(j)):
                        last = nc.tensor.transpose(psum[0:rows_, k, i * P:(i + 1) * P], tile, ident[:, :])
                    last.then_inc(step_done, 1)

            def tiles4(t):
                return lambda j: [t[:, (4 * j + i) * P:(4 * j + i + 1) * P] for i in range(4)]

            def ln_transposes():
                for b in range(B):
                    asked()
                    transposes(tiles4(wide[b % 2]))
                all_drained()

            def blocks(n, products, before=None):
                banks = None
                for i in range(n):
                    if before and i in before:
                        before[i]()
                    s = p.n["block"] % SLOTS
                    pe.wait_ge(lo_ready, p.next("block"))
                    todo = products(i, s)
                    if banks is None:
                        banks = {}
                    for j, st, mv_, width, first, last in todo:
                        if j not in banks:
                            banks[j] = free_bank()
                        ins = three(psum[:, banks[j], 0:width], st, mv_, first, last)
                    ins.then_inc(block_used, 1)

            def part(s, a, n, rows_=P):
                return (hi[0:rows_, s, a:a + n], lo[0:rows_, s, a:a + n])

            def tokens(t, k, b, rows_=P):
                return (t[0][0:rows_, k, b * P:(b + 1) * P], t[1][0:rows_, k, b * P:(b + 1) * P])

            xt = (xt_hi, xt_lo)
            th = list(zip(th_hi, th_lo))

            def token_major(t, n_kt, per_block, width, rows_=P, before=None):
                def products(i, s):
                    return [(b, tokens(t, k, b, rows_), part(s, (k - i * per_block) * width, width, rows_), width,
                             k == 0, k == n_kt - 1)
                            for k in range(i * per_block, min(n_kt, (i + 1) * per_block)) for b in range(B)]
                blocks(-(-n_kt // per_block), products, before)

            def feature_major(tiles=4):
                per_block = BLK // (tiles * P)

                def products(i, s):
                    return [(j, part(s, ((k - i * per_block) * tiles + j) * P, P), (xt_hi[:, k, :], xt_lo[:, k, :]),
                             TOK, k == 0, k == KT - 1)
                            for k in range(i * per_block, (i + 1) * per_block) for j in range(tiles)]
                blocks(KT // per_block, products)

            def ln_and_first_product(behind=0):
                base = p.n["bank"]
                early, per_block = min(LEAD, KT // 2), 2

                def token_tile(b):
                    asked()
                    assert p.n["bank"] == base + 8 * b
                    transposes(tiles4(wide[b % 2]))
                    p.next("bank", 4 if b < B - 1 else 0)

                def product(b, i):
                    for k in range(i * per_block, (i + 1) * per_block):
                        ins = three(psum[:, (base + 4 + b) % BANKS, :], tokens(xt, k, b),
                                    part((n0 + i) % SLOTS, (k - i * per_block) * W, W), k == 0, k == KT - 1)
                    return ins

                n0 = p.n["block"]
                token_tile(0)
                for b in range(1, 1 + behind):
                    token_tile(b)
                pe.wait_ge(lo_ready, p.value("block") + early)
                for b in range(B):
                    pe.wait_ge(bank_drained, base + 8 * b + 4)
                    for i in range(early):
                        ins = product(b, i)
                        if b == B - 1:
                            ins.then_inc(block_used, 1)
                    for b2 in range(max(1 + behind, 1) if b == 0 else b + 2, min(b + 3, B)):
                        token_tile(b2)
                p.next("block", early)
                for i in range(early, KT // per_block):
                    pe.wait_ge(lo_ready, p.next("block"))
                    for b in range(B):
                        ins = product(b, i)
                    ins.then_inc(block_used, 1)
                p.next("bank", 4)

            pe.wait_ge(tables_made, 3)
            with p.loop(B, block=2 * KT, bank=16, tokens=1, half=2):
                pe.wait_ge(tokens_ready, p.next("tokens"))
                transposes(tiles4(wide[2]))
                p.next("bank", 4)
                all_drained()
                for h in range(2):
                    ks = [free_bank() for _ in range(4)]
                    for i in range(KT):
                        s = p.n["block"] % Q_SLOTS
                        pe.wait_ge(lo_ready, p.next("block"))
                        for j in range(2):
                            mm(psum[:, ks[j], :], q1t[:, i * P:(i + 1) * P], q2[:, s, j * W:(j + 1) * W],
                               start=i == 0, stop=False)
                        for j in range(2):
                            ins = mm(psum[:, ks[2 + j], :], ones[:, :], q2[:, s, j * W:(j + 1) * W],
                                     start=i == 0, stop=i == KT - 1)
                        ins.then_inc(block_used, 1)
                    pe.wait_ge(correction_ready, p.next("half"))
                    for j in range(2):
                        ins = mm(psum[:, ks[j], :], ident[:, :], wide[h][:, j * W:(j + 1) * W], start=False, stop=True)
                    ins.then_inc(half_done, 1)

            ln_and_first_product(behind=1)
            feature_major()
            feature_major()
            all_drained()
            for b in range(B):
                k = free_bank()
                for j in range(4):
                    last = mm(psum[:, k, 0:P], wide[0][:, j * TOK + b * P:j * TOK + (b + 1) * P],
                              wide[1][:, j * TOK + b * P:j * TOK + (b + 1) * P], start=j == 0, stop=j == 3)
                last.then_inc(step_done, 1)
            asked()
            for b in range(B):
                nc.tensor.transpose(psum[:, free_bank(), 0:P], wide[0][:, b * P:(b + 1) * P], ident[:, :])\
                  .then_inc(step_done, 1)
            all_drained()
            for j in range(4):
                k = free_bank()
                for b in range(B):
                    last = mm(psum[:, k, b * P:(b + 1) * P], wide[2][:, b * HD + j * P:b * HD + (j + 1) * P],
                              wide[0][:, TOK + b * P:TOK + (b + 1) * P], start=True, stop=True)
                last.then_inc(step_done, 1)
            all_drained()
            for c in range(NC):
                token_major(th[0], 4, 2, W)

            def narrow(tiles, width):
                kept = p.n["bank"]
                feature_major(tiles)
                p.next("bank", kept + 4 - p.n["bank"])
                all_drained()
                k = free_bank()
                p.next("bank", 3)
                n, src = width
                for b in range(B):
                    last = nc.tensor.transpose(psum[:, k, b * n:(b + 1) * n],
                                               wide[2][0:n, src + b * P:src + (b + 1) * P], ident[0:n, 0:n])
                last.then_inc(step_done, 4)

            def lora(tile, rows_):
                own = [free_bank() for _ in range(B)]

                def states():
                    asked()
                    for b in range(B):
                        nc.tensor.transpose(psum[0:rows_, own[b], 0:P], tile(b), ident[:, :]).then_inc(step_done, 1)

                token_major(xt, KT, 2, W, before={6: states})
                asked()
                for c in range(NC - 1):
                    token_major(th[0], 1, 1, W, rows_)

                def products(i, s):
                    if i == KT // 2:
                        return [(b, tokens(th[0], 0, b, rows_), part(s, 0, W, rows_), W, False, True) for b in range(B)]
                    return [(b, tokens(xt, k, b), part(s, (k - 2 * i) * W, W), W, k == 0, False)
                            for k in (2 * i, 2 * i + 1) for b in range(B)]
                blocks(KT // 2 + 1, products)

            ln_and_first_product()
            narrow(2, (E0, TOK))
            token_major(xt, KT, 2, W)
            lora(lambda b: wide[2][:, 2 * W + b * P:2 * W + (b + 1) * P], E0 * R0)

            def rows_major(col):
                def products(i, s):
                    k, half = i // 2, i % 2
                    st = (xt_hi[:, k, col:col + P], xt_lo[:, k, col:col + P])
                    return [(2 * half + j, st, part(s, j * W, W), W, k == 0, k == KT - 1) for j in range(2)]
                blocks(2 * KT, products)

            def query():
                asked()
                transposes(tiles4(wide[1]))

            def probs():
                transposes(tiles4(wide[0]))

            def scores():
                rows_major(0)

            def values():
                rows_major(P)

            query()
            all_drained()
            scores()
            query()
            probs()
            with p.loop(B - 2, block=4 * KT, bank=16, ask_pe=1):
                scores()
                query()
                values()
                probs()
            scores()
            values()
            probs()
            all_drained()
            values()

            ln_transposes()
            feature_major()
            feature_major()
            with p.loop(G // 2, block=4 * NC, bank=32, ask_pe=2):
                for i in range(2):
                    asked()
                    for c in range(NC):
                        token_major(th[i], 4, 2, W)
            asked()
            for c in range(NC):
                token_major(th[0], 4, 2, W)

            feature_major()
            with p.loop(UNITS // 2, block=2 * (KT // 2 + NC), bank=40, ask_pe=2):
                for i in range(2):
                    feature_major()
                    asked()
                    for c in range(NC):
                        token_major(th[i], 2, 2, W)
            feature_major(tiles=2)
            asked()
            for c in range(NC):
                def products(i, s):
                    return [(b, tokens(th[i], k, b), part(s, k * W, W), W, i == k == 0, i == 1)
                            for k in range(2 - i) for b in range(B)]
                blocks(2, products, before={1: asked} if c == 0 else None)

            ln_and_first_product()
            narrow(1, (SM1, 0))
            token_major(xt, KT, 2, W)
            asked()
            k = free_bank()
            p.next("bank", 3)
            mm(psum[:, k, 0:B * 2 * E1], pick[:, :], hd, start=True, stop=True).then_inc(step_done, 4)
            lora(lambda b: wide[2][:, b * R1:(b + 1) * R1], R1)
            assert p.n["bank"] == TOTAL_BANKS and p.n["block"] == N_BLOCKS, (p.n["bank"], p.n["block"], N_BLOCKS)


TOTAL_BANKS = (16 * B) + (32 + 8 + 12 + 16) + (32 + 8 + 8 + 4 + 16) + 16 * B \
    + (16 + 8 + 16 * (G + 1) + 20 * UNITS + 2) + (32 + 8 + 8 + 4 + 4 + 16)


def tiled(w, tiles_per_block=2):
    k, n = w.shape
    kt = k // P
    nb = -(-kt // tiles_per_block)
    out = np.zeros((nb, P, BLK), np.float32)
    for i in range(nb):
        part = w[i * tiles_per_block * P:(i + 1) * tiles_per_block * P]
        m = part.shape[0] // P
        out[i, :, :m * n] = part.reshape(m, P, n).transpose(1, 0, 2).reshape(P, m * n)
    return out


def chunks(w, tiles_per_block=2):
    return [tiled(w[:, c * W:(c + 1) * W], tiles_per_block) for c in range(NC)]


def halves(w):
    return w.reshape(KT, P, 2, BLK).transpose(2, 0, 1, 3)


def kernel(x, ctx_4096, L0_xattn_x1_scale, L0_xattn_x1_zp, L0_xattn_x2_scale, L0_xattn_x2_zp, L0_attn_Wqkv,
           L0_attn_bqkv, L0_attn_Wo, L0_attn_bo, L0_ffn_W_base, L0_ffn_b_base, L0_ffn_W_router, L0_ffn_A, L0_ffn_B,
           L1_attn_up_w, L1_attn_gate_w, L1_attn_local_point, L1_attn_local_approx_output, L1_attn_fuse_weight,
           L1_attn_discount_factor, L1_attn_ffn_gate_w, L1_attn_ffn_up_w, L1_attn_ffn_down_w, L1_ffn_W, L1_ffn_b,
           L1_ffn_A, L1_ffn_Bmat, L1_ffn_LiMEs):
    import concourse.bacc as bacc
    from concourse.bass_utils import run_bass_kernel_spmd

    c = np.asarray(ctx_4096)
    parts = [halves(c[b]).reshape(-1, P, BLK) for b in range(B)]
    wqkv = np.asarray(L0_attn_Wqkv)
    parts += [tiled(wqkv[:, i * HD:(i + 1) * HD]) for i in (2, 0, 1)]
    parts += chunks(np.asarray(L0_attn_Wo))
    lora_a = np.asarray(L0_ffn_A).reshape(E0 * R0, D)
    router = np.concatenate([np.asarray(L0_ffn_W_router), np.zeros((P - E0, D), np.float32)])
    base = chunks(np.asarray(L0_ffn_W_base).T)
    lora_b = chunks(np.asarray(L0_ffn_B).transpose(0, 2, 1).reshape(E0 * R0, D), 1)
    parts += [base[0], tiled(np.concatenate([lora_a, router]).T, 4), base[1], base[2]] + lora_b[:3] \
        + [base[3], lora_b[3]]

    def rows(w):
        return halves(w).transpose(1, 0, 2, 3).reshape(-1, P, BLK)

    parts += [rows(c[0].T)]
    for b in range(1, B):
        parts += [rows(c[b].T), rows(c[b - 1])]
    parts += [rows(c[B - 1])]
    parts += [tiled(np.asarray(w).T) for w in (L1_attn_up_w, L1_attn_gate_w)]
    parts += chunks(np.asarray(L1_attn_local_approx_output).T)
    fuse = np.asarray(L1_attn_fuse_weight)
    for m in range(G):
        parts += chunks(fuse[:, :, m].T)
    gate, up, down = (np.asarray(w).T for w in (L1_attn_ffn_gate_w, L1_attn_ffn_up_w, L1_attn_ffn_down_w))

    def gate_up(j, tiles=2):
        f = slice(2 * j * P, (2 * j + tiles) * P)
        return tiled(np.concatenate([gate[:, f], up[:, f]], axis=1), BLK // (2 * tiles * P))

    def down_rows(j, tiles=2):
        return chunks(down[2 * j * P:(2 * j + tiles) * P])

    parts += [gate_up(0)]
    for j in range(1, UNITS):
        parts += [gate_up(j)] + down_rows(j - 1)
    parts += [gate_up(UNITS, 1)]
    for pair in zip(down_rows(UNITS - 1), down_rows(UNITS, 1)):
        parts += pair
    w1 = np.asarray(L1_ffn_W).T
    first = np.concatenate([w1[:, :E1], np.asarray(L1_ffn_A), np.zeros((D, P - SM1), np.float32)], axis=1)
    bmat = np.zeros((P, D), np.float32)
    bmat[:R1] = np.asarray(L1_ffn_Bmat)
    base, lora_b = chunks(w1), chunks(bmat, 1)
    parts += [base[0], tiled(first, 8), base[1], base[2]] + lora_b[:3] + [base[3], lora_b[3]]
    stream = np.concatenate(parts)
    assert stream.shape == (N_BLOCKS, P, BLK), stream.shape

    def wide_row(a):
        a = np.asarray(a).reshape(-1)
        return np.broadcast_to(a, (P, a.size))

    b1 = np.asarray(L1_ffn_b)
    bqkv = np.asarray(L0_attn_bqkv)
    consts = np.concatenate(
        [wide_row(a) for a in (L0_xattn_x1_scale, L0_xattn_x1_zp, L0_xattn_x2_scale, L0_xattn_x2_zp)]
        + [bqkv[:2 * HD].reshape(8, P).T, np.asarray(L1_attn_local_point).reshape(4, P).T]
        + [wide_row(a) for a in (L1_attn_discount_factor, b1[:E1], L1_ffn_LiMEs, bqkv[2 * HD:])], axis=1)
    assert consts.shape == (P, C_END)
    biases = np.stack([wide_row(a) for a in (L0_attn_bo, L0_ffn_b_base, b1)])

    arrays = {"x_in": np.asarray(x), "stream": stream, "biases": biases, "consts": consts}
    arrays = {k: np.ascontiguousarray(a) for k, a in arrays.items()}
    nc = bacc.Bacc("TRN2", target_bir_lowering=False, num_devices=1)
    args = [nc.dram_tensor(k, a.shape, F32, kind="ExternalInput").ap() for k, a in arrays.items()]
    out = nc.dram_tensor("x_out", (B, P, D), F32, kind="ExternalOutput").ap()
    build(nc, *args, out)
    return run_bass_kernel_spmd(nc, [arrays], core_ids=[0]).results[0]["x_out"]
```
